# Optimizing a Trainium2 kernel written in Bass

```python
import numpy as np
import jax
import jax.numpy as jnp

def _softmax(x, axis=-1):
    return jax.nn.softmax(x, axis=axis)

def _gelu(x):
    return jax.nn.gelu(x, approximate=True)

def _silu(x):
    return jax.nn.silu(x)

def _sigmoid(x):
    return jax.nn.sigmoid(x)

def _layernorm(x, axis=-1, eps=1e-05):
    m = jnp.mean(x, axis=axis, keepdims=True)
    v = jnp.var(x, axis=axis, keepdims=True)
    return (x - m) / jnp.sqrt(v + eps)

def _scatter_add(tgt, idx, src, axis=0):
    return tgt.at[idx].add(src)

def _segment_sum(src, seg, n):
    return jax.ops.segment_sum(src, seg, n)
kernel_name = 'mk_early_fusion_d1_tok_img1024_r4_4a8fe6'

def setup_inputs(seed: int=0):
    np.random.seed(seed)
    _w = jnp.asarray

    def _rec_inputs():
        import jax
        import jax.numpy as jnp
        _rk = jax.random.key(seed)
        x = -0.00016672 + 0.999947 * jax.random.normal(jax.random.fold_in(_rk, 1), (16, 3, 96, 96), jnp.float32)
        txt = -6.04713e-11 + 0.999984 * jax.random.normal(jax.random.fold_in(_rk, 2), (16, 32, 256), jnp.float32)
        return (x, txt)
    x, txt = _rec_inputs()

    def _L0_tok_setup():
        import jax, jax.numpy as jnp
        import numpy as np
        PATCH = 16
        EPS = 1e-05

        def _patchify(x, p):
            B, C, H, W = x.shape
            hp, wp = (H // p, W // p)
            x = x.reshape(B, C, hp, p, wp, p)
            x = x.transpose(0, 2, 4, 1, 3, 5)
            return x.reshape(B, hp * wp, C * p * p)
        key = jax.random.key(seed)
        ks = jax.random.split(key, 6)
        B, C, H = (64, 3, 96)
        E = 256
        P = PATCH
        N = (H // P) ** 2
        D = C * P * P
        x = jax.random.normal(ks[0], (B, C, H, H), dtype=jnp.float32)
        W = jax.random.normal(ks[1], (D, E), dtype=jnp.float32) * (1.0 / np.sqrt(D))
        b = jnp.zeros((E,), dtype=jnp.float32)
        cls_token = jax.random.normal(ks[2], (1, 1, E), dtype=jnp.float32) * 0.02
        pos_embedding = jax.random.normal(ks[3], (1, N + 1, E), dtype=jnp.float32) * 0.02
        gamma = jnp.ones((E,), dtype=jnp.float32)
        beta = jnp.zeros((E,), dtype=jnp.float32)
        return {'x': x, 'W': W, 'b': b, 'cls_token': cls_token, 'pos_embedding': pos_embedding, 'gamma': gamma, 'beta': beta}
    _L0_tok_all = _L0_tok_setup()
    _L0_tok_in = {k: v for k, v in _L0_tok_all.items() if k in ('W', 'b', 'cls_token', 'pos_embedding', 'gamma', 'beta')}
    del _L0_tok_all

    def _L0_attn_setup():
        import jax, jax.numpy as jnp
        import numpy as np
        import math
        D_MODEL = 256
        N_HEADS = 16
        D_HEAD = D_MODEL // N_HEADS
        DECAY_MAX = 0.99
        LN_EPS = 1e-05

        def _decay_mask(S):
            i = jnp.arange(S, dtype=jnp.float32)[:, None]
            j = jnp.arange(S, dtype=jnp.float32)[None, :]
            diff = i - j
            return jnp.where(diff >= 0, jnp.power(jnp.float32(DECAY_MAX), diff), 0.0)
        key = jax.random.key(seed)
        ks = jax.random.split(key, 12)
        B, S = (2, 512)
        x = jax.random.normal(ks[0], (B, S, D_MODEL), dtype=jnp.float32)

        def w(k):
            return jax.random.normal(k, (D_MODEL, D_MODEL), dtype=jnp.float32) * 0.02
        return {'x': x, 'Wq': w(ks[1]), 'bq': jnp.zeros((D_MODEL,), jnp.float32), 'Wk': w(ks[2]), 'bk': jnp.zeros((D_MODEL,), jnp.float32), 'Wv': w(ks[3]), 'bv': jnp.zeros((D_MODEL,), jnp.float32), 'Wg': w(ks[4]), 'bg': jnp.zeros((D_MODEL,), jnp.float32), 'Wo': w(ks[5]), 'bo': jnp.zeros((D_MODEL,), jnp.float32), 'gamma': jnp.ones((D_MODEL,), jnp.float32), 'beta': jnp.zeros((D_MODEL,), jnp.float32)}
    _L0_attn_all = _L0_attn_setup()
    _L0_attn_in = {k: v for k, v in _L0_attn_all.items() if k in ('Wq', 'bq', 'Wk', 'bk', 'Wv', 'bv', 'Wg', 'bg', 'Wo', 'bo', 'gamma', 'beta')}
    del _L0_attn_all

    def _L0_ffn_setup():
        import jax, jax.numpy as jnp
        import numpy as np
        HIDDEN = 256
        INTER = 1024
        N_EXPERTS = 8

        def geglu(x, w1, w2, w3):
            return jax.nn.gelu(x @ w1, approximate=False) * (x @ w2) @ w3
        key = jax.random.key(seed)
        ks = jax.random.split(key, 8)
        s = 0.02
        x = jax.random.normal(ks[0], (2, 512, HIDDEN), dtype=jnp.float32)
        w1s = jax.random.normal(ks[1], (HIDDEN, INTER), dtype=jnp.float32) * s
        w2s = jax.random.normal(ks[2], (HIDDEN, INTER), dtype=jnp.float32) * s
        w3s = jax.random.normal(ks[3], (INTER, HIDDEN), dtype=jnp.float32) * s
        W1 = jax.random.normal(ks[4], (N_EXPERTS, HIDDEN, INTER), dtype=jnp.float32) * s
        W2 = jax.random.normal(ks[5], (N_EXPERTS, HIDDEN, INTER), dtype=jnp.float32) * s
        W3 = jax.random.normal(ks[6], (N_EXPERTS, INTER, HIDDEN), dtype=jnp.float32) * s
        Wg = jax.random.normal(ks[7], (HIDDEN, N_EXPERTS), dtype=jnp.float32) * s
        return {'x': x, 'w1s': w1s, 'w2s': w2s, 'w3s': w3s, 'W1': W1, 'W2': W2, 'W3': W3, 'Wg': Wg}
    _L0_ffn_all = _L0_ffn_setup()
    _L0_ffn_in = {k: v for k, v in _L0_ffn_all.items() if k in ('w1s', 'w2s', 'w3s', 'W1', 'W2', 'W3', 'Wg')}
    del _L0_ffn_all
    return {'x': x, 'txt': txt, 'L0_tok_W': _L0_tok_in['W'], 'L0_tok_b': _L0_tok_in['b'], 'L0_tok_cls_token': _L0_tok_in['cls_token'], 'L0_tok_pos_embedding': _L0_tok_in['pos_embedding'], 'L0_tok_gamma': _L0_tok_in['gamma'], 'L0_tok_beta': _L0_tok_in['beta'], 'L0_attn_Wq': _L0_attn_in['Wq'], 'L0_attn_bq': _L0_attn_in['bq'], 'L0_attn_Wk': _L0_attn_in['Wk'], 'L0_attn_bk': _L0_attn_in['bk'], 'L0_attn_Wv': _L0_attn_in['Wv'], 'L0_attn_bv': _L0_attn_in['bv'], 'L0_attn_Wg': _L0_attn_in['Wg'], 'L0_attn_bg': _L0_attn_in['bg'], 'L0_attn_Wo': _L0_attn_in['Wo'], 'L0_attn_bo': _L0_attn_in['bo'], 'L0_attn_gamma': _L0_attn_in['gamma'], 'L0_attn_beta': _L0_attn_in['beta'], 'L0_ffn_w1s': _L0_ffn_in['w1s'], 'L0_ffn_w2s': _L0_ffn_in['w2s'], 'L0_ffn_w3s': _L0_ffn_in['w3s'], 'L0_ffn_W1': _L0_ffn_in['W1'], 'L0_ffn_W2': _L0_ffn_in['W2'], 'L0_ffn_W3': _L0_ffn_in['W3'], 'L0_ffn_Wg': _L0_ffn_in['Wg']}

def reference(x, txt, L0_tok_W, L0_tok_b, L0_tok_cls_token, L0_tok_pos_embedding, L0_tok_gamma, L0_tok_beta, L0_attn_Wq, L0_attn_bq, L0_attn_Wk, L0_attn_bk, L0_attn_Wv, L0_attn_bv, L0_attn_Wg, L0_attn_bg, L0_attn_Wo, L0_attn_bo, L0_attn_gamma, L0_attn_beta, L0_ffn_w1s, L0_ffn_w2s, L0_ffn_w3s, L0_ffn_W1, L0_ffn_W2, L0_ffn_W3, L0_ffn_Wg):
    import jax
    import jax.numpy as jnp

    def _L0_tok_ref(x, W, b, cls_token, pos_embedding, gamma, beta):
        import jax, jax.numpy as jnp
        import numpy as np
        PATCH = 16
        EPS = 1e-05

        def _patchify(x, p):
            B, C, H, W = x.shape
            hp, wp = (H // p, W // p)
            x = x.reshape(B, C, hp, p, wp, p)
            x = x.transpose(0, 2, 4, 1, 3, 5)
            return x.reshape(B, hp * wp, C * p * p)
        B = x.shape[0]
        patches = _patchify(x, PATCH)
        tok = jnp.einsum('bnd,de->bne', patches, W) + b
        cls = jnp.broadcast_to(cls_token, (B, 1, tok.shape[-1]))
        h = jnp.concatenate([cls, tok], axis=1) + pos_embedding
        mu = jnp.mean(h, axis=-1, keepdims=True)
        var = jnp.mean(jnp.square(h - mu), axis=-1, keepdims=True)
        out = (h - mu) * jax.lax.rsqrt(var + EPS) * gamma + beta
        return out

    def _L0_attn_ref(x, Wq, bq, Wk, bk, Wv, bv, Wg, bg, Wo, bo, gamma, beta):
        import jax, jax.numpy as jnp
        import numpy as np
        import math
        D_MODEL = 256
        N_HEADS = 16
        D_HEAD = D_MODEL // N_HEADS
        DECAY_MAX = 0.99
        LN_EPS = 1e-05

        def _decay_mask(S):
            i = jnp.arange(S, dtype=jnp.float32)[:, None]
            j = jnp.arange(S, dtype=jnp.float32)[None, :]
            diff = i - j
            return jnp.where(diff >= 0, jnp.power(jnp.float32(DECAY_MAX), diff), 0.0)
        B, S, D = x.shape
        H, DH = (N_HEADS, D_HEAD)
        Q = (x @ Wq + bq).reshape(B, S, H, DH).transpose(0, 2, 1, 3)
        K = (x @ Wk + bk).reshape(B, S, H, DH).transpose(0, 2, 1, 3)
        V = (x @ Wv + bv).reshape(B, S, H, DH).transpose(0, 2, 1, 3)
        scores = jnp.einsum('bhsd,bhtd->bhst', Q, K) / math.sqrt(DH)
        mask = _decay_mask(S)
        retained = jnp.einsum('bhst,bhtd->bhsd', scores * mask, V)
        retained = retained.transpose(0, 2, 1, 3).reshape(B, S, D)
        mu = jnp.mean(retained, axis=-1, keepdims=True)
        var = jnp.var(retained, axis=-1, keepdims=True)
        normed = (retained - mu) * jax.lax.rsqrt(var + LN_EPS) * gamma + beta
        G = jax.nn.sigmoid(x @ Wg + bg)
        return normed * G @ Wo + bo

    def _L0_ffn_ref(x, w1s, w2s, w3s, W1, W2, W3, Wg):
        import jax, jax.numpy as jnp
        import numpy as np
        HIDDEN = 256
        INTER = 1024
        N_EXPERTS = 8

        def geglu(x, w1, w2, w3):
            return jax.nn.gelu(x @ w1, approximate=False) * (x @ w2) @ w3
        B, T, C = x.shape
        xf = x.reshape(-1, C)
        shared = geglu(xf, w1s, w2s, w3s)
        logits = xf @ Wg
        idx = jnp.argmax(logits, axis=-1)
        final = jnp.zeros_like(xf)
        for e in range(N_EXPERTS):
            y = geglu(xf, W1[e], W2[e], W3[e])
            final = final + jnp.where((idx == e)[:, None], y, 0.0)
        return (shared + final).reshape(B, T, C)
    h = _L0_tok_ref(x, L0_tok_W, L0_tok_b, L0_tok_cls_token, L0_tok_pos_embedding, L0_tok_gamma, L0_tok_beta)
    h = jnp.concatenate([h, txt], axis=1)
    h = h + _L0_attn_ref(_layernorm(h, axis=-1), L0_attn_Wq, L0_attn_bq, L0_attn_Wk, L0_attn_bk, L0_attn_Wv, L0_attn_bv, L0_attn_Wg, L0_attn_bg, L0_attn_Wo, L0_attn_bo, L0_attn_gamma, L0_attn_beta)
    h = h + _L0_ffn_ref(_layernorm(h, axis=-1), L0_ffn_w1s, L0_ffn_w2s, L0_ffn_w3s, L0_ffn_W1, L0_ffn_W2, L0_ffn_W3, L0_ffn_Wg)
    return h

_drawn_inputs = setup_inputs


def setup_inputs(seed=0):
    import zlib

    import numpy as np

    out = dict(_drawn_inputs(seed))
    spreads = {'L0_tok_b': (0.0, 0.1),
     'L0_tok_gamma': (1.0, 0.2),
     'L0_tok_beta': (0.0, 0.1),
     'L0_attn_bq': (0.0, 0.1),
     'L0_attn_bk': (0.0, 0.1),
     'L0_attn_bv': (0.0, 0.1),
     'L0_attn_bg': (0.0, 0.8),
     'L0_attn_bo': (0.0, 0.1),
     'L0_attn_gamma': (1.0, 0.2),
     'L0_attn_beta': (0.0, 0.555)}
    factors = {}
    for name, (base, spread) in spreads.items():
        noise = np.random.default_rng([zlib.crc32(name.encode()), seed]).standard_normal(out[name].shape)
        drawn = base * np.exp(spread * noise) if base else spread * noise
        out[name] = jnp.asarray(drawn.astype(out[name].dtype))
    for name, factor in factors.items():
        out[name] = (out[name] * factor).astype(out[name].dtype)
    return out
```

```python
from contextlib import ExitStack

import concourse.bass as bass
import numpy as np
from concourse import mybir

F32 = mybir.dt.float32
F32R = mybir.dt.float32r
I32 = mybir.dt.int32
ALU = mybir.AluOpType
ACT = mybir.ActivationFunctionType
AX = mybir.AxisListType

P = 128
EPS = 1e-5
DECAY = 0.99
HEADS = 16
DH = 16
PATCH = 16
GB = 4
E_ROUTED = 8
ROWS = 128


def shapes_of(B, C, HW, S_TXT, D, F):
    z = {}
    z["B"], z["C"], z["HW"], z["D"], z["F"] = B, C, HW, D, F
    z["HP"] = HW // PATCH
    z["NP"] = z["HP"] ** 2
    z["NC"] = z["NP"] + 1
    z["S"] = z["NC"] + S_TXT
    z["T"] = B * z["S"]
    z["NG"] = B // GB
    z["SH_TILES"] = -(-z["T"] // ROWS)
    z["MAX_ROUTED"] = (z["T"] - E_ROUTED) // ROWS + E_ROUTED
    return z


def constants(z):
    S = z["S"]
    n_thr = -(-z["T"] // ROWS)
    cols, parts = {}, []

    def put(name, a):
        full = np.zeros((P, a.shape[1]), np.float32)
        full[:a.shape[0]] = a
        at = sum(x.shape[1] for x in parts)
        cols[name] = (at, at + a.shape[1])
        parts.append(full)

    put("ident", np.eye(P, dtype=np.float32))
    t = np.arange(S)
    put("earlier", (t[:, None] < t[None, :]).astype(np.float32))
    put("ones", np.ones((P, P), np.float32))
    diff = (t[None, :] - t[:, None]).astype(np.float32)
    decay = np.power(np.float32(DECAY), np.maximum(diff, 0), dtype=np.float32)
    put("decay", np.where(diff >= 0, decay / np.float32(DH ** 0.5), 0).astype(np.float32))
    e = np.arange(E_ROUTED, dtype=np.float32)[None, :]
    put("expert", np.repeat(e, P, 0))
    put("expert_late", np.repeat(e + E_ROUTED, P, 0))
    thr = np.arange(n_thr, dtype=np.float32)[None, :] * ROWS
    thr[0, 0] = -1
    put("thr", np.repeat(thr, P, 0))
    put("tile", np.repeat(np.arange(z["MAX_ROUTED"], dtype=np.float32)[None, :], P, 0))
    head = np.arange(P) // DH
    put("even", (head % 2 == 0).astype(np.float32)[:, None])
    put("odd", (head % 2 == 1).astype(np.float32)[:, None])
    return np.concatenate(parts, 1), cols


def build(nc, a, out, z, cols):
    B, C, D, F, S, NC, NP, HP, HW, T = (z[k] for k in ("B", "C", "D", "F", "S", "NC", "NP", "HP", "HW", "T"))
    NG, SH, MAXR = z["NG"], z["SH_TILES"], z["MAX_ROUTED"]
    KD = D // P
    KX = C * PATCH * PATCH // P
    GS = GB * S
    QR = HP * B
    XH = HP // 2 * QR
    ZP = 84
    HALF = F // 2
    FC = HALF // P
    WCOLS = KD * F
    E = E_ROUTED
    NTHR = cols["thr"][1] - cols["thr"][0]
    X_ROWS = (SH + MAXR + 2) * ROWS

    xs = nc.dram_tensor("xs", (X_ROWS, D), F32, kind="Internal").ap()
    ys = nc.dram_tensor("ys", ((SH + MAXR) * ROWS, D), F32, kind="Internal").ap()
    hs = nc.dram_tensor("hs", (SH * ROWS, D), F32, kind="Internal").ap()
    row_d = nc.dram_tensor("row_d", (SH * ROWS, 1), I32, kind="Internal").ap()

    with ExitStack() as ctx:
        base = -(-nc.sbuf_base // 64) * 64
        part = 3 * WCOLS * 4
        kept = [base, base + 2 * part]
        spare = [base + 2 * part, base + 4 * part]
        kept[0], kept[1] = base + 4 * part, nc.sbuf_usable_end

        def sb(name, shape, dt=F32, at=kept):
            size = -(-int(np.prod(shape[1:])) * 4 // 64) * 64
            assert at[0] + size <= at[1], f"no room for {name}: {at}"
            at[0] += size
            return nc.alloc_sbuf_tensor_at(name, shape, dt, offset=at[0] - size)

        def ps(name, shape):
            return ctx.enter_context(nc.psum_tensor(name, shape, F32))

        def sem(name):
            return ctx.enter_context(nc.semaphore(name))

        const = sb("const", [P, max(c[1] for c in cols.values())])
        w_parts = sb("w_parts", [P, 2, 2, 3 * WCOLS], F32R, at=[base, base + 4 * part])
        w_hi, w_lo = w_parts[:, :, 0, :], w_parts[:, :, 1, :]
        raw = [sb(f"raw{m}", [P, WCOLS]) for m in range(3)]
        rows_sb = sb("rows_sb", [P, B], I32)
        tab = sb("tab", [P, MAXR + 2], I32)
        h = sb("h", [S, B, D])

        def cst(name, n=P):
            lo, hi = cols[name]
            return const[0:n, lo:hi]

        rest = list(kept)
        fronts = [spare, list(rest)]

        def front_sb(name, shape, dt=F32):
            size = -(-int(np.prod(shape[1:])) * 4 // 64) * 64
            at = next(x for x in fronts if x[0] + size <= x[1])
            return sb(name, shape, dt, at=at)

        eps = front_sb("eps", [P, 1])
        tick = front_sb("tick", [1, 1])
        even = [base, base + 2 * part]
        img = sb("img", [QR, C, PATCH * HW], at=even)
        img_p = sb("img_p", [QR, C, PATCH * HW], at=even)
        zero = front_sb("zero", [ZP, D])
        w_tok = front_sb("w_tok", [P, KX, D])
        w_q, w_k, w_v, w_g, w_o = (front_sb(n, [P, KD, D]) for n in ("w_q", "w_k", "w_v", "w_g", "w_o"))
        w_r = front_sb("w_r", [P, KD, E])
        vec_rows = front_sb("vec_rows", [6 * KD, P])
        vec = front_sb("vec", [P, 6 * KD])
        row_bias = front_sb("row_bias", [NC, D])
        gam_b = front_sb("gam_b", [NC, D])
        bet_b = front_sb("bet_b", [NC, D])
        bv_b = front_sb("bv_b", [S, D])
        bo_b = front_sb("bo_b", [S, D])
        pt = front_sb("pt", [P, KX, B * NP])
        tokT_all = front_sb("tokT_all", [P, KD, B, NC])
        tokT = front_sb("tokT", [P, KD, GB, S])
        tok = front_sb("tok", [NC, GB, D])
        xn = front_sb("xn", [S, GB, D])
        xnT = front_sb("xnT", [P, KD, GS])
        qq = front_sb("qq", [P, KD, GB, 2, S])
        kT = front_sb("kT", [P, KD, GS])
        vv = front_sb("vv", [S, GB, D])
        gate = front_sb("gate", [P, KD, GS])
        pr = front_sb("pr", [S, 2, HEADS, S])
        rn = front_sb("rn", [S, GB, D])
        uT = front_sb("uT", [P, KD, GS])
        h2 = front_sb("h2", [S, GB, D])
        xn2 = front_sb("xn2", [S, GB, D])
        x2T = front_sb("x2T", [P, KD, GS])
        lg = front_sb("lg", [S, B, E])
        lns = {n: {k: front_sb(f"{n}_{k}s", [S, GB] + w) for k, w in
                   (("st", [6]), ("mv", [2]), ("sd", []), ("r", []), ("nmr", []))} for n in ("lt", "lx", "lr", "l2")}
        mx = front_sb("mx", [S, B])
        eq = front_sb("eq", [S, B, E])
        idx = front_sb("idx", [S, B])
        pick = front_sb("pick", [S, B, E])
        tot = front_sb("tot", [S, E, B])
        cin = front_sb("cin", [S, E, B])
        cex = front_sb("cex", [S, E, B])
        cnt = front_sb("cnt", [S, E])
        over = front_sb("over", [S, E, NTHR])
        tiles = front_sb("tiles", [S, E])
        tin = front_sb("tin", [S, E])
        tex = front_sb("tex", [S, E])
        delta = front_sb("delta", [S, E])
        pos = front_sb("pos", [S, B, E])
        posm = front_sb("posm", [S, B, E])
        row_f = front_sb("row_f", [S, B])
        ord_c = front_sb("ord_c", [1, MAXR, E])
        tab_f = front_sb("tab_f", [1, MAXR + 2])

        rear = list(rest)
        xr = sb("xr", [ROWS, D], at=rear)
        xT_hi = sb("xT_hi", [P, KD, ROWS], F32R, at=rear)
        xT_lo = sb("xT_lo", [P, KD, ROWS], F32R, at=rear)
        gl = sb("gl", [ROWS, 2, HALF], at=rear)
        hid = sb("hid", [ROWS, 2, HALF], at=rear)
        hT_hi = sb("hT_hi", [P, 2, FC, ROWS], F32R, at=rear)
        hT_lo = sb("hT_lo", [P, 2, FC, ROWS], F32R, at=rear)
        y_sb = sb("y_sb", [ROWS, 2, D], at=rear)
        row_t = sb("row_t", [ROWS, SH], I32, at=rear)
        h_fl = sb("h_fl", [ROWS, SH, D], at=rear)
        ysh = sb("ysh", [ROWS, SH, D], at=rear)
        yg = sb("yg", [ROWS, SH, D], at=rear)

        pS = ps("pS", [P, 4, 512])
        pT = ps("pT", [P, 2, 512])
        pV = ps("pV", [P, 2, 512])
        pU = [(pS[:, 0, :], pS[:, 1, :]), (pS[:, 2, :], pS[:, 3, :])]
        pH = [pT[:, 0, :], pT[:, 1, :]]
        pY, pX = pV[:, 0, 0:D], pV[:, 1, 0:KD * ROWS]

        names = """zero_y last_st cls_ok const_in attn_in vecs_in txt_in img_in rest_in w0_in w1_in w2_in eps_set col_set zero_set zero_out
            vec_t vec_ok xtr pt_act pt_dve tokmm tokT_ok imgp_act imgp_dve emb_act emb_dve tok_t tok_ok ht_c ht_ok xn_ok xn_t xnT_act xnT_dve
            q_mm k_mm v_mm g_mm q_ok k_ok v_ok g_ok sc p_ok pv rn_ok rn_t z_ok u_ok o_mm hb_ok h2_ok xn2_ok
            h2_st xn2_st xn2_cp x2_t x2T_act x2T_dve lg_mm lg_ok pick_ok count_mm route rows_ok tab_ok row_st
            scattered wsp_hi wsp_lo12 wsp_lo3 xr_in xt xhi xlo u0 u1 g0 g1 hid0 hid1 tr0 tr1 hi0 hi1 lo0 lo1
            y_mm y_ev y_st row_in h_in ysh_in gathered sum1 sum2 out_st""".split()
        s = {n: sem(n) for n in names}
        for n in lns:
            for k in ("st", "mv", "sd", "r", "nmr"):
                s[f"{n}_{k}"] = sem(f"{n}_{k}")

        x_in = a["x"]
        tokens = xs[0:T, :].rearrange("(b t) d -> t b d", t=S)

        block = ctx.enter_context(nc.Block())

        @block.sync
        def _(sp):
            sp.dma_start(const[:, :], a["const"]).then_inc(s["const_in"], 16)
            for r in range(HP):
                sp.dma_start(img[r * B:(r + 1) * B, :, :],
                             x_in[:, :, r * PATCH:(r + 1) * PATCH, :].rearrange("b c r w -> b c (r w)")).then_inc(s["img_in"], 16)
            for n, v in enumerate(("tok_b", "bq", "bk", "bg", "ga", "ba")):
                sp.dma_start(vec_rows[n * KD:(n + 1) * KD, :],
                             a[v].rearrange("(m p) -> m p", p=P)).then_inc(s["vecs_in"], 16)
            sp.dma_start(w_tok[:, :, :], a["tok_W"].rearrange("(k p) n -> p k n", p=P)).then_inc(s["rest_in"], 16)
            sp.dma_start(row_bias[:, :], a["pos"][0]).then_inc(s["rest_in"], 16)
            sp.dma_start(tok[0:1, 0, :], a["cls"][0]).then_inc(s["rest_in"], 16)
            sp.dma_start(gam_b[:, :], a["tg"].partition_broadcast(NC)).then_inc(s["rest_in"], 16)
            sp.dma_start(bet_b[:, :], a["tb"].partition_broadcast(NC)).then_inc(s["rest_in"], 16)
            sp.dma_start(bv_b[:, :], a["bv"].partition_broadcast(S)).then_inc(s["rest_in"], 16)
            sp.dma_start(bo_b[:, :], a["bo"].partition_broadcast(S)).then_inc(s["rest_in"], 16)
            sp.dma_start(h[NC:S, :, :], a["txt"].rearrange("b t d -> t b d")).then_inc(s["txt_in"], 16)
            for w, v in ((w_q, "Wq"), (w_k, "Wk"), (w_v, "Wv"), (w_g, "Wg"), (w_o, "Wo"), (w_r, "Wr")):
                sp.dma_start(w[:, :, :], a[v].rearrange("(k p) n -> p k n", p=P)).then_inc(s["attn_in"], 16)
            for m, v in enumerate(("w1s", "w2s", "w3s")):
                sp.dma_start(raw[m][:, :].rearrange("p (k n) -> p k n", k=a[v].shape[0] // P),
                             a[v].rearrange("(k p) n -> p k n", p=P)).then_inc(s[f"w{m}_in"], 16)
            with sp.Fori(1, E + 1) as k:
                for m, v in enumerate(("W1", "W2", "W3")):
                    if m < 2:
                        sp.wait_ge(s["wsp_lo12"], 2 * k - 1 + m)
                    else:
                        sp.wait_ge(s["wsp_lo3"], k)
                    n = a[v].shape[2]
                    sp.dma_start(raw[m][:, :].rearrange("p (k n) -> p k n", n=n),
                                 a[v][bass.ds(k - 1, 1)].rearrange("e (k p) n -> p (e k) n", p=P))\
                        .then_inc(s[f"w{m}_in"], 16)
            sp.wait_ge(s["last_st"], 16)
            full = (SH - 1)
            last = T - full * ROWS
            sp.dma_start(h_fl[:, 0:full, :], hs[0:full * ROWS, :].rearrange("(c p) d -> p c d", p=ROWS)).then_inc(s["h_in"], 16)
            sp.dma_start(h_fl[0:last, full, :], hs[full * ROWS:T, :]).then_inc(s["h_in"], 16)
            sp.dma_start(ysh[:, 0:full, :], ys[0:full * ROWS, :].rearrange("(c p) d -> p c d", p=ROWS)).then_inc(s["ysh_in"], 16)
            sp.dma_start(ysh[0:last, full, :], ys[full * ROWS:T, :]).then_inc(s["ysh_in"], 16)
            flat = out.rearrange("b t d -> (b t) d")
            for c in range(SH):
                n = min(ROWS, T - c * ROWS)
                sp.wait_ge(s["sum2"], c + 1)
                sp.dma_start(flat[c * ROWS:c * ROWS + n, :], h_fl[0:n, c, :]).then_inc(s["out_st"], 16)
            sp.wait_ge(s["out_st"], 16 * SH)

        @block.gpsimd
        def _(pool):
            pool.memset(zero[:, :], 0.0).then_inc(s["zero_set"], 1)
            pool.memset(eps[:, :], EPS).then_inc(s["eps_set"], 1)
            pool.memset(tokT_all[:, :, :, 0:1], 0.0)
            pool.memset(tokT[:, :, :, :], 0.0).then_inc(s["col_set"], 1)
            pool.wait_ge(s["zero_set"], 1)
            n = (X_ROWS - T) // ZP
            assert (X_ROWS - T) % ZP == 0
            pool.dma_start(xs[T:X_ROWS, :].rearrange("(c p) d -> p c d", p=ZP),
                           zero[:, :].unsqueeze(1).to_broadcast([ZP, n, D])).then_inc(s["zero_out"], 16)
            n = MAXR - E
            pool.dma_start(ys[(SH + E) * ROWS:, :].rearrange("(p c) d -> p c d", c=2 * n),
                           zero[0:ROWS // 2, :].unsqueeze(1).to_broadcast([ROWS // 2, 2 * n, D])).then_inc(s["zero_y"], 16)
            pool.wait_ge(s["rest_in"], 112)
            pool.wait_ge(s["txt_in"], 16)

            def residual_bias(g):
                pool.wait_ge(s["ht_ok"], g + 1)
                pool.wait_ge(s["h2_st"], 16 * g)
                pool.wait_ge(s["xn2_ok"], g)
                pool.tensor_tensor(h2[:, :, :], h[:, bass.ds(g * GB, GB), :],
                                   bo_b[:, :].unsqueeze(1).to_broadcast([S, GB, D]), ALU.add).then_inc(s["hb_ok"], 1)

            residual_bias(0)
            with pool.Fori(1, NG) as i:
                residual_bias(i)

            def lower(k, m, par):
                pool.wait_ge(s["wsp_hi"], 3 * k + m + 1)
                sl = bass.ds(m * WCOLS, WCOLS)
                pool.tensor_tensor(w_lo[:, par, sl], raw[m][:, :], w_hi[:, par, sl].bitcast(F32), ALU.subtract)\
                    .then_inc(s["wsp_lo12"], 1)

            lower(0, 0, 0)
            lower(0, 1, 0)
            pool.wait_ge(s["rows_ok"], 1)
            pool.wait_ge(s["xn2_cp"], 16 * NG)
            pool.wait_ge(s["zero_out"], 16)
            for b in range(B):
                pool.indirect_dma_start(out=xs, out_offset=bass.IndirectOffsetOnAxis(ap=rows_sb[0:S, b:b + 1], axis=0),
                                        in_=h[0:S, b, :], in_offset=None).then_inc(s["scattered"], 16)
            pool.dma_start(row_d[0:T, :].rearrange("(b t) o -> t (b o)", t=S), rows_sb[0:S, :],
                           allow_slow_non_contiguous=True).then_inc(s["row_st"], 16)
            pool.wait_ge(s["row_st"], 16)
            full, rest_rows = T // ROWS, T % ROWS
            pool.dma_start(row_t[:, 0:full], row_d[0:full * ROWS, :].rearrange("(c p) o -> p (c o)", p=ROWS),
                           allow_slow_non_contiguous=True)\
                .then_inc(s["row_in"], 16)
            pool.dma_start(row_t[0:rest_rows, full:full + 1], row_d[full * ROWS:T, :]).then_inc(s["row_in"], 16)
            with pool.Fori(0, E // 2) as kk:
                for r in (1, 2):
                    lower(2 * kk + r, 0, r % 2)
                    lower(2 * kk + r, 1, r % 2)
            pool.wait_ge(s["row_in"], 32)
            pool.wait_ge(s["last_st"], 16)
            for c in range(SH):
                n = min(ROWS, T - c * ROWS)
                pool.indirect_dma_start(out=yg[0:n, c, :], out_offset=None, in_=ys,
                                        in_offset=bass.IndirectOffsetOnAxis(ap=row_t[0:n, c:c + 1], axis=0))\
                    .then_inc(s["gathered"], 16)

        @block.tensor
        def _(pe):
            ident = cst("ident")

            def mm(o, l, r, start, stop):
                return pe.matmul(o, l, r, start=start, stop=stop)

            banks = [pS[:, r, :] for r in range(4)] + [pT[:, 0, :], pT[:, 1, :], pV[:, 0, :], pV[:, 1, :]]

            def x1():
                for j in range(2 * KX):
                    pe.wait_ge(s["imgp_dve"], 1)
                    if j >= 2 * KX // C:
                        pe.wait_ge(s["imgp_act"], 1)
                    if j >= 4 * KX // C:
                        pe.wait_ge(s["imgp_dve"], 2)
                    if j >= 8:
                        pe.wait_ge(s["pt_act"] if j % 2 == 0 else s["pt_dve"], (j - 8) // 2 + 1)
                    k = j // 2
                    for q in range(HP // 2):
                        wp = j % 2 * (HP // 2) + q
                        at = wp * PATCH * PATCH + (k % 2) * P
                        last = pe.transpose(banks[j % 8][:, q * QR:(q + 1) * QR], img_p[:, k // 2, at:at + P],
                                            ident[0:QR, 0:QR])
                    last.then_inc(s["xtr"], 1)

            def x2():
                pe.wait_ge(s["pt_act"], 4)
                pe.wait_ge(s["pt_dve"], 4)
                for k in range(KX):
                    pe.wait_ge(s["pt_act"], k + 1)
                    pe.wait_ge(s["pt_dve"], k + 1)
                    for m in range(KD):
                        for hf in range(2):
                            last = mm(banks[4 + 2 * m + hf][:, 0:XH], w_tok[:, k, m * P:(m + 1) * P],
                                      pt[:, k, hf * XH:(hf + 1) * XH], k == 0, k == KX - 1)
                last.then_inc(s["tokmm"], 1)

            def x3(g):
                pe.wait_ge(s["tokT_ok"], g + 1)
                pe.wait_ge(s["v_ok"], g)
                if not isinstance(g, int) or g > 1:
                    pe.wait_ge(s["x2T_dve"], g - 1)
                    pe.wait_ge(s["x2T_act"], g - 1)
                for b in range(GB):
                    for m in range(KD):
                        at = (b % 2) * D + m * P
                        last = pe.transpose(pT[0:S, b // 2, at:at + P], tokT[:, m, b, :], ident)
                last.then_inc(s["tok_t"], 1)

            def transposes(src, name):
                for m in range(KD):
                    for b in range(GB):
                        last = pe.transpose(pT[:, m, b * S:(b + 1) * S], src[:, b, m * P:(m + 1) * P], ident[0:S, 0:S])
                    last.then_inc(s[name], 1)

            def x6(g):
                pe.wait_ge(s["xn_ok"], g + 1)
                transposes(xn, "xn_t")

            def project(bank, w, name):
                for m in range(KD):
                    for k in range(KD):
                        last = mm(pS[:, bank + m, 0:GS], w[:, k, m * P:(m + 1) * P], xnT[:, k, :], k == 0, k == KD - 1)
                    last.then_inc(s[name], 1)

            def x7(g):
                pe.wait_ge(s["xnT_act"], g + 1)
                pe.wait_ge(s["xnT_dve"], g + 1)
                project(2, w_q, "q_mm")
                pe.wait_ge(s["h2_ok"], g)
                project(0, w_k, "k_mm")
                pe.wait_ge(s["z_ok"], g)
                for b in range(GB):
                    for k in range(KD):
                        last = mm(pT[0:S, b // 2, (b % 2) * D:(b % 2 + 1) * D], xnT[:, k, b * S:(b + 1) * S],
                                  w_v[:, k, :], k == 0, k == KD - 1)
                last.then_inc(s["v_mm"], 1)
                pe.wait_ge(s["rn_ok"], g)
                for m in range(KD):
                    for k in range(KD):
                        last = mm(pV[:, m, 0:GS], w_g[:, k, m * P:(m + 1) * P], xnT[:, k, :], k == 0, k == KD - 1)
                    last.then_inc(s["g_mm"], 1)

            def y1(g):
                pe.wait_ge(s["q_ok"], g + 1)
                pe.wait_ge(s["k_ok"], g + 1)
                pe.wait_ge(s["lg_ok"], g)

                def scores(b):
                    if b:
                        pe.wait_ge(s["p_ok"], GB * g + b)
                    for m in range(KD):
                        for r in range(4):
                            q = slice(32 * r, 32 * r + 32)
                            last = mm(pS[0:S, r, m * 2 * S:(m + 1) * 2 * S], kT[q, m, b * S:(b + 1) * S],
                                      qq[q, m, b, :, :], True, True)
                    last.then_inc(s["sc"], 1)

                def retain(b):
                    pe.wait_ge(s["p_ok"], GB * g + b + 1)
                    if b == 0:
                        pe.wait_ge(s["v_ok"], g + 1)
                        pe.wait_ge(s["g_ok"], g + 1)
                    for hd in range(HEADS):
                        m, r, o = hd // 8, hd % 8 // 2, hd % 2
                        last = mm(pV[0:S, b // 2, (b % 2) * D + hd * DH:(b % 2) * D + (hd + 1) * DH],
                                  pr[:, b % 2, r * 4 + m * 2 + o, :], vv[:, b, hd * DH:(hd + 1) * DH], True, True)
                    last.then_inc(s["pv"], 1)

                scores(0)
                for b in range(1, GB):
                    scores(b)
                    retain(b - 1)
                retain(GB - 1)

            def y3(g, last=False):
                pe.wait_ge(s["rn_ok"], g + 1)
                if not last:
                    pe.wait_ge(s["xnT_act"], g + 2)
                    pe.wait_ge(s["xnT_dve"], g + 2)
                else:
                    pe.wait_ge(s["x2T_act"], g)
                    pe.wait_ge(s["x2T_dve"], g)
                transposes(rn, "rn_t")

            def y4(g):
                pe.wait_ge(s["u_ok"], g + 1)
                for b in range(GB):
                    for k in range(KD):
                        last = mm(pS[0:S, b // 2, (b % 2) * D:(b % 2 + 1) * D], uT[:, k, b * S:(b + 1) * S],
                                  w_o[:, k, :], k == 0, k == KD - 1)
                last.then_inc(s["o_mm"], 1)

            def y6(g, last=False):
                pe.wait_ge(s["xn2_ok"], g + 1)
                if not last:
                    pe.wait_ge(s["v_ok"], g + 2)
                    pe.wait_ge(s["q_ok"], g + 2)
                transposes(xn2, "x2_t")
                pe.wait_ge(s["x2T_act"], g + 1)
                pe.wait_ge(s["x2T_dve"], g + 1)
                for b in range(GB):
                    for k in range(KD):
                        last = mm(pS[0:S, 3, b * E:(b + 1) * E], x2T[:, k, b * S:(b + 1) * S], w_r[:, k, :],
                                  k == 0, k == KD - 1)
                last.then_inc(s["lg_mm"], 1)

            pe.wait_ge(s["const_in"], 16)
            pe.wait_ge(s["vecs_in"], 96)
            pe.transpose(pV[:, 0, 0:6 * KD], vec_rows[:, :], ident[0:6 * KD, 0:6 * KD]).then_inc(s["vec_t"], 1)
            pe.wait_ge(s["vec_ok"], 1)
            x1()
            pe.wait_ge(s["rest_in"], 112)
            x2()
            pe.wait_ge(s["emb_act"], 1)
            pe.wait_ge(s["emb_dve"], 1)
            x3(0)
            x6(0)
            pe.wait_ge(s["attn_in"], 96)
            x7(0)

            def step(i):
                x3(i + 1)
                y1(i)
                x6(i + 1)
                y3(i)
                y4(i)
                x7(i + 1)
                y6(i)
            step(0)
            with pe.Fori(1, NG - 1) as i:
                step(i)
            y1(NG - 1)
            y3(NG - 1, last=True)
            y4(NG - 1)
            y6(NG - 1, last=True)
            pe.wait_ge(s["pick_ok"], 1)
            picks = pick[:, :, :].rearrange("t b e -> t (b e)")
            mm(pV[0:S, 0, 0:B * E], cst("earlier", S), picks, True, True)
            mm(pV[0:S, 1, 0:B * E], cst("ones", S)[:, 0:S], picks, True, True).then_inc(s["count_mm"], 1)

            def x_transpose(t):
                pe.wait_ge(s["xr_in"], 16 * t + 16)
                for m in range(KD):
                    last = pe.transpose(pX[:, m * ROWS:(m + 1) * ROWS], xr[:, m * P:(m + 1) * P], ident)
                last.then_inc(s["xt"], 1)

            def up(hf, par, name):
                for k in range(KD):
                    xh, xl = xT_hi[:, k, :], xT_lo[:, k, :]
                    for part, st, w in ((xh, True, w_hi), (xh, False, w_lo), (xl, False, w_hi)):
                        for j in range(2):
                            at = j * WCOLS + k * F + hf * HALF
                            last = mm(pU[hf][j], part, w[:, par, at:at + HALF],
                                      k == 0 and st, k == KD - 1 and part is xl)
                last.then_inc(s[name], 1)

            def hid_transpose(hf, name):
                for c in range(FC):
                    last = pe.transpose(pH[hf][:, c * P:(c + 1) * P], hid[:, hf, c * P:(c + 1) * P], ident)
                last.then_inc(s[name], 1)

            def down(hf, par):
                for c in range(FC):
                    at = 2 * WCOLS + (hf * FC + c) * D
                    for n, (l, w) in enumerate(((hT_hi, w_hi), (hT_hi, w_lo), (hT_lo, w_hi))):
                        last = mm(pY, l[:, hf, c, :], w[:, par, at:at + D], hf == 0 and c == 0 and n == 0,
                                  hf == 1 and c == FC - 1 and n == 2)
                return last

            def slot(t, e, par, e1, par1, first=False, final=False):
                if not final:
                    pe.wait_ge(s["wsp_hi"], 3 * e + 2)
                    pe.wait_ge(s["wsp_lo12"], 2 * e + 2)
                    pe.wait_ge(s["xhi"], t + 1)
                    pe.wait_ge(s["xlo"], t + 1)
                    pe.wait_ge(s["hid0"], t)
                    up(0, par, "u0")
                if not first:
                    pe.wait_ge(s["hid1"], t)
                    pe.wait_ge(s["lo1"], t - 1)
                    hid_transpose(1, "tr1")
                    pe.wait_ge(s["lo0"], t)
                    pe.wait_ge(s["wsp_hi"], 3 * e1 + 3)
                    pe.wait_ge(s["wsp_lo3"], e1 + 1)
                    pe.wait_ge(s["y_ev"], t - 1)
                    down(0, par1)
                if not final:
                    up(1, par, "u1")
                    x_transpose(t + 1)
                if not first:
                    pe.wait_ge(s["lo1"], t)
                    down(1, par1).then_inc(s["y_mm"], 1)
                if not final:
                    pe.wait_ge(s["hid0"], t + 1)
                    hid_transpose(0, "tr0")

            x_transpose(0)
            slot(0, 0, 0, 0, 0, first=True)
            slot(1, 0, 0, 0, 0)
            with pe.Fori(2, SH) as t:
                slot(t, 0, 0, 0, 0)
            pe.wait_ge(s["tab_ok"], 1)
            nt = pe.value_load(tab[0:1, MAXR + 1:MAXR + 2], min_val=SH + E - 1, max_val=SH + MAXR - 1) + 1
            with pe.Fori(SH, nt) as t:
                e1 = pe.value_load(tab[0:1, bass.ds(t - SH, 1)], min_val=0, max_val=E)
                e = pe.value_load(tab[0:1, bass.ds(t - SH + 1, 1)], min_val=1, max_val=E)
                slot(t, e, bass.ds(e % 2, 1), e1, bass.ds(e1 % 2, 1))
            slot(nt, E, 0, E, 0, final=True)

        @block.scalar
        def _(act):
            def norm(name, src, dst, done, n, g):
                l = lns[name]
                act.wait_ge(s[name + "_mv"], g + 1)
                act.activation(l["sd"][0:n, :], l["mv"][0:n, :, 1], ACT.Sqrt, bias=eps[0:n, :]).then_inc(s[name + "_sd"], 1)
                if dst is None:
                    return
                act.wait_ge(s[name + "_nmr"], g + 1)
                for b in range(GB):
                    last = act.activation(dst[:, b, :], src(b), ACT.Identity, bias=l["nmr"][0:n, b:b + 1],
                                          scale=l["r"][0:n, b:b + 1])
                last.then_inc(s[done], 1)

            def regroup(c):
                act.wait_ge(s["img_in"], 16 * HP)
                act.activation(img_p[:, c, :].rearrange("q (wp r v) -> q wp r v", r=PATCH, v=PATCH),
                           img[:, c, :].rearrange("q (r wp v) -> q wp r v", r=PATCH, v=PATCH), ACT.Copy).then_inc(s["imgp_act"], 1)

            def x1():
                for j in range(0, 2 * KX, 2):
                    act.wait_ge(s["xtr"], j + 1)
                    act.activation(pt[:, j // 2, 0:XH], ([pS[:, r, :] for r in range(4)] + [pT[:, 0, :], pT[:, 1, :],
                                   pV[:, 0, :], pV[:, 1, :]])[j % 8][:, 0:XH], ACT.Copy).then_inc(s["pt_act"], 1)
                act.wait_ge(s["tokmm"], 1)
                act.wait_ge(s["vec_ok"], 1)
                for hf in range(2):
                    dst = tokT_all[:, 0, :, 1:NC].rearrange("p b (hp wp) -> p wp hp b", wp=HP)
                    last = act.activation(dst[:, hf * HP // 2:(hf + 1) * HP // 2],
                                          pT[:, hf, 0:XH].rearrange("p (wp hp b) -> p wp hp b", hp=HP, b=B),
                                          ACT.Identity, bias=vec[:, 0:1])
                last.then_inc(s["emb_act"], 1)

            def x2(g):
                act.wait_ge(s["tok_t"], g)
                act.activation(tokT[:, :, :, 0:NC], tokT_all[:, :, bass.ds(g * GB, GB), :], ACT.Copy).then_inc(s["tokT_ok"], 1)

            def x5(g):
                act.wait_ge(s["xn_t"], 2 * g)
                norm("lx", lambda b: h[:, bass.ds(g * GB + b, 1), :].rearrange("t b d -> t (b d)"), xn, "xn_ok", S, g)

            def x6(g):
                act.wait_ge(s["xn_t"], 2 * g + 1)
                act.wait_ge(s["g_mm"], 2 * g)
                act.activation(xnT[:, 0, :], pT[:, 0, 0:GS], ACT.Copy).then_inc(s["xnT_act"], 1)

            def x7(g):
                act.wait_ge(s["sc"], GB * g)
                for m in range(KD):
                    act.wait_ge(s["k_mm"], 2 * g + m + 1)
                    last = act.activation(kT[:, m, :], pS[:, m, 0:GS], ACT.Identity, bias=vec[:, 2 * KD + m:2 * KD + m + 1])
                last.then_inc(s["k_ok"], 1)
                act.wait_ge(s["u_ok"], g)
                for m in range(KD):
                    act.wait_ge(s["g_mm"], 2 * g + m + 1)
                    last = act.activation(gate[:, m, :], pV[:, m, 0:GS], ACT.Sigmoid, bias=vec[:, 3 * KD + m:3 * KD + m + 1])
                last.then_inc(s["g_ok"], 1)

            def y2(g):
                act.wait_ge(s["rn_t"], 2 * g)
                norm("lr", lambda b: pV[0:S, b // 2, (b % 2) * D:(b % 2 + 1) * D], rn, "rn_ok", S, g)

            def y3(g):
                act.wait_ge(s["o_mm"], g)
                for m in range(KD):
                    act.wait_ge(s["rn_t"], 2 * g + m + 1)
                    last = act.activation(uT[:, m, :], pT[:, m, 0:GS], ACT.Identity,
                                          scale=vec[:, 4 * KD + m:4 * KD + m + 1], bias=vec[:, 5 * KD + m:5 * KD + m + 1])
                last.then_inc(s["z_ok"], 1)

            def y5(g):
                act.wait_ge(s["xn2_st"], 16 * g)
                act.wait_ge(s["xn2_cp"], 16 * g)
                act.wait_ge(s["x2_t"], 2 * g)
                norm("l2", lambda b: h2[:, b, :], xn2, "xn2_ok", S, g)
                hrows = hs[0:T, :].rearrange("(b t) d -> t b d", t=S)
                act.dma_start(hrows[:, bass.ds(g * GB, GB), :], h2[:, :, :]).then_inc(s["h2_st"], 16)
                act.wait_ge(s["xn2_ok"], g + 1)
                act.dma_start(tokens[:, bass.ds(g * GB, GB), :], xn2[:, :, :]).then_inc(s["xn2_st"], 16)
                act.dma_start(h[0:S, bass.ds(g * GB, GB), :], xn2[:, :, :]).then_inc(s["xn2_cp"], 16)

            def y6(g):
                act.wait_ge(s["x2_t"], 2 * g + 1)
                act.wait_ge(s["lg_mm"], g)
                act.activation(x2T[:, 0, :], pT[:, 0, 0:GS], ACT.Copy).then_inc(s["x2T_act"], 1)

            def split_hi(k, m, par):
                act.wait_ge(s[f"w{m}_in"], 16 * k + 16)
                act.activation(w_hi[:, par, m * WCOLS:(m + 1) * WCOLS], raw[m][:, :], ACT.Copy).then_inc(s["wsp_hi"], 1)

            act.wait_ge(s["eps_set"], 1)
            regroup(1)
            x1()
            act.wait_ge(s["emb_act"], 1)
            act.wait_ge(s["emb_dve"], 1)
            act.wait_ge(s["col_set"], 1)
            x2(0)
            act.wait_ge(s["txt_in"], 16)
            norm("lt", None, None, None, NC, 0)
            x5(0)
            x6(0)
            act.wait_ge(s["vec_ok"], 1)
            x7(0)

            def step(i):
                x2(i + 1)
                norm("lt", None, None, None, NC, i + 1)
                x5(i + 1)
                x6(i + 1)
                y2(i)
                y3(i)
                x7(i + 1)
                y5(i)
                y6(i)
            step(0)
            with act.Fori(1, NG - 1) as i:
                step(i)
            for m in range(3):
                split_hi(0, m, 0)
            y2(NG - 1)
            y3(NG - 1)
            y5(NG - 1)
            y6(NG - 1)

            def load_rows(t):
                act.dma_start(xr[:, :], xs[bass.ds(t * ROWS, ROWS), :]).then_inc(s["xr_in"], 16)

            def x_hi(t):
                act.wait_ge(s["xt"], t + 1)
                act.activation(xT_hi[:, :, :].rearrange("p k n -> p (k n)"), pX, ACT.Copy).then_inc(s["xhi"], 1)

            def slot(t, split=None, first=False, final=False, gated=False):
                if not final:
                    act.wait_ge(s["u0"], t + 1)
                    act.wait_ge(s["hid0"], t)
                    act.activation(gl[:, 0, :], pU[0][0], ACT.Gelu).then_inc(s["g0"], 1)
                if not first:
                    act.wait_ge(s["tr1"], t)
                    act.wait_ge(s["y_mm"], t - 1)
                    act.activation(hT_hi[:, 1, :, :].rearrange("p c n -> p (c n)"), pH[1], ACT.Copy).then_inc(s["hi1"], 1)
                if split:
                    split(0)
                if not final:
                    act.wait_ge(s["u1"], t + 1)
                    act.wait_ge(s["hid1"], t)
                    act.activation(gl[:, 1, :], pU[1][0], ACT.Gelu).then_inc(s["g1"], 1)
                    x_hi(t + 1)
                    if gated:
                        act.wait_ge(s["scattered"], 16 * B)
                    load_rows(t + 2)
                if not first:
                    act.wait_ge(s["y_mm"], t)
                    y_at = bass.ds((t + 1) % 2, 1)
                    act.wait_ge(s["y_st"], 16 * (t - 1))
                    act.activation(y_sb[:, y_at, :].rearrange("p a d -> p (a d)"), pY, ACT.Copy).then_inc(s["y_ev"], 1)
                    act.wait_ge(s["y_ev"], t)
                    act.dma_start(ys[bass.ds((t - 1) * ROWS, ROWS), :],
                                  y_sb[:, y_at, :].rearrange("p a d -> p (a d)")).then_inc(s["last_st" if final else "y_st"], 16)
                if not final:
                    act.wait_ge(s["tr0"], t + 1)
                    act.activation(hT_hi[:, 0, :, :].rearrange("p c n -> p (c n)"), pH[0], ACT.Copy).then_inc(s["hi0"], 1)
                if split:
                    split(1)

            act.wait_ge(s["xn2_st"], 16 * NG)
            act.wait_ge(s["zero_out"], 16)
            act.wait_ge(s["zero_y"], 16)
            act.wait_ge(s["tab_ok"], 1)
            act.wait_ge(s["h2_st"], 16 * NG)
            load_rows(0)
            x_hi(0)
            load_rows(1)

            def split_first(n):
                for m in ((0, 1), (2,))[n]:
                    split_hi(1, m, 1)
            slot(0, split=split_first, first=True)
            slot(1)
            with act.Fori(2, SH - 2) as t:
                slot(t)
            with act.Fori(SH - 2, SH) as t:
                slot(t, gated=True)
            act.wait_ge(s["tab_ok"], 1)
            nt = act.value_load(tab[0:1, MAXR + 1:MAXR + 2], min_val=SH + E - 1, max_val=SH + MAXR - 1) + 1
            with act.Fori(SH, nt) as t:
                e1 = act.value_load(tab[0:1, bass.ds(t - SH, 1)], min_val=0, max_val=E)
                e = act.value_load(tab[0:1, bass.ds(t - SH + 1, 1)], min_val=1, max_val=E)

                def split_next(n):
                    with act.If(e != e1):
                        with act.If(e < E):
                            for m in ((0, 1), (2,))[n]:
                                split_dyn(e + 1, m)

                def split_dyn(k, m):
                    act.wait_ge(s[f"w{m}_in"], 16 * k + 16)
                    act.activation(w_hi[:, bass.ds(k % 2, 1), m * WCOLS:(m + 1) * WCOLS].rearrange("p a n -> p (a n)"),
                                   raw[m][:, :], ACT.Copy).then_inc(s["wsp_hi"], 1)
                slot(t, split=split_next)
            slot(nt, final=True)

        @block.vector
        def _(dve):
            def stats(name, src, n, g):
                l = lns[name]
                for b in range(GB):
                    last = dve.bn_stats(l["st"][0:n, b, :], src(b))
                last.then_inc(s[name + "_st"], 1)
                dve.wait_ge(s[name + "_st"], g + 1)
                dve.memset(tick[:, :], 0.0)
                for b in range(GB):
                    last = dve.bn_aggr(l["mv"][0:n, b, :], l["st"][0:n, b, :])
                last.then_inc(s[name + "_mv"], 1)

            def recip(name, n, g, with_mean=True):
                l = lns[name]
                dve.wait_ge(s[name + "_sd"], g + 1)
                dve.reciprocal(l["r"][0:n, :], l["sd"][0:n, :]).then_inc(s[name + "_r"], 1)
                if with_mean:
                    dve.wait_ge(s[name + "_r"], g + 1)
                    dve.scalar_tensor_tensor(out=l["nmr"][0:n, :], in0=l["mv"][0:n, :, 0], scalar=-1.0,
                                             in1=l["r"][0:n, :], op0=ALU.mult, op1=ALU.mult).then_inc(s[name + "_nmr"], 1)

            def regroup(c):
                dve.wait_ge(s["img_in"], 16 * HP)
                dve.tensor_copy(img_p[:, c, :].rearrange("q (wp r v) -> q wp r v", r=PATCH, v=PATCH),
                                img[:, c, :].rearrange("q (r wp v) -> q wp r v", r=PATCH, v=PATCH)).then_inc(s["imgp_dve"], 1)

            def x1():
                for j in range(1, 2 * KX, 2):
                    dve.wait_ge(s["xtr"], j + 1)
                    bank = (pS[:, j % 8, :] if j % 8 < 4 else (pT if j % 8 < 6 else pV)[:, j % 2, :])
                    dve.tensor_copy(pt[:, j // 2, XH:2 * XH], bank[:, 0:XH]).then_inc(s["pt_dve"], 1)
                dve.wait_ge(s["tokmm"], 1)
                for hf in range(2):
                    dst = tokT_all[:, 1, :, 1:NC].rearrange("p b (hp wp) -> p wp hp b", wp=HP)
                    last = dve.tensor_scalar(dst[:, hf * HP // 2:(hf + 1) * HP // 2],
                                             pV[:, hf, 0:XH].rearrange("p (wp hp b) -> p wp hp b", hp=HP, b=B),
                                             vec[:, 1:2], None, ALU.add)
                last.then_inc(s["emb_dve"], 1)

            def x3(g):
                dve.wait_ge(s["tok_t"], g + 1)
                dve.tensor_tensor(tok[:, :, :], pT[0:NC, :, :].rearrange("t a (b d) -> t (a b) d", d=D),
                                  row_bias[:, :].unsqueeze(1).to_broadcast([NC, GB, D]), ALU.add).then_inc(s["tok_ok"], 1)

            def x4a(g):
                dve.wait_ge(s["tok_ok"], g + 1)
                stats("lt", lambda b: tok[:, b, :], NC, g)

            def x4b(g):
                recip("lt", NC, g, with_mean=False)
                l = lns["lt"]
                dve.wait_ge(s["lt_r"], g + 1)
                for b in range(GB):
                    last = dve.scalar_tensor_tensor(out=tok[:, b, :], in0=tok[:, b, :], scalar=l["mv"][0:NC, b, 0:1],
                                                    in1=gam_b[:, :], op0=ALU.subtract, op1=ALU.mult)
                last.then_inc(s["ht_c"], 1)
                dve.wait_ge(s["ht_c"], g + 1)
                for b in range(GB):
                    last = dve.scalar_tensor_tensor(
                        out=h[0:NC, bass.ds(g * GB + b, 1), :].rearrange("t b d -> t (b d)"), in0=tok[:, b, :],
                        scalar=l["r"][0:NC, b:b + 1], in1=bet_b[:, :], op0=ALU.mult, op1=ALU.add)
                last.then_inc(s["ht_ok"], 1)

            def x5a(g):
                dve.wait_ge(s["ht_ok"], g + 1)
                dve.memset(tick[:, :], 0.0)
                stats("lx", lambda b: h[:, bass.ds(g * GB + b, 1), :].rearrange("t b d -> t (b d)"), S, g)

            def x5b(g):
                recip("lx", S, g)

            def x6(g):
                dve.wait_ge(s["xn_t"], 2 * g + 2)
                dve.wait_ge(s["g_mm"], 2 * g)
                dve.tensor_copy(xnT[:, 1, :], pT[:, 1, 0:GS]).then_inc(s["xnT_dve"], 1)

            def x7(g):
                dve.wait_ge(s["sc"], GB * g)
                for m in range(KD):
                    dve.wait_ge(s["q_mm"], 2 * g + m + 1)
                    for o, which in enumerate(("even", "odd")):
                        last = dve.tensor_scalar(qq[:, m, :, o, :], pS[:, 2 + m, 0:GS].rearrange("p (b t) -> p b t", b=GB),
                                                 vec[:, KD + m:KD + m + 1], cst(which), ALU.add, ALU.mult)
                last.then_inc(s["q_ok"], 1)
                dve.wait_ge(s["v_mm"], g + 1)
                dve.wait_ge(s["pv"], GB * g)
                dve.tensor_tensor(vv[:, :, :], pT[0:S, :, :].rearrange("t a (b d) -> t (a b) d", d=D),
                                  bv_b[:, :].unsqueeze(1).to_broadcast([S, GB, D]), ALU.add).then_inc(s["v_ok"], 1)

            def y1(g, b):
                dve.wait_ge(s["sc"], GB * g + b + 1)
                if b >= 2:
                    dve.wait_ge(s["pv"], GB * g + b - 1)
                dve.tensor_tensor(pr[:, b % 2, :, :].rearrange("t (r m) s -> t r m s", r=4),
                                  pS[0:S, :, 0:4 * S].rearrange("t r (m s) -> t r m s", m=4),
                                  cst("decay", S).unsqueeze(1).unsqueeze(1).to_broadcast([S, 4, 4, S]), ALU.mult)\
                    .then_inc(s["p_ok"], 1)

            def y2(g):
                dve.wait_ge(s["pv"], GB * g + GB)
                stats("lr", lambda b: pV[0:S, b // 2, (b % 2) * D:(b % 2 + 1) * D], S, g)
                recip("lr", S, g)

            def y3(g):
                dve.wait_ge(s["z_ok"], g + 1)
                dve.tensor_tensor(uT[:, :, :], uT[:, :, :], gate[:, :, :], ALU.mult).then_inc(s["u_ok"], 1)

            def y4(g):
                dve.wait_ge(s["o_mm"], g + 1)
                dve.wait_ge(s["hb_ok"], g + 1)
                dve.tensor_tensor(h2[:, :, :], pS[0:S, 0:2, :].rearrange("t a (b d) -> t (a b) d", d=D), h2[:, :, :],
                                  ALU.add).then_inc(s["h2_ok"], 1)

            def y5(g):
                dve.wait_ge(s["h2_ok"], g + 1)
                stats("l2", lambda b: h2[:, b, :], S, g)
                recip("l2", S, g)

            def y6(g):
                dve.wait_ge(s["x2_t"], 2 * g + 2)
                dve.tensor_copy(x2T[:, 1, :], pT[:, 1, 0:GS]).then_inc(s["x2T_dve"], 1)
                dve.wait_ge(s["lg_mm"], g + 1)
                dve.tensor_copy(lg[:, bass.ds(g * GB, GB), :], pS[0:S, 3, 0:GB * E].rearrange("t (b e) -> t b e", e=E))\
                    .then_inc(s["lg_ok"], 1)

            dve.wait_ge(s["vec_t"], 1)
            dve.tensor_copy(vec[:, :], pV[:, 0, 0:6 * KD]).then_inc(s["vec_ok"], 1)
            dve.wait_ge(s["vec_ok"], 1)
            dve.wait_ge(s["rest_in"], 112)
            dve.tensor_tensor(row_bias[0:1, :], row_bias[0:1, :], tok[0:1, 0, :], ALU.add).then_inc(s["cls_ok"], 1)
            regroup(0)
            regroup(2)
            x1()
            dve.wait_ge(s["cls_ok"], 1)
            x3(0)
            x4a(0)
            x4b(0)
            dve.wait_ge(s["txt_in"], 16)
            x5a(0)
            x5b(0)
            x6(0)
            x7(0)

            def step(i):
                x3(i + 1)
                y1(i, 0)
                x4a(i + 1)
                y1(i, 1)
                x4b(i + 1)
                y1(i, 2)
                x5a(i + 1)
                y1(i, 3)
                x5b(i + 1)
                y2(i)
                x6(i + 1)
                y3(i)
                y4(i)
                x7(i + 1)
                y5(i)
                y6(i)
            step(0)
            with dve.Fori(1, NG - 1) as i:
                step(i)
            for b in range(GB):
                y1(NG - 1, b)
            y2(NG - 1)
            y3(NG - 1)
            y4(NG - 1)
            y5(NG - 1)
            y6(NG - 1)

            n = [0]

            def then(ins):
                n[0] += 1
                ins.then_inc(s["route"], 1)
                dve.wait_ge(s["route"], n[0])

            dve.wait_ge(s["lg_ok"], NG)
            be = [S, B, E]
            then(dve.tensor_reduce(mx[:, :], lg[:, :, :], AX.X, ALU.max))
            then(dve.tensor_tensor(eq[:, :, :], lg[:, :, :], mx[:, :].unsqueeze(2).to_broadcast(be), ALU.is_equal))
            then(dve.scalar_tensor_tensor(out=posm[:, :, :], in0=eq[:, :, :], scalar=-float(E),
                                          in1=cst("expert_late", S).unsqueeze(1).to_broadcast(be),
                                          op0=ALU.mult, op1=ALU.add))
            then(dve.tensor_reduce(idx[:, :], posm[:, :, :], AX.X, ALU.min))
            dve.tensor_tensor(pick[:, :, :], cst("expert", S).unsqueeze(1).to_broadcast(be),
                              idx[:, :].unsqueeze(2).to_broadcast(be), ALU.is_equal).then_inc(s["pick_ok"], 1)
            dve.wait_ge(s["count_mm"], 1)
            then(dve.tensor_copy(tot[:, :, :], pV[0:S, 1, 0:B * E].rearrange("t (b e) -> t e b", e=E)))
            fl = "t e b -> t (e b)"
            then(dve.tensor_tensor_scan(cin[:, :, :].rearrange(fl), cst("ones", S)[:, 0:B * E], tot[:, :, :].rearrange(fl),
                                        0.0, ALU.mult, ALU.add))
            then(dve.tensor_tensor(cex[:, :, :], cin[:, :, :], tot[:, :, :], ALU.subtract))
            then(dve.tensor_tensor(cnt[:, :], cin[:, :, B - 1], cex[:, :, 0], ALU.subtract))
            then(dve.tensor_tensor(over[:, :, :], cnt[:, :].unsqueeze(2).to_broadcast([S, E, NTHR]),
                                   cst("thr", S).unsqueeze(1).to_broadcast([S, E, NTHR]), ALU.is_gt))
            then(dve.tensor_reduce(tiles[:, :], over[:, :, :], AX.X, ALU.add))
            then(dve.tensor_tensor_scan(tin[:, :], cst("ones", S)[:, 0:E], tiles[:, :], 0.0, ALU.mult, ALU.add))
            then(dve.tensor_tensor(tex[:, :], tin[:, :], tiles[:, :], ALU.subtract))
            then(dve.scalar_tensor_tensor(out=delta[:, :], in0=tex[:, :], scalar=float(ROWS), in1=cex[:, :, 0],
                                          op0=ALU.mult, op1=ALU.subtract))
            then(dve.tensor_tensor(pos[:, :, :].rearrange("t b e -> t e b"), cex[:, :, :],
                                   delta[:, :].unsqueeze(2).to_broadcast([S, E, B]), ALU.add))
            then(dve.tensor_tensor(posm[:, :, :], pos[:, :, :], pV[0:S, 0, 0:B * E].rearrange("t (b e) -> t b e", e=E), ALU.add))
            then(dve.tensor_tensor(pos[:, :, :], posm[:, :, :], pick[:, :, :], ALU.mult))
            then(dve.tensor_reduce(row_f[:, :], pos[:, :, :], AX.X, ALU.add))
            dve.tensor_scalar(rows_sb[0:S, :], row_f[:, :], float(SH * ROWS), None, ALU.add).then_inc(s["rows_ok"], 1)
            then(dve.tensor_tensor(ord_c[:, :, :], tex[0:1, :].unsqueeze(1).to_broadcast([1, MAXR, E]),
                                   cst("tile", 1).unsqueeze(2).to_broadcast([1, MAXR, E]), ALU.is_le))
            dve.memset(tab_f[0:1, 0:1], 0.0)
            dve.tensor_reduce(tab_f[0:1, 1:MAXR + 1], ord_c[:, :, :], AX.X, ALU.add)
            then(dve.tensor_scalar(tab_f[0:1, MAXR + 1:MAXR + 2], tin[0:1, E - 1:E], float(SH - 1), None, ALU.add))
            dve.tensor_copy(tab[0:1, :], tab_f[:, :]).then_inc(s["tab_ok"], 1)

            def lower3(k, par):
                dve.wait_ge(s["wsp_hi"], 3 * k + 3)
                w3 = slice(2 * WCOLS, 3 * WCOLS)
                if isinstance(par, int):
                    lo, hi = w_lo[:, par, w3], w_hi[:, par, w3]
                else:
                    lo, hi = (w[:, par, w3].rearrange("p a n -> p (a n)") for w in (w_lo, w_hi))
                dve.tensor_tensor(lo, raw[2][:, :], hi.bitcast(F32), ALU.subtract).then_inc(s["wsp_lo3"], 1)

            def x_lo(t):
                dve.wait_ge(s["xhi"], t + 1)
                dve.tensor_tensor(xT_lo[:, :, :].rearrange("p k n -> p (k n)"), pX,
                                  xT_hi[:, :, :].rearrange("p k n -> p (k n)").bitcast(F32), ALU.subtract).then_inc(s["xlo"], 1)

            def hidden(hf, t):
                dve.wait_ge(s[f"g{hf}"], t + 1)
                dve.wait_ge(s[f"tr{hf}"], t)
                dve.tensor_tensor(hid[:, hf, :], pU[hf][1], gl[:, hf, :], ALU.mult).then_inc(s[f"hid{hf}"], 1)

            def hidden_lo(hf, t):
                dve.wait_ge(s[f"hi{hf}"], t + 1)
                f = "p c n -> p (c n)"
                dve.tensor_tensor(hT_lo[:, hf, :, :].rearrange(f), pH[hf], hT_hi[:, hf, :, :].rearrange(f).bitcast(F32),
                                  ALU.subtract).then_inc(s[f"lo{hf}"], 1)

            def slot(t, split=None, first=False, final=False):
                if not final:
                    hidden(0, t)
                if not first:
                    hidden_lo(1, t - 1)
                if not final:
                    hidden(1, t)
                    x_lo(t + 1)
                    hidden_lo(0, t)
                if split:
                    split()

            lower3(0, 0)
            x_lo(0)
            slot(0, split=lambda: lower3(1, 1), first=True)
            slot(1)
            with dve.Fori(2, SH) as t:
                slot(t)
            dve.wait_ge(s["tab_ok"], 1)
            nt = dve.value_load(tab[0:1, MAXR + 1:MAXR + 2], min_val=SH + E - 1, max_val=SH + MAXR - 1) + 1
            with dve.Fori(SH, nt) as t:
                e1 = dve.value_load(tab[0:1, bass.ds(t - SH, 1)], min_val=0, max_val=E)
                e = dve.value_load(tab[0:1, bass.ds(t - SH + 1, 1)], min_val=1, max_val=E)

                def split_next():
                    with dve.If(e != e1):
                        with dve.If(e < E):
                            lower3(e + 1, bass.ds((e + 1) % 2, 1))
                slot(t, split=split_next)
            slot(nt, final=True)
            dve.wait_ge(s["h_in"], 32)
            dve.wait_ge(s["ysh_in"], 32)
            for c in range(SH):
                n_r = min(ROWS, T - c * ROWS)
                dve.tensor_tensor(ysh[0:n_r, c, :], ysh[0:n_r, c, :], h_fl[0:n_r, c, :], ALU.add).then_inc(s["sum1"], 1)
            dve.wait_ge(s["gathered"], 16 * SH)
            for c in range(SH):
                n_r = min(ROWS, T - c * ROWS)
                dve.wait_ge(s["sum1"], c + 1)
                dve.tensor_tensor(h_fl[0:n_r, c, :], ysh[0:n_r, c, :], yg[0:n_r, c, :], ALU.add).then_inc(s["sum2"], 1)


INS = {"x": "x", "txt": "txt", "tok_W": "L0_tok_W", "tok_b": "L0_tok_b", "cls": "L0_tok_cls_token",
       "pos": "L0_tok_pos_embedding", "tg": "L0_tok_gamma", "tb": "L0_tok_beta", "Wq": "L0_attn_Wq", "bq": "L0_attn_bq",
       "Wk": "L0_attn_Wk", "bk": "L0_attn_bk", "Wv": "L0_attn_Wv", "bv": "L0_attn_bv", "Wg": "L0_attn_Wg",
       "bg": "L0_attn_bg", "Wo": "L0_attn_Wo", "bo": "L0_attn_bo", "ga": "L0_attn_gamma", "ba": "L0_attn_beta",
       "w1s": "L0_ffn_w1s", "w2s": "L0_ffn_w2s", "w3s": "L0_ffn_w3s", "W1": "L0_ffn_W1", "W2": "L0_ffn_W2",
       "W3": "L0_ffn_W3", "Wr": "L0_ffn_Wg"}


def kernel(**inputs):
    import concourse.bacc as bacc
    from concourse.bass_utils import run_bass_kernel_spmd

    nc = bacc.Bacc("TRN2", target_bir_lowering=False, num_devices=1)
    arrays = {n: np.ascontiguousarray(inputs[full]) for n, full in INS.items()}
    B, C, H, _ = arrays["x"].shape
    z = shapes_of(B, C, H, arrays["txt"].shape[1], arrays["txt"].shape[2], arrays["w1s"].shape[1])
    arrays["const"], cols = constants(z)
    aps = {n: nc.dram_tensor("in_" + n, v.shape, F32, kind="ExternalInput").ap() for n, v in arrays.items()}
    out = nc.dram_tensor("out_h", (B, z["S"], z["D"]), F32, kind="ExternalOutput").ap()
    build(nc, aps, out, z, cols)
    r = run_bass_kernel_spmd(nc, [{"in_" + n: v for n, v in arrays.items()}], core_ids=[0])
    return r.results[0]["out_h"]
```

```python
from contextlib import ExitStack

import concourse.bass as bass
import numpy as np
from concourse import mybir

F32 = mybir.dt.float32
F32R = mybir.dt.float32r
I32 = mybir.dt.int32
ALU = mybir.AluOpType
ACT = mybir.ActivationFunctionType
AX = mybir.AxisListType

P = 128
EPS = 1e-5
DECAY = 0.99
HEADS = 16
DH = 16
PATCH = 16
GB = 4
E_ROUTED = 8
ROWS = 128
RING = 3


def shapes_of(B, C, HW, S_TXT, D, F):
    z = {}
    z["B"], z["C"], z["HW"], z["D"], z["F"] = B, C, HW, D, F
    z["HP"] = HW // PATCH
    z["NP"] = z["HP"] ** 2
    z["NC"] = z["NP"] + 1
    z["S"] = z["NC"] + S_TXT
    z["T"] = B * z["S"]
    z["NG"] = B // GB
    z["SH_TILES"] = -(-z["T"] // ROWS)
    z["MAX_ROUTED"] = (z["T"] - E_ROUTED) // ROWS + E_ROUTED
    return z


def constants(z):
    S = z["S"]
    n_thr = -(-z["T"] // ROWS)
    cols, parts = {}, []

    def put(name, a):
        full = np.zeros((P, a.shape[1]), np.float32)
        full[:a.shape[0]] = a
        at = sum(x.shape[1] for x in parts)
        cols[name] = (at, at + a.shape[1])
        parts.append(full)

    put("ident", np.eye(P, dtype=np.float32))
    t = np.arange(S)
    put("earlier", (t[:, None] < t[None, :]).astype(np.float32))
    put("ones", np.ones((P, P), np.float32))
    diff = (t[None, :] - t[:, None]).astype(np.float32)
    decay = np.power(np.float32(DECAY), np.maximum(diff, 0), dtype=np.float32)
    put("decay", np.where(diff >= 0, decay / np.float32(DH ** 0.5), 0).astype(np.float32))
    e = np.arange(E_ROUTED, dtype=np.float32)[None, :]
    put("expert", np.repeat(e, P, 0))
    put("expert_late", np.repeat(e + E_ROUTED, P, 0))
    thr = np.arange(n_thr, dtype=np.float32)[None, :] * ROWS
    thr[0, 0] = -1
    put("thr", np.repeat(thr, P, 0))
    put("tile", np.repeat(np.arange(z["MAX_ROUTED"], dtype=np.float32)[None, :], P, 0))
    head = np.arange(P) // DH
    put("even", (head % 2 == 0).astype(np.float32)[:, None])
    put("odd", (head % 2 == 1).astype(np.float32)[:, None])
    return np.concatenate(parts, 1), cols


def build(nc, a, out, z, cols):
    B, C, D, F, S, NC, NP, HP, HW, T = (z[k] for k in ("B", "C", "D", "F", "S", "NC", "NP", "HP", "HW", "T"))
    NG, SH, MAXR = z["NG"], z["SH_TILES"], z["MAX_ROUTED"]
    KD = D // P
    KX = C * PATCH * PATCH // P
    GS = GB * S
    QR = HP * B
    XH = HP // 2 * QR
    ZP = 84
    HALF = F // 2
    FC = HALF // P
    WCOLS = KD * F
    E = E_ROUTED
    NTHR = cols["thr"][1] - cols["thr"][0]
    X_ROWS = (SH + MAXR + 2) * ROWS

    xs = nc.dram_tensor("xs", (X_ROWS, D), F32, kind="Internal").ap()
    ys = nc.dram_tensor("ys", ((SH + MAXR) * ROWS, D), F32, kind="Internal").ap()
    hs = nc.dram_tensor("hs", (SH * ROWS, D), F32, kind="Internal").ap()
    row_d = nc.dram_tensor("row_d", (SH * ROWS, 1), I32, kind="Internal").ap()

    with ExitStack() as ctx:
        base = -(-nc.sbuf_base // 64) * 64
        part = 3 * WCOLS * 4
        slots = [[base + 2 * k * part, base + 2 * (k + 1) * part] for k in range(RING)]
        kept = [slots[-1][1], nc.sbuf_usable_end]

        def sb(name, shape, dt=F32, at=kept):
            size = -(-int(np.prod(shape[1:])) * 4 // 64) * 64
            assert at[0] + size <= at[1], f"no room for {name}: {at}"
            at[0] += size
            return nc.alloc_sbuf_tensor_at(name, shape, dt, offset=at[0] - size)

        def ps(name, shape):
            return ctx.enter_context(nc.psum_tensor(name, shape, F32))

        def sem(name):
            return ctx.enter_context(nc.semaphore(name))

        const = sb("const", [P, max(c[1] for c in cols.values())])
        w_parts = sb("w_parts", [P, RING, 2, 3 * WCOLS], F32R, at=[slots[0][0], slots[-1][1]])
        w_hi, w_lo = w_parts[:, :, 0, :], w_parts[:, :, 1, :]
        raw = [sb(f"raw{m}", [P, WCOLS]) for m in range(3)]
        rows_sb = sb("rows_sb", [P, B], I32)
        tab = sb("tab", [P, MAXR + 2], I32)
        h = sb("h", [S, B, D], at=slots[2])

        def cst(name, n=P):
            lo, hi = cols[name]
            return const[0:n, lo:hi]

        rest = list(kept)
        early = [list(rest), slots[1], slots[0]]

        def front_sb(name, shape, dt=F32):
            size = -(-int(np.prod(shape[1:])) * 4 // 64) * 64
            at = next(x for x in early if x[0] + size <= x[1])
            return sb(name, shape, dt, at=at)

        def late_sb(name, shape, dt=F32):
            return sb(name, shape, dt, at=slots[2])

        eps = late_sb("eps", [P, 1])
        tick = late_sb("tick", [1, 5])
        img = sb("img", [QR, C, PATCH * HW], at=slots[0])
        img_p = sb("img_p", [QR, C, PATCH * HW], at=slots[0])
        pt = front_sb("pt", [P, KX, B * NP])
        w_tok = front_sb("w_tok", [P, KX, D])
        zero = front_sb("zero", [ZP, D])
        w_q, w_k, w_v, w_g, w_o = (front_sb(n, [P, KD, D]) for n in ("w_q", "w_k", "w_v", "w_g", "w_o"))
        w_r = late_sb("w_r", [P, KD, E])
        vec_rows = front_sb("vec_rows", [6 * KD, P])
        vec = late_sb("vec", [P, 6 * KD])
        row_bias = front_sb("row_bias", [NC, D])
        gam_b = front_sb("gam_b", [NC, D])
        bet_b = front_sb("bet_b", [NC, D])
        bv_b = front_sb("bv_b", [S, D])
        bo_b = late_sb("bo_b", [S, D])
        tokT_all = front_sb("tokT_all", [P, KD, B, NC])
        tokT = front_sb("tokT", [P, KD, GB, S])
        tok = front_sb("tok", [NC, GB, D])
        xn = front_sb("xn", [S, GB, D])
        xnT = front_sb("xnT", [P, KD, GS])
        qq = front_sb("qq", [P, KD, GB, 2, S])
        kT = front_sb("kT", [P, KD, GS])
        vv = front_sb("vv", [S, GB, D])
        gate = front_sb("gate", [P, KD, GS])
        pr = front_sb("pr", [S, 2, HEADS, S])
        r_even = front_sb("r_even", [P, 2, KD, S])
        rT = front_sb("rT", [P, KD, GS])
        sqT = front_sb("sqT", [P, KD, GS])
        sdT = front_sb("sdT", [P, GS])
        uT = front_sb("uT", [P, KD, GS])
        h2 = late_sb("h2", [S, GB, D])
        xn2 = late_sb("xn2", [S, GB, D])
        x2T = late_sb("x2T", [P, KD, GS])
        lg = late_sb("lg", [S, B, E])
        lns = {n: {k: late_sb(f"{n}_{k}s", [S, GB] + w) for k, w in
                   (("st", [6]), ("mv", [2]), ("sd", []), ("r", []), ("nmr", []), ("tick", []))} for n in ("lt", "lx", "l2")}
        befo = late_sb("befo", [S, B, E])
        mx = late_sb("mx", [S, B])
        eq = late_sb("eq", [S, B, E])
        idx = late_sb("idx", [S, B])
        pick = late_sb("pick", [S, B, E])
        tot = late_sb("tot", [S, E, B])
        cin = late_sb("cin", [S, E, B])
        cex = late_sb("cex", [S, E, B])
        cnt = late_sb("cnt", [S, E])
        over = late_sb("over", [S, E, NTHR])
        tiles = late_sb("tiles", [S, E])
        tin = late_sb("tin", [S, E])
        tex = late_sb("tex", [S, E])
        delta = late_sb("delta", [S, E])
        pos = late_sb("pos", [S, B, E])
        posm = late_sb("posm", [S, B, E])
        row_f = late_sb("row_f", [S, B])
        ord_c = late_sb("ord_c", [1, MAXR, E])
        tab_f = late_sb("tab_f", [1, MAXR + 2])

        rear = list(rest)
        xr = sb("xr", [ROWS, D], at=rear)
        xT_hi = sb("xT_hi", [P, KD, ROWS], F32R, at=rear)
        xT_lo = sb("xT_lo", [P, KD, ROWS], F32R, at=rear)
        gl = sb("gl", [ROWS, 2, HALF], at=rear)
        hid = sb("hid", [ROWS, 2, HALF], at=rear)
        hT_hi = sb("hT_hi", [P, 2, FC, ROWS], F32R, at=rear)
        hT_lo = sb("hT_lo", [P, 2, FC, ROWS], F32R, at=rear)
        y_sb = sb("y_sb", [ROWS, D], at=rear)
        row_t = sb("row_t", [ROWS, SH], I32, at=rear)
        h_fl = sb("h_fl", [ROWS, SH, D], at=rear)
        tail = [base, base + 2 * part]
        ysh = sb("ysh", [ROWS, SH, D], at=tail)
        yg = sb("yg", [ROWS, SH, D], at=tail)

        pS = ps("pS", [P, 4, 512])
        pT = ps("pT", [P, 2, 512])
        pV = ps("pV", [P, 2, 512])
        pU = [(pS[:, 0, :], pS[:, 1, :]), (pS[:, 2, :], pS[:, 3, :])]
        pH = [pT[:, 0, :], pT[:, 1, :]]
        pY, pX = pV[:, 0, 0:D], pV[:, 1, 0:KD * ROWS]
        pX0 = pS[:, 2, 0:KD * ROWS]
        pC = pT[0:S, 1, :]

        names = """zero_y last_st cls_ok emb0_act emb0_dve const_in attn_in vecs_in txt_in img_in rest_in w0_in w1_in w2_in eps_set col_set zero_set zero_out
            vec_t vec_ok xtr pt_act pt_dve tokmm tokT_ok imgp_act imgp_dve emb_act emb_dve tok_t tok_ok tn_ok ht_c ht_ok xn_ok xn_t xnT_act xnT_dve
            q_mm k_mm v_mm g_mm q_ok k_ok v_ok g_ok sc p_ok pv re_ok rt_ok mean_mm cen_ok sq_ok var_mm sdT_ok rinv_ok zn_ok z_ok u_ok o_mm hb_ok h2_ok xn2_ok
            h2_st xn2_st xn2_cp x2_t x2T_ok lg_mm lg_ok pick_ok count_mm route rows_ok tab_ok row_st
            scattered wsp_hi wsp_hi3 wsp_lo12 wsp_lo3 xr_in xt xhi xlo u0 u1 g0 g1 hid0 hid1 tr0 tr1 hi0 hi1 lo0 lo1 count_ok
            y_mm y_ev y_st row_in h_in ysh_in gathered sum1 sum2 out_st""".split()
        s = {n: sem(n) for n in names}
        for n in lns:
            for k in ("st", "mv", "sd", "r", "nmr"):
                s[f"{n}_{k}"] = sem(f"{n}_{k}")

        x_in = a["x"]
        tokens = xs[0:T, :].rearrange("(b t) d -> t b d", t=S)

        block = ctx.enter_context(nc.Block())

        @block.sync
        def _(sp):
            sp.dma_start(const[:, :], a["const"]).then_inc(s["const_in"], 16)
            for r in range(HP):
                sp.dma_start(img[r * B:(r + 1) * B, :, :],
                             x_in[:, :, r * PATCH:(r + 1) * PATCH, :].rearrange("b c r w -> b c (r w)")).then_inc(s["img_in"], 16)
            for n, v in enumerate(("tok_b", "bq", "bk", "bg", "ga", "ba")):
                sp.dma_start(vec_rows[n * KD:(n + 1) * KD, :],
                             a[v].rearrange("(m p) -> m p", p=P)).then_inc(s["vecs_in"], 16)
            sp.dma_start(w_tok[:, :, :], a["tok_W"].rearrange("(k p) n -> p k n", p=P)).then_inc(s["rest_in"], 16)
            sp.dma_start(row_bias[:, :], a["pos"][0]).then_inc(s["rest_in"], 16)
            sp.dma_start(tok[0:1, 0, :], a["cls"][0]).then_inc(s["rest_in"], 16)
            sp.dma_start(gam_b[:, :], a["tg"].partition_broadcast(NC)).then_inc(s["rest_in"], 16)
            sp.dma_start(bet_b[:, :], a["tb"].partition_broadcast(NC)).then_inc(s["rest_in"], 16)
            sp.dma_start(bv_b[:, :], a["bv"].partition_broadcast(S)).then_inc(s["rest_in"], 16)
            sp.dma_start(bo_b[:, :], a["bo"].partition_broadcast(S)).then_inc(s["rest_in"], 16)
            sp.dma_start(h[NC:S, :, :], a["txt"].rearrange("b t d -> t b d")).then_inc(s["txt_in"], 16)
            for w, v in ((w_q, "Wq"), (w_k, "Wk"), (w_v, "Wv"), (w_g, "Wg"), (w_o, "Wo"), (w_r, "Wr")):
                sp.dma_start(w[:, :, :], a[v].rearrange("(k p) n -> p k n", p=P)).then_inc(s["attn_in"], 16)
            for m, v in enumerate(("w1s", "w2s", "w3s")):
                sp.dma_start(raw[m][:, :].rearrange("p (k n) -> p k n", k=a[v].shape[0] // P),
                             a[v].rearrange("(k p) n -> p k n", p=P)).then_inc(s[f"w{m}_in"], 16)

            def load_expert(k):
                for m, v in enumerate(("W1", "W2", "W3")):
                    if m < 2:
                        sp.wait_ge(s["wsp_lo12"], 2 * k - 1 + m)
                    else:
                        sp.wait_ge(s["wsp_lo3"], k)
                    n = a[v].shape[2]
                    sp.dma_start(raw[m][:, :].rearrange("p (k n) -> p k n", n=n),
                                 a[v][bass.ds(k - 1, 1)].rearrange("e (k p) n -> p (e k) n", p=P))\
                        .then_inc(s[f"w{m}_in"], 16)
            with sp.Fori(1, RING + 2) as k:
                load_expert(k)
            sp.wait_ge(s["h2_st"], 16 * NG)
            full = SH - 1
            last = T - full * ROWS
            sp.dma_start(h_fl[:, 0:full, :], hs[0:full * ROWS, :].rearrange("(c p) d -> p c d", p=ROWS)).then_inc(s["h_in"], 16)
            sp.dma_start(h_fl[0:last, full, :], hs[full * ROWS:T, :]).then_inc(s["h_in"], 16)
            with sp.Fori(RING + 2, E + 1) as k:
                load_expert(k)
            sp.wait_ge(s["last_st"], 16)
            sp.dma_start(ysh[:, 0:full, :], ys[0:full * ROWS, :].rearrange("(c p) d -> p c d", p=ROWS)).then_inc(s["ysh_in"], 16)
            sp.dma_start(ysh[0:last, full, :], ys[full * ROWS:T, :]).then_inc(s["ysh_in"], 16)
            flat = out.rearrange("b t d -> (b t) d")
            for c in range(SH):
                n = min(ROWS, T - c * ROWS)
                sp.wait_ge(s["sum2"], c + 1)
                sp.dma_start(flat[c * ROWS:c * ROWS + n, :], h_fl[0:n, c, :]).then_inc(s["out_st"], 16)
            sp.wait_ge(s["out_st"], 16 * SH)

        @block.gpsimd
        def _(pool):
            pool.memset(zero[:, :], 0.0).then_inc(s["zero_set"], 1)
            pool.memset(eps[:, :], EPS).then_inc(s["eps_set"], 1)
            pool.memset(tokT_all[:, :, :, 0:1], 0.0)
            pool.memset(tokT[:, :, :, :], 0.0).then_inc(s["col_set"], 1)
            pool.wait_ge(s["rest_in"], 112)
            pool.wait_ge(s["txt_in"], 16)
            pool.wait_ge(s["zero_set"], 1)
            n = (X_ROWS - T) // ZP
            assert (X_ROWS - T) % ZP == 0
            pool.dma_start(xs[T:X_ROWS, :].rearrange("(c p) d -> p c d", p=ZP),
                           zero[:, :].unsqueeze(1).to_broadcast([ZP, n, D])).then_inc(s["zero_out"], 16)
            n = MAXR - E
            pool.dma_start(ys[(SH + E) * ROWS:, :].rearrange("(p c) d -> p c d", c=2 * n),
                           zero[0:ROWS // 2, :].unsqueeze(1).to_broadcast([ROWS // 2, 2 * n, D])).then_inc(s["zero_y"], 16)

            def residual_bias(g):
                pool.wait_ge(s["ht_ok"], g + 1)
                pool.wait_ge(s["h2_st"], 16 * g)
                pool.wait_ge(s["xn2_ok"], g)
                pool.tensor_tensor(h2[:, :, :], h[:, bass.ds(g * GB, GB), :],
                                   bo_b[:, :].unsqueeze(1).to_broadcast([S, GB, D]), ALU.add).then_inc(s["hb_ok"], 1)

            def lower(k, m, slot):
                pool.wait_ge(s["wsp_hi"], 2 * k + m + 1)
                w = slice(m * WCOLS, (m + 1) * WCOLS)
                lo, hi = w_lo[:, slot, w], w_hi[:, slot, w]
                if not isinstance(k, int):
                    lo, hi = (x.rearrange("p a n -> p (a n)") for x in (lo, hi))
                pool.tensor_tensor(lo, raw[m][:, :], hi.bitcast(F32), ALU.subtract).then_inc(s["wsp_lo12"], 1)

            def x4(g):
                pool.wait_ge(s["ht_c"], g + 1)
                pool.tensor_tensor(h[0:NC, bass.ds(g * GB, GB), :], tok[:, :, :],
                                   bet_b[:, :].unsqueeze(1).to_broadcast([NC, GB, D]), ALU.add).then_inc(s["ht_ok"], 1)

            x4(0)
            lower(0, 0, 0)
            lower(0, 1, 0)
            x4(1)
            residual_bias(0)
            with pool.Fori(1, NG - 1) as i:
                x4(i + 1)
                residual_bias(i)
            residual_bias(NG - 1)
            pool.wait_ge(s["rows_ok"], 1)
            pool.wait_ge(s["xn2_cp"], 16 * NG)
            pool.wait_ge(s["zero_out"], 16)
            for b in range(B):
                pool.indirect_dma_start(out=xs, out_offset=bass.IndirectOffsetOnAxis(ap=rows_sb[0:S, b:b + 1], axis=0),
                                        in_=h[0:S, b, :], in_offset=None).then_inc(s["scattered"], 16)
            pool.dma_start(row_d[0:T, :].rearrange("(b t) o -> t (b o)", t=S), rows_sb[0:S, :],
                           allow_slow_non_contiguous=True).then_inc(s["row_st"], 16)
            pool.wait_ge(s["row_st"], 16)
            full, rest_rows = T // ROWS, T % ROWS
            pool.dma_start(row_t[:, 0:full], row_d[0:full * ROWS, :].rearrange("(c p) o -> p (c o)", p=ROWS),
                           allow_slow_non_contiguous=True)\
                .then_inc(s["row_in"], 16)
            pool.dma_start(row_t[0:rest_rows, full:full + 1], row_d[full * ROWS:T, :]).then_inc(s["row_in"], 16)
            with pool.Fori(1, E + 1) as k:
                lower(k, 0, bass.ds(k % RING, 1))
                lower(k, 1, bass.ds(k % RING, 1))
            pool.wait_ge(s["row_in"], 32)
            pool.wait_ge(s["last_st"], 16)
            for c in range(SH):
                n = min(ROWS, T - c * ROWS)
                pool.indirect_dma_start(out=yg[0:n, c, :], out_offset=None, in_=ys,
                                        in_offset=bass.IndirectOffsetOnAxis(ap=row_t[0:n, c:c + 1], axis=0))\
                    .then_inc(s["gathered"], 16)

        @block.tensor
        def _(pe):
            ident = cst("ident")

            def mm(o, l, r, start, stop):
                return pe.matmul(o, l, r, start=start, stop=stop)

            banks = [pS[:, r, :] for r in range(4)] + [pT[:, 0, :], pT[:, 1, :], pV[:, 0, :], pV[:, 1, :]]

            def x1():
                for j in range(2 * KX):
                    pe.wait_ge(s["imgp_dve"], 1)
                    if j >= 2 * KX // C:
                        pe.wait_ge(s["imgp_act"], 1)
                    if j >= 4 * KX // C:
                        pe.wait_ge(s["imgp_dve"], 2)
                    if j >= 8:
                        pe.wait_ge(s["pt_act"] if j % 2 == 0 else s["pt_dve"], (j - 8) // 2 + 1)
                    k = j // 2
                    for q in range(HP // 2):
                        wp = j % 2 * (HP // 2) + q
                        at = wp * PATCH * PATCH + (k % 2) * P
                        last = pe.transpose(banks[j % 8][:, q * QR:(q + 1) * QR], img_p[:, k // 2, at:at + P],
                                            ident[0:QR, 0:QR])
                    last.then_inc(s["xtr"], 1)

            def x2(banks, batches, ks):
                b0, b1 = batches
                for k in ks:
                    pe.wait_ge(s["pt_act"], k + 1)
                    pe.wait_ge(s["pt_dve"], k + 1)
                    for m in range(KD):
                        last = mm(banks[:, m, 0:(b1 - b0) * NP], w_tok[:, k, m * P:(m + 1) * P],
                                  pt[:, k, :].rearrange("p (n b) -> p n b", b=B)[:, :, b0:b1], k == 0, k == KX - 1)
                if k == KX - 1:
                    last.then_inc(s["tokmm"], 1)

            def x3(g):
                if isinstance(g, int) and g == 0:
                    pe.wait_ge(s["emb0_act"], 1)
                    pe.wait_ge(s["emb0_dve"], 1)
                else:
                    pe.wait_ge(s["tokT_ok"], g)
                pe.wait_ge(s["v_ok"], g)
                for b in range(GB):
                    for m in range(KD):
                        at = (b % 2) * D + m * P
                        last = pe.transpose(pT[0:S, b // 2, at:at + P], tokT[:, m, b, :], ident)
                last.then_inc(s["tok_t"], 1)

            def transposes(bank, src, name):
                for m in range(KD):
                    for b in range(GB):
                        last = pe.transpose(bank[:, m, b * S:(b + 1) * S], src[:, b, m * P:(m + 1) * P], ident[0:S, 0:S])
                    last.then_inc(s[name], 1)

            def x6(g):
                pe.wait_ge(s["xn_ok"], g + 1)
                if not isinstance(g, int) or g > 1:
                    pe.wait_ge(s["lg_ok"], g - 1)
                transposes(pT, xn, "xn_t")

            def project(g, banks, w, name):
                for m in range(KD):
                    for k in range(KD):
                        last = mm(banks[:, m, 0:GS], w[:, k, m * P:(m + 1) * P], xnT[:, k, :], k == 0, k == KD - 1)
                    last.then_inc(s[name], 1)

            def to_tokens(bank, left, w, name):
                for b in range(GB):
                    for k in range(KD):
                        last = mm(bank[0:S, b // 2, (b % 2) * D:(b % 2 + 1) * D], left[:, k, b * S:(b + 1) * S],
                                  w[:, k, :], k == 0, k == KD - 1)
                last.then_inc(s[name], 1)

            def x7_qk(g):
                pe.wait_ge(s["xnT_act"], g + 1)
                pe.wait_ge(s["xnT_dve"], g + 1)
                pe.wait_ge(s["p_ok"], 2 * GB * g)
                project(g, pS[:, 2:4, :], w_q, "q_mm")
                project(g, pS[:, 0:2, :], w_k, "k_mm")

            def x7_vg(g):
                to_tokens(pT, xnT, w_v, "v_mm")
                pe.wait_ge(s["q_ok"], g + 1)
                project(g, pS[:, 2:4, :], w_g, "g_mm")

            def scores(g, b):
                for half in range(2):
                    if b == 0:
                        pe.wait_ge(s["q_ok"], g + 1)
                        pe.wait_ge(s["k_ok"], g + 1)
                        pe.wait_ge(s["g_ok"], g + 1)
                    else:
                        pe.wait_ge(s["p_ok"], 2 * (GB * g + b) - 1 + half)
                    for m in range(KD):
                        for r in (2 * half, 2 * half + 1):
                            q = slice(32 * r, 32 * r + 32)
                            last = mm(pS[0:S, r, m * 2 * S:(m + 1) * 2 * S], kT[q, m, b * S:(b + 1) * S],
                                      qq[q, m, b, :, :], True, True)
                    last.then_inc(s["sc"], 1)

            def retain(g, b):
                if b == 0:
                    pe.wait_ge(s["v_ok"], g + 1)
                    pe.wait_ge(s["h2_ok"], g)
                if b >= 2:
                    pe.wait_ge(s["rt_ok"], GB * g + b - 1)
                for half in range(2):
                    pe.wait_ge(s["p_ok"], 2 * (GB * g + b) + 1 + half)
                    for m in range(KD):
                        for r in (2 * half, 2 * half + 1):
                            last = mm(pV[32 * r:32 * r + 32, b % 2, m * 2 * S:(m + 1) * 2 * S],
                                      vv[:, b, m * P + 32 * r:m * P + 32 * r + 32],
                                      pr[:, b % 2, r * 4 + m * 2:r * 4 + m * 2 + 2, :], True, True)
                last.then_inc(s["pv"], 1)

            def y1(g, between):
                for b in range(GB + 1):
                    if b < GB:
                        scores(g, b)
                    if b:
                        retain(g, b - 1)
                    if b in between:
                        between[b]()

            def column_sums(bank, src, name):
                for m in range(KD):
                    last = mm(bank[:, 0:GS], cst("ones"), src[:, m, :], m == 0, m == KD - 1)
                last.then_inc(s[name], 1)

            def y2_mean(g):
                pe.wait_ge(s["rt_ok"], GB * g + GB)
                column_sums(pV[:, 0, :], rT, "mean_mm")

            def y2_var(g):
                pe.wait_ge(s["sq_ok"], g + 1)
                column_sums(pV[:, 1, :], sqT, "var_mm")

            def y4(g):
                pe.wait_ge(s["u_ok"], g + 1)
                to_tokens(pV, uT, w_o, "o_mm")

            def y6_transpose(g, last=False):
                pe.wait_ge(s["xn2_ok"], g + 1)
                pe.wait_ge(s["v_ok"], min(g + 2, NG) if isinstance(g, int) else g + 2)
                if last:
                    pe.wait_ge(s["lg_ok"], g)
                elif isinstance(g, int) and g == NG - 2:
                    pass
                else:
                    pe.wait_ge(s["tok_ok"], g + 3)
                transposes(pT, xn2, "x2_t")

            def y6_logits(g):
                pe.wait_ge(s["x2T_ok"], g + 1)
                for b in range(GB):
                    for k in range(KD):
                        last = mm(pT[0:S, 0, b * E:(b + 1) * E], x2T[:, k, b * S:(b + 1) * S], w_r[:, k, :],
                                  k == 0, k == KD - 1)
                last.then_inc(s["lg_mm"], 1)

            def x_transpose(t, bank):
                pe.wait_ge(s["xr_in"], 16 * t + 16)
                for m in range(KD):
                    last = pe.transpose(bank[:, m * ROWS:(m + 1) * ROWS], xr[:, m * P:(m + 1) * P], ident)
                last.then_inc(s["xt"], 1)

            def weights_ready(k):
                pe.wait_ge(s["wsp_hi"], 2 * k + 2)
                pe.wait_ge(s["wsp_lo12"], 2 * k + 2)

            def x_ready(t):
                pe.wait_ge(s["xhi"], t + 1)
                pe.wait_ge(s["xlo"], t + 1)

            def up(hf, slot, name):
                for k in range(KD):
                    xh, xl = xT_hi[:, k, :], xT_lo[:, k, :]
                    for part, st, w in ((xh, True, w_hi), (xh, False, w_lo), (xl, False, w_hi)):
                        for j in range(2):
                            at = j * WCOLS + k * F + hf * HALF
                            last = mm(pU[hf][j], part, w[:, slot, at:at + HALF],
                                      k == 0 and st, k == KD - 1 and part is xl)
                last.then_inc(s[name], 1)

            pe.wait_ge(s["const_in"], 16)
            pe.wait_ge(s["vecs_in"], 96)
            pe.transpose(pV[:, 0, 0:6 * KD], vec_rows[:, :], ident[0:6 * KD, 0:6 * KD]).then_inc(s["vec_t"], 1)
            pe.wait_ge(s["vec_ok"], 1)
            x1()
            pe.wait_ge(s["rest_in"], 112)
            pe.wait_ge(s["pt_act"], 4)
            pe.wait_ge(s["pt_dve"], 4)
            x2(pV, (0, GB), range(KX))
            x2(pS, (GB, B), range(KX // 3))
            x3(0)
            x2(pS, (GB, B), range(KX // 3, KX))
            x6(0)
            pe.wait_ge(s["attn_in"], 96)
            pe.wait_ge(s["emb_act"], 1)
            pe.wait_ge(s["emb_dve"], 1)
            x7_qk(0)
            x7_vg(0)

            def step(i, first=False):
                if first:
                    y1(i, {0: lambda: x3(i + 1)})
                else:
                    y1(i, {0: lambda: x3(i + 1), 3: lambda: y6_transpose(i - 1), 4: lambda: y6_logits(i - 1)})
                x6(i + 1)
                y2_mean(i)
                x7_qk(i + 1)
                y2_var(i)
                x7_vg(i + 1)
                y4(i)
            step(0, first=True)
            with pe.Fori(1, NG - 1) as i:
                step(i)
            y1(NG - 1, {3: lambda: y6_transpose(NG - 2), 4: lambda: y6_logits(NG - 2)})
            y2_mean(NG - 1)
            x_transpose(0, pX0)
            y2_var(NG - 1)
            weights_ready(0)
            x_ready(0)
            up(0, 0, "u0")
            up(1, 0, "u1")
            y4(NG - 1)
            pe.wait_ge(s["h2_ok"], NG)
            x_transpose(1, pX)
            y6_transpose(NG - 1, last=True)
            y6_logits(NG - 1)

            def count():
                pe.wait_ge(s["pick_ok"], 1)
                picks = pick[:, :, :].rearrange("t b e -> t (b e)")
                mm(pC[:, 0:B * E], cst("earlier", S), picks, True, True)
                mm(pC[:, B * E:2 * B * E], cst("ones", S)[:, 0:S], picks, True, True).then_inc(s["count_mm"], 1)
                pe.wait_ge(s["count_ok"], 1)

            def hid_transpose(hf, name):
                for c in range(FC):
                    last = pe.transpose(pH[hf][:, c * P:(c + 1) * P], hid[:, hf, c * P:(c + 1) * P], ident)
                last.then_inc(s[name], 1)

            def down(hf, par):
                for c in range(FC):
                    at = 2 * WCOLS + (hf * FC + c) * D
                    for n, (l, w) in enumerate(((hT_hi, w_hi), (hT_hi, w_lo), (hT_lo, w_hi))):
                        last = mm(pY, l[:, hf, c, :], w[:, par, at:at + D], hf == 0 and c == 0 and n == 0,
                                  hf == 1 and c == FC - 1 and n == 2)
                return last

            def slot(t, e, at, e1, at1, counting=False, final=False):
                pe.wait_ge(s["hid0"], t)
                pe.wait_ge(s["lo0"], t - 1)
                hid_transpose(0, "tr0")
                if not final:
                    weights_ready(e)
                    x_ready(t)
                    up(0, at, "u0")
                if counting:
                    count()
                pe.wait_ge(s["hid1"], t)
                pe.wait_ge(s["lo1"], t - 1)
                hid_transpose(1, "tr1")
                pe.wait_ge(s["lo0"], t)
                pe.wait_ge(s["wsp_hi3"], e1 + 1)
                pe.wait_ge(s["wsp_lo3"], e1 + 1)
                pe.wait_ge(s["y_ev"], t - 1)
                down(0, at1)
                if not final:
                    up(1, at, "u1")
                    x_transpose(t + 1, pX)
                pe.wait_ge(s["lo1"], t)
                down(1, at1).then_inc(s["y_mm"], 1)

            pe.wait_ge(s["lg_ok"], NG)
            slot(1, 0, 0, 0, 0, counting=True)
            with pe.Fori(2, SH) as t:
                slot(t, 0, 0, 0, 0)
            pe.wait_ge(s["tab_ok"], 1)
            nt = pe.value_load(tab[0:1, MAXR + 1:MAXR + 2], min_val=SH + E - 1, max_val=SH + MAXR - 1) + 1
            with pe.Fori(SH, nt) as t:
                e1 = pe.value_load(tab[0:1, bass.ds(t - SH, 1)], min_val=0, max_val=E)
                e = pe.value_load(tab[0:1, bass.ds(t - SH + 1, 1)], min_val=1, max_val=E)
                slot(t, e, bass.ds(e % RING, 1), e1, bass.ds(e1 % RING, 1))
            slot(nt, E, E % RING, E, E % RING, final=True)

        @block.scalar
        def _(act):
            def deviation(name, n, g):
                l = lns[name]
                act.wait_ge(s[name + "_mv"], g + 1)
                act.activation(l["sd"][0:n, :], l["mv"][0:n, :, 1], ACT.Sqrt, bias=eps[0:n, :]).then_inc(s[name + "_sd"], 1)

            def norm(name, src, dst, done, n, g):
                l = lns[name]
                act.wait_ge(s[name + "_nmr"], g + 1)
                for b in range(GB):
                    last = act.activation(dst[:, b, :], src(b), ACT.Identity, bias=l["nmr"][0:n, b:b + 1],
                                          scale=l["r"][0:n, b:b + 1])
                last.then_inc(s[done], 1)

            def regroup(c):
                act.wait_ge(s["img_in"], 16 * HP)
                act.activation(img_p[:, c, :].rearrange("q (wp r v) -> q wp r v", r=PATCH, v=PATCH),
                           img[:, c, :].rearrange("q (r wp v) -> q wp r v", r=PATCH, v=PATCH), ACT.Copy).then_inc(s["imgp_act"], 1)

            def x1():
                for j in range(0, 2 * KX, 2):
                    act.wait_ge(s["xtr"], j + 1)
                    act.activation(pt[:, j // 2, 0:XH], ([pS[:, r, :] for r in range(4)] + [pT[:, 0, :], pT[:, 1, :],
                                   pV[:, 0, :], pV[:, 1, :]])[j % 8][:, 0:XH], ACT.Copy).then_inc(s["pt_act"], 1)

            def embedded(m, n_mm, src, batches, dst, done):
                b0, b1 = batches
                act.wait_ge(s["tokmm"], n_mm)
                act.activation(dst.rearrange("p b (hp wp) -> p wp hp b", wp=HP),
                               src[:, m, 0:(b1 - b0) * NP].rearrange("p (wp hp b) -> p wp hp b", hp=HP, b=b1 - b0),
                               ACT.Identity, bias=vec[:, m:m + 1]).then_inc(s[done], 1)

            def split_hi(k, m):
                act.wait_ge(s[f"w{m}_in"], 16 * k + 16)
                w = slice(m * WCOLS, (m + 1) * WCOLS)
                if isinstance(k, int):
                    hi = w_hi[:, k % RING, w]
                else:
                    hi = w_hi[:, bass.ds(k % RING, 1), w].rearrange("p a n -> p (a n)")
                act.activation(hi, raw[m][:, :], ACT.Copy).then_inc(s["wsp_hi"], 1)

            def x2(g):
                act.wait_ge(s["tok_t"], g)
                act.activation(tokT[:, :, :, 0:NC], tokT_all[:, :, bass.ds(g * GB, GB), :], ACT.Copy).then_inc(s["tokT_ok"], 1)

            def x4(g):
                norm("lt", lambda b: tok[:, b, :], tok, "tn_ok", NC, g)

            def x5(g):
                act.wait_ge(s["xn_t"], 2 * g)
                norm("lx", lambda b: h[:, bass.ds(g * GB + b, 1), :].rearrange("t b d -> t (b d)"), xn, "xn_ok", S, g)

            def x6(g):
                act.wait_ge(s["xn_t"], 2 * g + 1)
                act.wait_ge(s["g_mm"], 2 * g)
                act.activation(xnT[:, 0, :], pT[:, 0, 0:GS], ACT.Copy).then_inc(s["xnT_act"], 1)

            def x7_keys(g):
                act.wait_ge(s["sc"], 2 * GB * g)
                for m in range(KD):
                    act.wait_ge(s["k_mm"], 2 * g + m + 1)
                    last = act.activation(kT[:, m, :], pS[:, m, 0:GS], ACT.Identity, bias=vec[:, 2 * KD + m:2 * KD + m + 1])
                last.then_inc(s["k_ok"], 1)

            def x7_gate(g):
                act.wait_ge(s["u_ok"], g)
                for m in range(KD):
                    act.wait_ge(s["g_mm"], 2 * g + m + 1)
                    last = act.activation(gate[:, m, :], pS[:, 2 + m, 0:GS], ACT.Sigmoid,
                                          bias=vec[:, 3 * KD + m:3 * KD + m + 1])
                last.then_inc(s["g_ok"], 1)

            def retained(b):
                return pV[:, b % 2, 0:4 * S].rearrange("p (m o t) -> p m o t", m=KD, o=2)

            def y1(g, b):
                act.wait_ge(s["pv"], GB * g + b + 1)
                act.activation(r_even[:, b % 2, :, :], retained(b)[:, :, 0, :], ACT.Copy, scale=cst("even")).then_inc(s["re_ok"], 1)

            def y2_square(g):
                act.wait_ge(s["cen_ok"], g + 1)
                act.wait_ge(s["var_mm"], g)
                act.activation(sqT[:, :, :], rT[:, :, :], ACT.Square).then_inc(s["sq_ok"], 1)

            def y2_deviation(g):
                act.wait_ge(s["var_mm"], g + 1)
                act.wait_ge(s["zn_ok"], g)
                act.activation(sdT[:, :], pV[:, 1, 0:GS], ACT.Sqrt, bias=eps[:, :], scale=1.0 / D).then_inc(s["sdT_ok"], 1)

            def y3(g):
                act.wait_ge(s["zn_ok"], g + 1)
                act.wait_ge(s["o_mm"], g)
                for m in range(KD):
                    last = act.activation(uT[:, m, :], rT[:, m, :], ACT.Identity,
                                          scale=vec[:, 4 * KD + m:4 * KD + m + 1], bias=vec[:, 5 * KD + m:5 * KD + m + 1])
                last.then_inc(s["z_ok"], 1)

            def y5(g):
                act.wait_ge(s["xn2_st"], 16 * g)
                act.wait_ge(s["xn2_cp"], 16 * g)
                act.wait_ge(s["x2_t"], 2 * g)
                norm("l2", lambda b: h2[:, b, :], xn2, "xn2_ok", S, g)
                hrows = hs[0:T, :].rearrange("(b t) d -> t b d", t=S)
                act.dma_start(hrows[:, bass.ds(g * GB, GB), :], h2[:, :, :]).then_inc(s["h2_st"], 16)
                act.wait_ge(s["xn2_ok"], g + 1)
                act.dma_start(tokens[:, bass.ds(g * GB, GB), :], xn2[:, :, :]).then_inc(s["xn2_st"], 16)
                act.dma_start(h[0:S, bass.ds(g * GB, GB), :], xn2[:, :, :]).then_inc(s["xn2_cp"], 16)

            def y6_transposed(g):
                act.wait_ge(s["lg_mm"], g)
                for m in range(KD):
                    act.wait_ge(s["x2_t"], 2 * g + m + 1)
                    last = act.activation(x2T[:, m, :], pT[:, m, 0:GS], ACT.Copy)
                last.then_inc(s["x2T_ok"], 1)

            def y6_logits(g):
                act.wait_ge(s["lg_mm"], g + 1)
                act.activation(lg[:, bass.ds(g * GB, GB), :].rearrange("t b e -> t (b e)"), pT[0:S, 0, 0:GB * E],
                               ACT.Copy).then_inc(s["lg_ok"], 1)

            def load_rows(t):
                act.dma_start(xr[:, :], xs[bass.ds(t * ROWS, ROWS), :]).then_inc(s["xr_in"], 16)

            def x_hi(t, bank):
                act.wait_ge(s["xt"], t + 1)
                act.activation(xT_hi[:, :, :].rearrange("p k n -> p (k n)"), bank, ACT.Copy).then_inc(s["xhi"], 1)

            def gelu(hf, t):
                act.wait_ge(s[f"u{hf}"], t + 1)
                act.wait_ge(s[f"hid{hf}"], t)
                act.activation(gl[:, hf, :], pU[hf][0], ACT.Gelu).then_inc(s[f"g{hf}"], 1)

            act.wait_ge(s["eps_set"], 1)
            regroup(1)
            x1()
            act.wait_ge(s["xtr"], 2 * KX)
            act.wait_ge(s["vec_ok"], 1)
            act.wait_ge(s["col_set"], 1)
            embedded(0, 1, pV, (0, GB), tokT[:, 0, :, 1:NC], "emb0_act")
            split_hi(0, 0)
            split_hi(0, 1)
            act.wait_ge(s["txt_in"], 16)
            deviation("lt", NC, 0)
            x4(0)
            embedded(0, 2, pS, (GB, B), tokT_all[:, 0, GB:B, 1:NC], "emb_act")
            deviation("lx", S, 0)
            x5(0)
            x6(0)
            act.wait_ge(s["vec_ok"], 1)
            x7_keys(0)
            x7_gate(0)
            act.wait_ge(s["emb_act"], 1)
            act.wait_ge(s["emb_dve"], 1)

            def step(i, first=False, last=False):
                deviation("lt", NC, i + 1)
                x4(i + 1)
                y1(i, 0)
                y1(i, 1)
                if not first:
                    deviation("l2", S, i - 1)
                if not first:
                    y5(i - 1)
                deviation("lx", S, i + 1)
                y1(i, 2)
                if not first:
                    y6_transposed(i - 1)
                y1(i, 3)
                x5(i + 1)
                if not first:
                    y6_logits(i - 1)
                x6(i + 1)
                y2_square(i)
                x7_keys(i + 1)
                y2_deviation(i)
                y3(i)
                x7_gate(i + 1)
                if not last:
                    x2(i + 2)
            x2(1)
            step(0, first=True)
            with act.Fori(1, NG - 2) as i:
                step(i)
            step(NG - 2, last=True)
            act.wait_ge(s["zero_out"], 16)
            act.wait_ge(s["xn2_st"], 16)
            load_rows(0)
            y1(NG - 1, 0)
            deviation("l2", S, NG - 2)
            y1(NG - 1, 1)
            y5(NG - 2)
            y1(NG - 1, 2)
            y6_transposed(NG - 2)
            y1(NG - 1, 3)
            y6_logits(NG - 2)
            y2_square(NG - 1)
            x_hi(0, pX0)
            load_rows(1)
            y2_deviation(NG - 1)
            y3(NG - 1)
            gelu(0, 0)
            gelu(1, 0)
            deviation("l2", S, NG - 1)
            y5(NG - 1)
            x_hi(1, pX)
            act.wait_ge(s["xn2_st"], 16 * (NG - 1))
            load_rows(2)
            y6_transposed(NG - 1)
            y6_logits(NG - 1)
            assert 2 * ROWS <= GS and 3 * ROWS <= (NG - 1) * GS

            def slot(t, look=None, split=None, final=False, gated=False):
                act.wait_ge(s["tr0"], t)
                act.activation(hT_hi[:, 0, :, :].rearrange("p c n -> p (c n)"), pH[0], ACT.Copy).then_inc(s["hi0"], 1)
                if look:
                    look()
                if not final:
                    gelu(0, t)
                act.wait_ge(s["tr1"], t)
                act.wait_ge(s["y_mm"], t - 1)
                act.activation(hT_hi[:, 1, :, :].rearrange("p c n -> p (c n)"), pH[1], ACT.Copy).then_inc(s["hi1"], 1)
                if split:
                    split(0)
                if not final:
                    gelu(1, t)
                    x_hi(t + 1, pX)
                    if gated:
                        act.wait_ge(s["scattered"], 16 * B)
                    load_rows(t + 2)
                if split:
                    split(1)
                act.wait_ge(s["y_mm"], t)
                act.wait_ge(s["y_st"], 16 * (t - 1))
                act.activation(y_sb[:, :], pY, ACT.Copy).then_inc(s["y_ev"], 1)
                act.wait_ge(s["y_ev"], t)
                act.dma_start(ys[bass.ds((t - 1) * ROWS, ROWS), :], y_sb[:, :])\
                    .then_inc(s["last_st" if final else "y_st"], 16)

            act.wait_ge(s["xn2_st"], 16 * NG)
            act.wait_ge(s["zero_y"], 16)
            slot(1, split=lambda m: split_hi(1, m))
            with act.Fori(2, SH - 2) as t:
                slot(t)
            slot(SH - 2, gated=True)
            slot(SH - 1, split=lambda m: split_hi(2, m))
            act.wait_ge(s["tab_ok"], 1)
            nt = act.value_load(tab[0:1, MAXR + 1:MAXR + 2], min_val=SH + E - 1, max_val=SH + MAXR - 1) + 1
            with act.Fori(SH, nt) as t:
                expert = {}

                def look():
                    expert["before"] = act.value_load(tab[0:1, bass.ds(t - SH, 1)], min_val=0, max_val=E)
                    expert["now"] = act.value_load(tab[0:1, bass.ds(t - SH + 1, 1)], min_val=1, max_val=E)

                def split_next(m):
                    with act.If(expert["now"] != expert["before"]):
                        with act.If(expert["now"] < E - 1):
                            split_hi(expert["now"] + 2, m)
                slot(t, look, split_next)
            slot(nt, final=True)

        @block.vector
        def _(dve):
            def sums(name, src, n, batches):
                for b in batches:
                    last = dve.bn_stats(lns[name]["st"][0:n, b, :], src(b))
                return last

            def stats(name, src, n, g, batches=range(GB)):
                l = lns[name]
                sums(name, src, n, batches).then_inc(s[name + "_st"], 1)
                dve.wait_ge(s[name + "_st"], g + 1)
                dve.memset(l["tick"][0:1, :], 0.0)
                for b in range(GB):
                    last = dve.bn_aggr(l["mv"][0:n, b, :], l["st"][0:n, b, :])
                last.then_inc(s[name + "_mv"], 1)

            def recip(name, n, g, with_mean=True):
                l = lns[name]
                dve.wait_ge(s[name + "_sd"], g + 1)
                dve.reciprocal(l["r"][0:n, :], l["sd"][0:n, :]).then_inc(s[name + "_r"], 1)
                if with_mean:
                    dve.wait_ge(s[name + "_r"], g + 1)
                    dve.scalar_tensor_tensor(out=l["nmr"][0:n, :], in0=l["mv"][0:n, :, 0], scalar=-1.0,
                                             in1=l["r"][0:n, :], op0=ALU.mult, op1=ALU.mult).then_inc(s[name + "_nmr"], 1)

            def regroup(c):
                dve.wait_ge(s["img_in"], 16 * HP)
                dve.tensor_copy(img_p[:, c, :].rearrange("q (wp r v) -> q wp r v", r=PATCH, v=PATCH),
                                img[:, c, :].rearrange("q (r wp v) -> q wp r v", r=PATCH, v=PATCH)).then_inc(s["imgp_dve"], 1)

            def x1():
                for j in range(1, 2 * KX, 2):
                    dve.wait_ge(s["xtr"], j + 1)
                    bank = (pS[:, j % 8, :] if j % 8 < 4 else (pT if j % 8 < 6 else pV)[:, j % 2, :])
                    dve.tensor_copy(pt[:, j // 2, XH:2 * XH], bank[:, 0:XH]).then_inc(s["pt_dve"], 1)

            def embedded(m, n_mm, src, batches, dst, done):
                b0, b1 = batches
                dve.wait_ge(s["tokmm"], n_mm)
                dve.tensor_scalar(dst.rearrange("p b (hp wp) -> p wp hp b", wp=HP),
                                  src[:, m, 0:(b1 - b0) * NP].rearrange("p (wp hp b) -> p wp hp b", hp=HP, b=b1 - b0),
                                  vec[:, m:m + 1], None, ALU.add).then_inc(s[done], 1)

            def split3(k):
                w3 = slice(2 * WCOLS, 3 * WCOLS)
                if isinstance(k, int):
                    lo, hi = w_lo[:, k % RING, w3], w_hi[:, k % RING, w3]
                else:
                    lo, hi = (w[:, bass.ds(k % RING, 1), w3].rearrange("p a n -> p (a n)") for w in (w_lo, w_hi))
                dve.wait_ge(s["w2_in"], 16 * k + 16)
                dve.tensor_copy(hi, raw[2][:, :]).then_inc(s["wsp_hi3"], 1)
                dve.wait_ge(s["wsp_hi3"], k + 1)
                dve.tensor_tensor(lo, raw[2][:, :], hi.bitcast(F32), ALU.subtract).then_inc(s["wsp_lo3"], 1)

            def x_lo(t, bank):
                dve.wait_ge(s["xhi"], t + 1)
                dve.tensor_tensor(xT_lo[:, :, :].rearrange("p k n -> p (k n)"), bank,
                                  xT_hi[:, :, :].rearrange("p k n -> p (k n)").bitcast(F32), ALU.subtract).then_inc(s["xlo"], 1)

            def hidden(hf, t):
                dve.wait_ge(s[f"g{hf}"], t + 1)
                if not isinstance(t, int) or t > 0:
                    dve.wait_ge(s[f"tr{hf}"], t)
                dve.tensor_tensor(hid[:, hf, :], pU[hf][1], gl[:, hf, :], ALU.mult).then_inc(s[f"hid{hf}"], 1)

            def hidden_lo(hf, t):
                dve.wait_ge(s[f"hi{hf}"], t + 1)
                f = "p c n -> p (c n)"
                dve.tensor_tensor(hT_lo[:, hf, :, :].rearrange(f), pH[hf], hT_hi[:, hf, :, :].rearrange(f).bitcast(F32),
                                  ALU.subtract).then_inc(s[f"lo{hf}"], 1)

            def x3(g):
                dve.wait_ge(s["tok_t"], g + 1)
                dve.wait_ge(s["ht_ok"], g)
                dve.tensor_tensor(tok[:, :, :], pT[0:NC, :, :].rearrange("t a (b d) -> t (a b) d", d=D),
                                  row_bias[:, :].unsqueeze(1).to_broadcast([NC, GB, D]), ALU.add).then_inc(s["tok_ok"], 1)

            def x4a(g):
                dve.wait_ge(s["tok_ok"], g + 1)
                sums("lt", lambda b: tok[:, b, :], NC, range(GB // 2))

            def x4b(g):
                stats("lt", lambda b: tok[:, b, :], NC, g, range(GB // 2, GB))

            def x4c(g):
                recip("lt", NC, g)

            def x4d(g):
                dve.wait_ge(s["tn_ok"], g + 1)
                dve.tensor_tensor(tok[:, :, :], tok[:, :, :], gam_b[:, :].unsqueeze(1).to_broadcast([NC, GB, D]), ALU.mult)\
                    .then_inc(s["ht_c"], 1)

            def x5a(g):
                dve.wait_ge(s["ht_ok"], g + 1)
                dve.memset(tick[:, 1:2], 0.0)
                stats("lx", lambda b: h[:, bass.ds(g * GB + b, 1), :].rearrange("t b d -> t (b d)"), S, g)

            def x5b(g):
                recip("lx", S, g)

            def x6(g):
                dve.wait_ge(s["xn_t"], 2 * g + 2)
                dve.wait_ge(s["g_mm"], 2 * g)
                dve.tensor_copy(xnT[:, 1, :], pT[:, 1, 0:GS]).then_inc(s["xnT_dve"], 1)

            def x7_queries(g):
                dve.wait_ge(s["sc"], 2 * GB * g)
                for m in range(KD):
                    dve.wait_ge(s["q_mm"], 2 * g + m + 1)
                    for o, which in enumerate(("even", "odd")):
                        last = dve.tensor_scalar(qq[:, m, :, o, :], pS[:, 2 + m, 0:GS].rearrange("p (b t) -> p b t", b=GB),
                                                 vec[:, KD + m:KD + m + 1], cst(which), ALU.add, ALU.mult)
                last.then_inc(s["q_ok"], 1)

            def x7_values(g):
                dve.wait_ge(s["v_mm"], g + 1)
                dve.wait_ge(s["pv"], GB * g)
                dve.tensor_tensor(vv[:, :, :], pT[0:S, :, :].rearrange("t a (b d) -> t (a b) d", d=D),
                                  bv_b[:, :].unsqueeze(1).to_broadcast([S, GB, D]), ALU.add).then_inc(s["v_ok"], 1)

            def y1(g, b):
                for half in range(2):
                    dve.wait_ge(s["sc"], 2 * (GB * g + b) + 1 + half)
                    if b >= 2:
                        dve.wait_ge(s["pv"], GB * g + b - 1)
                    a = 2 * half
                    dve.tensor_tensor(pr[:, b % 2, 8 * half:8 * half + 8, :].rearrange("t (r m) s -> t r m s", r=2),
                                      pS[0:S, a:a + 2, 0:4 * S].rearrange("t r (m s) -> t r m s", m=4),
                                      cst("decay", S).unsqueeze(1).unsqueeze(1).to_broadcast([S, 2, 4, S]), ALU.mult)\
                        .then_inc(s["p_ok"], 1)

            def y1_gather(g, b):
                dve.wait_ge(s["re_ok"], GB * g + b + 1)
                odd = pV[:, b % 2, 0:4 * S].rearrange("p (m o t) -> p m o t", m=KD, o=2)[:, :, 1, :]
                dve.scalar_tensor_tensor(out=rT[:, :, b * S:(b + 1) * S], in0=odd, scalar=cst("odd"), in1=r_even[:, b % 2, :, :],
                                         op0=ALU.mult, op1=ALU.add).then_inc(s["rt_ok"], 1)

            def y2_center(g):
                dve.wait_ge(s["mean_mm"], g + 1)
                dve.scalar_tensor_tensor(out=rT[:, :, :], in0=pV[:, 0:1, 0:GS].to_broadcast([P, KD, GS]), scalar=-1.0 / D,
                                         in1=rT[:, :, :], op0=ALU.mult, op1=ALU.add).then_inc(s["cen_ok"], 1)

            def y2_scale(g):
                dve.wait_ge(s["sdT_ok"], g + 1)
                dve.reciprocal(sdT[:, :], sdT[:, :]).then_inc(s["rinv_ok"], 1)
                dve.wait_ge(s["rinv_ok"], g + 1)
                dve.tensor_tensor(rT[:, :, :], rT[:, :, :], sdT[:, :].unsqueeze(1).to_broadcast([P, KD, GS]), ALU.mult)\
                    .then_inc(s["zn_ok"], 1)

            def y3(g):
                dve.wait_ge(s["z_ok"], g + 1)
                dve.tensor_tensor(uT[:, :, :], uT[:, :, :], gate[:, :, :], ALU.mult).then_inc(s["u_ok"], 1)

            def y4(g):
                dve.wait_ge(s["o_mm"], g + 1)
                dve.wait_ge(s["hb_ok"], g + 1)
                dve.tensor_tensor(h2[:, :, :], pV[0:S, :, :].rearrange("t a (b d) -> t (a b) d", d=D), h2[:, :, :],
                                  ALU.add).then_inc(s["h2_ok"], 1)

            def y5a(g):
                dve.wait_ge(s["h2_ok"], g + 1)
                dve.memset(tick[:, 4:5], 0.0)
                sums("l2", lambda b: h2[:, b, :], S, range(GB // 2))

            def y5b(g):
                stats("l2", lambda b: h2[:, b, :], S, g, range(GB // 2, GB))

            def y5c(g):
                recip("l2", S, g)

            dve.wait_ge(s["vec_t"], 1)
            dve.tensor_copy(vec[:, :], pV[:, 0, 0:6 * KD]).then_inc(s["vec_ok"], 1)
            dve.wait_ge(s["vec_ok"], 1)
            dve.wait_ge(s["rest_in"], 112)
            dve.tensor_tensor(row_bias[0:1, :], row_bias[0:1, :], tok[0:1, 0, :], ALU.add).then_inc(s["cls_ok"], 1)
            regroup(0)
            regroup(2)
            x1()
            dve.wait_ge(s["xtr"], 2 * KX)
            dve.wait_ge(s["cls_ok"], 1)
            dve.wait_ge(s["col_set"], 1)
            embedded(1, 1, pV, (0, GB), tokT[:, 1, :, 1:NC], "emb0_dve")
            split3(0)
            x3(0)
            x4a(0)
            x4b(0)
            x4c(0)
            x4d(0)
            embedded(1, 2, pS, (GB, B), tokT_all[:, 1, GB:B, 1:NC], "emb_dve")
            dve.wait_ge(s["txt_in"], 16)
            x5a(0)
            x5b(0)
            x6(0)
            x7_queries(0)
            x7_values(0)

            def step(i, first=False):
                y1(i, 0)
                x3(i + 1)
                x4a(i + 1)
                y1(i, 1)
                x4b(i + 1)
                if not first:
                    y5a(i - 1)
                x4c(i + 1)
                y1(i, 2)
                if not first:
                    y5b(i - 1)
                y1_gather(i, 0)
                x4d(i + 1)
                y1_gather(i, 1)
                if not first:
                    y5c(i - 1)
                y1(i, 3)
                x5a(i + 1)
                x5b(i + 1)
                y1_gather(i, 2)
                y1_gather(i, 3)
                x6(i + 1)
                y2_center(i)
                x7_queries(i + 1)
                y2_scale(i)
                x7_values(i + 1)
                y3(i)
                y4(i)
            assert GB == 4
            step(0, first=True)
            with dve.Fori(1, NG - 1) as i:
                step(i)
            y1(NG - 1, 0)
            y5a(NG - 2)
            y5b(NG - 2)
            y1(NG - 1, 1)
            y5c(NG - 2)
            y1_gather(NG - 1, 0)
            y1(NG - 1, 2)
            y1_gather(NG - 1, 1)
            y1(NG - 1, 3)
            y1_gather(NG - 1, 2)
            y1_gather(NG - 1, 3)
            y2_center(NG - 1)
            x_lo(0, pX0)
            y2_scale(NG - 1)
            y3(NG - 1)
            hidden(0, 0)
            hidden(1, 0)
            y4(NG - 1)
            y5a(NG - 1)
            y5b(NG - 1)
            y5c(NG - 1)
            x_lo(1, pX)

            n = {"route": 0, "count_ok": 0}

            def then(ins, name="route"):
                n[name] += 1
                ins.then_inc(s[name], 1)
                dve.wait_ge(s[name], n[name])

            dve.wait_ge(s["lg_ok"], NG)
            be = [S, B, E]
            then(dve.tensor_reduce(mx[:, :], lg[:, :, :], AX.X, ALU.max))
            then(dve.tensor_tensor(eq[:, :, :], lg[:, :, :], mx[:, :].unsqueeze(2).to_broadcast(be), ALU.is_equal))
            then(dve.scalar_tensor_tensor(out=posm[:, :, :], in0=eq[:, :, :], scalar=-float(E),
                                          in1=cst("expert_late", S).unsqueeze(1).to_broadcast(be),
                                          op0=ALU.mult, op1=ALU.add))
            then(dve.tensor_reduce(idx[:, :], posm[:, :, :], AX.X, ALU.min))
            dve.tensor_tensor(pick[:, :, :], cst("expert", S).unsqueeze(1).to_broadcast(be),
                              idx[:, :].unsqueeze(2).to_broadcast(be), ALU.is_equal).then_inc(s["pick_ok"], 1)
            hidden_lo(0, 0)
            hidden(0, 1)
            dve.wait_ge(s["count_mm"], 1)
            dve.tensor_copy(befo[:, :, :], pC[:, 0:B * E].rearrange("t (b e) -> t b e", e=E))
            then(dve.tensor_copy(tot[:, :, :], pC[:, B * E:2 * B * E].rearrange("t (b e) -> t e b", e=E)), "count_ok")
            hidden_lo(1, 0)
            hidden(1, 1)
            x_lo(2, pX)

            def slot(t, between=None, look=None, final=False):
                hidden_lo(0, t - 1)
                if look:
                    look()
                if not final:
                    hidden(0, t)
                hidden_lo(1, t - 1)
                if between:
                    between()
                if not final:
                    x_lo(t + 1, pX)
                    hidden(1, t)

            def places():
                fl = "t e b -> t (e b)"
                then(dve.tensor_tensor_scan(cin[:, :, :].rearrange(fl), cst("ones", S)[:, 0:B * E], tot[:, :, :].rearrange(fl),
                                            0.0, ALU.mult, ALU.add))
                then(dve.tensor_tensor(cex[:, :, :], cin[:, :, :], tot[:, :, :], ALU.subtract))
                then(dve.tensor_tensor(cnt[:, :], cin[:, :, B - 1], cex[:, :, 0], ALU.subtract))
                then(dve.tensor_tensor(over[:, :, :], cnt[:, :].unsqueeze(2).to_broadcast([S, E, NTHR]),
                                       cst("thr", S).unsqueeze(1).to_broadcast([S, E, NTHR]), ALU.is_gt))
                then(dve.tensor_reduce(tiles[:, :], over[:, :, :], AX.X, ALU.add))
                then(dve.tensor_tensor_scan(tin[:, :], cst("ones", S)[:, 0:E], tiles[:, :], 0.0, ALU.mult, ALU.add))
                then(dve.tensor_tensor(tex[:, :], tin[:, :], tiles[:, :], ALU.subtract))

            def rows_and_table():
                then(dve.scalar_tensor_tensor(out=delta[:, :], in0=tex[:, :], scalar=float(ROWS), in1=cex[:, :, 0],
                                              op0=ALU.mult, op1=ALU.subtract))
                then(dve.tensor_tensor(pos[:, :, :].rearrange("t b e -> t e b"), cex[:, :, :],
                                       delta[:, :].unsqueeze(2).to_broadcast([S, E, B]), ALU.add))
                then(dve.tensor_tensor(posm[:, :, :], pos[:, :, :], befo[:, :, :], ALU.add))
                then(dve.tensor_tensor(pos[:, :, :], posm[:, :, :], pick[:, :, :], ALU.mult))
                then(dve.tensor_reduce(row_f[:, :], pos[:, :, :], AX.X, ALU.add))
                dve.tensor_scalar(rows_sb[0:S, :], row_f[:, :], float(SH * ROWS), None, ALU.add).then_inc(s["rows_ok"], 1)
                then(dve.tensor_tensor(ord_c[:, :, :], tex[0:1, :].unsqueeze(1).to_broadcast([1, MAXR, E]),
                                       cst("tile", 1).unsqueeze(2).to_broadcast([1, MAXR, E]), ALU.is_le))
                dve.memset(tab_f[0:1, 0:1], 0.0)
                dve.tensor_reduce(tab_f[0:1, 1:MAXR + 1], ord_c[:, :, :], AX.X, ALU.add)
                then(dve.tensor_scalar(tab_f[0:1, MAXR + 1:MAXR + 2], tin[0:1, E - 1:E], float(SH - 1), None, ALU.add))
                dve.tensor_copy(tab[0:1, :], tab_f[:, :]).then_inc(s["tab_ok"], 1)

            slot(2, places)
            slot(3, rows_and_table)
            with dve.Fori(4, SH - 2) as t:
                slot(t)
            slot(SH - 2, lambda: split3(1))
            slot(SH - 1)
            dve.wait_ge(s["tab_ok"], 1)
            nt = dve.value_load(tab[0:1, MAXR + 1:MAXR + 2], min_val=SH + E - 1, max_val=SH + MAXR - 1) + 1
            with dve.Fori(SH, nt) as t:
                expert = {}

                def look():
                    expert["before"] = dve.value_load(tab[0:1, bass.ds(t - SH, 1)], min_val=0, max_val=E)
                    expert["now"] = dve.value_load(tab[0:1, bass.ds(t - SH + 1, 1)], min_val=1, max_val=E)

                def split_next():
                    with dve.If(expert["now"] != expert["before"]):
                        with dve.If(expert["now"] < E):
                            split3(expert["now"] + 1)
                slot(t, split_next, look)
            slot(nt, final=True)
            dve.wait_ge(s["h_in"], 32)
            dve.wait_ge(s["ysh_in"], 32)
            for c in range(SH):
                n_r = min(ROWS, T - c * ROWS)
                dve.tensor_tensor(ysh[0:n_r, c, :], ysh[0:n_r, c, :], h_fl[0:n_r, c, :], ALU.add).then_inc(s["sum1"], 1)
            dve.wait_ge(s["gathered"], 16 * SH)
            for c in range(SH):
                n_r = min(ROWS, T - c * ROWS)
                dve.wait_ge(s["sum1"], c + 1)
                dve.tensor_tensor(h_fl[0:n_r, c, :], ysh[0:n_r, c, :], yg[0:n_r, c, :], ALU.add).then_inc(s["sum2"], 1)


INS = {"x": "x", "txt": "txt", "tok_W": "L0_tok_W", "tok_b": "L0_tok_b", "cls": "L0_tok_cls_token",
       "pos": "L0_tok_pos_embedding", "tg": "L0_tok_gamma", "tb": "L0_tok_beta", "Wq": "L0_attn_Wq", "bq": "L0_attn_bq",
       "Wk": "L0_attn_Wk", "bk": "L0_attn_bk", "Wv": "L0_attn_Wv", "bv": "L0_attn_bv", "Wg": "L0_attn_Wg",
       "bg": "L0_attn_bg", "Wo": "L0_attn_Wo", "bo": "L0_attn_bo", "ga": "L0_attn_gamma", "ba": "L0_attn_beta",
       "w1s": "L0_ffn_w1s", "w2s": "L0_ffn_w2s", "w3s": "L0_ffn_w3s", "W1": "L0_ffn_W1", "W2": "L0_ffn_W2",
       "W3": "L0_ffn_W3", "Wr": "L0_ffn_Wg"}


def kernel(**inputs):
    import concourse.bacc as bacc
    from concourse.bass_utils import run_bass_kernel_spmd

    nc = bacc.Bacc("TRN2", target_bir_lowering=False, num_devices=1)
    arrays = {n: np.ascontiguousarray(inputs[full]) for n, full in INS.items()}
    B, C, H, _ = arrays["x"].shape
    z = shapes_of(B, C, H, arrays["txt"].shape[1], arrays["txt"].shape[2], arrays["w1s"].shape[1])
    arrays["const"], cols = constants(z)
    aps = {n: nc.dram_tensor("in_" + n, v.shape, F32, kind="ExternalInput").ap() for n, v in arrays.items()}
    out = nc.dram_tensor("out_h", (B, z["S"], z["D"]), F32, kind="ExternalOutput").ap()
    build(nc, aps, out, z, cols)
    r = run_bass_kernel_spmd(nc, [{"in_" + n: v for n, v in arrays.items()}], core_ids=[0])
    return r.results[0]["out_h"]
```

```python
from contextlib import ExitStack

import concourse.bass as bass
import numpy as np
from concourse import mybir

F32 = mybir.dt.float32
F32R = mybir.dt.float32r
I32 = mybir.dt.int32
ALU = mybir.AluOpType
ACT = mybir.ActivationFunctionType
AX = mybir.AxisListType

P = 128
EPS = 1e-5
DECAY = 0.99
HEADS = 16
DH = 16
PATCH = 16
GB = 4
E_ROUTED = 8
ROWS = 128
LATE = 2
RING = 3


def shapes_of(B, C, HW, S_TXT, D, F):
    z = {}
    z["B"], z["C"], z["HW"], z["D"], z["F"] = B, C, HW, D, F
    z["HP"] = HW // PATCH
    z["NP"] = z["HP"] ** 2
    z["NC"] = z["NP"] + 1
    z["S"] = z["NC"] + S_TXT
    z["T"] = B * z["S"]
    z["NG"] = B // GB
    z["SH_TILES"] = -(-z["T"] // ROWS)
    z["MAX_ROUTED"] = (z["T"] - E_ROUTED) // ROWS + E_ROUTED
    return z


def constants(z):
    S = z["S"]
    n_thr = -(-z["T"] // ROWS)
    cols, parts = {}, []

    def put(name, a):
        full = np.zeros((P, a.shape[1]), np.float32)
        full[:a.shape[0]] = a
        at = sum(x.shape[1] for x in parts)
        cols[name] = (at, at + a.shape[1])
        parts.append(full)

    put("ident", np.eye(P, dtype=np.float32))
    t = np.arange(S)
    put("earlier", (t[:, None] < t[None, :]).astype(np.float32))
    put("ones", np.ones((P, P), np.float32))
    diff = (t[None, :] - t[:, None]).astype(np.float32)
    decay = np.power(np.float32(DECAY), np.maximum(diff, 0), dtype=np.float32)
    put("decay", np.where(diff >= 0, decay / np.float32(DH ** 0.5), 0).astype(np.float32))
    e = np.arange(E_ROUTED, dtype=np.float32)[None, :]
    put("expert", np.repeat(e, P, 0))
    put("expert_late", np.repeat(e + E_ROUTED, P, 0))
    thr = np.arange(n_thr, dtype=np.float32)[None, :] * ROWS
    thr[0, 0] = -1
    put("thr", np.repeat(thr, P, 0))
    put("tile", np.repeat(np.arange(z["MAX_ROUTED"], dtype=np.float32)[None, :], P, 0))
    head = np.arange(P) // DH
    put("even", (head % 2 == 0).astype(np.float32)[:, None])
    put("odd", (head % 2 == 1).astype(np.float32)[:, None])
    return np.concatenate(parts, 1), cols


def build(nc, a, out, z, cols):
    B, C, D, F, S, NC, NP, HP, HW, T = (z[k] for k in ("B", "C", "D", "F", "S", "NC", "NP", "HP", "HW", "T"))
    NG, SH, MAXR = z["NG"], z["SH_TILES"], z["MAX_ROUTED"]
    KD = D // P
    KX = C * PATCH * PATCH // P
    GS = GB * S
    QR = HP * B
    XH = HP // 2 * QR
    HALF = F // 2
    FC = HALF // P
    WCOLS = KD * F
    E = E_ROUTED
    NTHR = cols["thr"][1] - cols["thr"][0]
    EARLY = SH - LATE
    AGAIN = E + 1

    xs = nc.dram_tensor("xs", ((SH + MAXR) * ROWS, D), F32, kind="Internal").ap()
    ys = nc.dram_tensor("ys", ((EARLY + MAXR) * ROWS, D), F32, kind="Internal").ap()
    hs = nc.dram_tensor("hs", (SH * ROWS, D), F32, kind="Internal").ap()
    row_d = nc.dram_tensor("row_d", (SH * ROWS, 1), I32, kind="Internal").ap()

    with ExitStack() as ctx:
        base = -(-nc.sbuf_base // 64) * 64
        part = 3 * WCOLS * 4
        slots = [[base + 2 * k * part, base + 2 * (k + 1) * part] for k in range(RING)]
        kept = [slots[-1][1], nc.sbuf_usable_end]

        def sb(name, shape, dt=F32, at=kept):
            size = -(-int(np.prod(shape[1:])) * 4 // 64) * 64
            assert at[0] + size <= at[1], f"no room for {name}: {at}"
            at[0] += size
            return nc.alloc_sbuf_tensor_at(name, shape, dt, offset=at[0] - size)

        def ps(name, shape):
            return ctx.enter_context(nc.psum_tensor(name, shape, F32))

        def sem(name):
            return ctx.enter_context(nc.semaphore(name))

        const = sb("const", [P, max(c[1] for c in cols.values())])
        w_parts = sb("w_parts", [P, RING, 2, 3 * WCOLS], F32R, at=[slots[0][0], slots[-1][1]])
        w_hi, w_lo = w_parts[:, :, 0, :], w_parts[:, :, 1, :]
        raw = [sb(f"raw{m}", [P, WCOLS]) for m in range(3)]
        rows_sb = sb("rows_sb", [P, 2, B], I32)
        LAST, SPLIT3, SPLIT12, ROWS_AT = MAXR + 1, MAXR + 2, 2 * MAXR + 2, 3 * MAXR + 2
        tab = sb("tab", [P, ROWS_AT + MAXR], I32)
        h = sb("h", [S, B, D], at=slots[2])

        def cst(name, n=P):
            lo, hi = cols[name]
            return const[0:n, lo:hi]

        rest = list(kept)
        early = [list(rest), slots[1], slots[0]]

        def front_sb(name, shape, dt=F32):
            size = -(-int(np.prod(shape[1:])) * 4 // 64) * 64
            at = next(x for x in early if x[0] + size <= x[1])
            return sb(name, shape, dt, at=at)

        def late_sb(name, shape, dt=F32):
            return sb(name, shape, dt, at=slots[2])

        eps = late_sb("eps", [P, 1])
        tick = late_sb("tick", [1, 5])
        img = sb("img", [QR, C, PATCH * HW], at=slots[0])
        img_p = sb("img_p", [QR, C, PATCH * HW], at=slots[0])
        pt = front_sb("pt", [P, KX, B * NP])
        w_tok = front_sb("w_tok", [P, KX, D])
        zero = front_sb("zero", [P, D])
        w_q, w_k, w_v, w_g, w_o = (front_sb(n, [P, KD, D]) for n in ("w_q", "w_k", "w_v", "w_g", "w_o"))
        w_r = late_sb("w_r", [P, KD, E])
        vec_rows = front_sb("vec_rows", [6 * KD, P])
        vec = late_sb("vec", [P, 6 * KD])
        row_bias = front_sb("row_bias", [NC, D])
        gam_b = front_sb("gam_b", [NC, D])
        bet_b = front_sb("bet_b", [NC, D])
        bv_b = front_sb("bv_b", [S, D])
        bo_b = late_sb("bo_b", [S, D])
        tokT_all = front_sb("tokT_all", [P, KD, B, NC])
        tokT = front_sb("tokT", [P, KD, GB, S])
        tok = front_sb("tok", [NC, GB, D])
        xn = front_sb("xn", [S, GB, D])
        xnT = front_sb("xnT", [P, KD, GS])
        qq = front_sb("qq", [P, KD, GB, 2, S])
        kT = front_sb("kT", [P, KD, GS])
        vv = front_sb("vv", [S, GB, D])
        gate = front_sb("gate", [P, KD, GS])
        pr = front_sb("pr", [S, 2, HEADS, S])
        r_even = front_sb("r_even", [P, 2, KD, S])
        rT = front_sb("rT", [P, KD, GS])
        sqT = front_sb("sqT", [P, KD, GS])
        sdT = front_sb("sdT", [P, GS])
        uT = front_sb("uT", [P, KD, GS])
        h2 = late_sb("h2", [S, GB, D])
        xn2 = late_sb("xn2", [S, GB, D])
        x2T = late_sb("x2T", [P, KD, GS])
        lg = late_sb("lg", [S, B, E])
        lns = {n: {k: late_sb(f"{n}_{k}s", [S, GB] + w) for k, w in
                   (("st", [6]), ("mv", [2]), ("sd", []), ("r", []), ("nmr", []), ("tick", []))} for n in ("lt", "lx", "l2")}
        befo = late_sb("befo", [S, B, E])
        mx = late_sb("mx", [S, B])
        eq = late_sb("eq", [S, B, E])
        idx = late_sb("idx", [S, B])
        pick = late_sb("pick", [S, B, E])
        tot = late_sb("tot", [S, E, B])
        cin = late_sb("cin", [S, E, B])
        cex = late_sb("cex", [S, E, B])
        cnt = late_sb("cnt", [S, E])
        over = late_sb("over", [S, E, NTHR])
        tiles = late_sb("tiles", [S, E])
        tin = late_sb("tin", [S, E])
        tex = late_sb("tex", [S, E])
        delta = late_sb("delta", [S, E])
        pos = late_sb("pos", [S, B, E])
        posm = late_sb("posm", [S, B, E])
        row_f = late_sb("row_f", [S, B])
        ord_c = late_sb("ord_c", [1, MAXR, E])
        tab_f = late_sb("tab_f", [1, ROWS_AT + MAXR])
        first = late_sb("first", [1, MAXR])
        second = late_sb("second", [1, MAXR])
        beyond = late_sb("beyond", [1, MAXR])
        back = late_sb("back", [1, 1])

        rear = list(rest)
        xr = sb("xr", [ROWS, D], at=rear)
        xT_hi = sb("xT_hi", [P, KD, ROWS], F32R, at=rear)
        xT_lo = sb("xT_lo", [P, KD, ROWS], F32R, at=rear)
        gl = sb("gl", [ROWS, 2, HALF], at=rear)
        hid = sb("hid", [ROWS, 2, HALF], at=rear)
        hT_hi = sb("hT_hi", [P, 2, FC, ROWS], F32R, at=rear)
        hT_lo = sb("hT_lo", [P, 2, FC, ROWS], F32R, at=rear)
        y_sb = sb("y_sb", [ROWS, D], at=rear)
        row_t = sb("row_t", [ROWS, SH], I32, at=rear)
        h_fl = sb("h_fl", [ROWS, SH, D], at=rear)
        tail = [base + (E - 1) % RING * 2 * part, base + ((E - 1) % RING + 1) * 2 * part]
        ysh = sb("ysh", [ROWS, EARLY, D], at=tail)
        yg = sb("yg", [ROWS, SH, D], at=tail)

        pS = ps("pS", [P, 4, 512])
        pT = ps("pT", [P, 2, 512])
        pV = ps("pV", [P, 2, 512])
        pU = [(pS[:, 0, :], pS[:, 1, :]), (pS[:, 2, :], pS[:, 3, :])]
        pH = [pT[:, 0, :], pT[:, 1, :]]
        pY, pX = pV[:, 0, 0:D], pV[:, 1, 0:KD * ROWS]
        pX0 = pS[:, 2, 0:KD * ROWS]
        banks = [pS[:, r, :] for r in range(4)] + [pT[:, 0, :], pT[:, 1, :], pV[:, 0, :], pV[:, 1, :]]
        pC = pT[0:S, 1, :]

        names = (
            "const_in vecs_in img_in rest_in txt_in attn_in w0_in w1_in w2_in "
            "eps_set col_set zero_set zero_out zero_y "
            "vec_t vec_ok cls_ok imgp_act imgp_dve xtr pt_act pt_dve tokmm "
            "emb0_act emb0_dve emb_act emb_dve tokT_ok "
            "tok_t tok_ok tn_ok ht_c ht_ok "
            "xn_ok xn_t xnT_act xnT_dve "
            "q_mm k_mm v_mm g_mm q_ok k_ok v_ok g_ok "
            "sc p_ok pv re_ok rt_ok "
            "mean_mm cen_ok sq_ok var_mm sdT_ok rinv_ok zn_ok z_ok "
            "u_ok o_mm hb_ok h2_ok xn2_ok h2_st xn2_st xn2_cp "
            "x2_t x2T_ok lg_mm lg_ok "
            "pick_ok count_mm count_ok route rows_ok tab_ok row_st row_in scattered "
            "w12_hi w12_lo w3_hi w3_lo "
            "xr_in x_tr x_hi x_lo "
            "up0 up1 gelu0 gelu1 hid0 hid1 hid_tr0 hid_tr1 hid_hi0 hid_hi1 hid_lo0 hid_lo1 "
            "y_mm y_ev y_st last_st "
            "h_in ysh_in gathered gathered_late sum1 sum2 sum3 late_out out_st").split()
        s = {n: sem(n) for n in names}
        for n in lns:
            for k in ("st", "mv", "sd", "r", "nmr"):
                s[f"{n}_{k}"] = sem(f"{n}_{k}")

        x_in = a["x"]
        tokens = xs[0:T, :].rearrange("(b t) d -> t b d", t=S)

        block = ctx.enter_context(nc.Block())

        @block.sync
        def _(sp):
            sp.dma_start(const[:, :], a["const"]).then_inc(s["const_in"], 16)
            for r in range(HP):
                sp.dma_start(img[r * B:(r + 1) * B, :, :],
                             x_in[:, :, r * PATCH:(r + 1) * PATCH, :].rearrange("b c r w -> b c (r w)")).then_inc(s["img_in"], 16)
            for n, v in enumerate(("tok_b", "bq", "bk", "bg", "ga", "ba")):
                sp.dma_start(vec_rows[n * KD:(n + 1) * KD, :],
                             a[v].rearrange("(m p) -> m p", p=P)).then_inc(s["vecs_in"], 16)
            sp.dma_start(w_tok[:, :, :], a["tok_W"].rearrange("(k p) n -> p k n", p=P)).then_inc(s["rest_in"], 16)
            sp.dma_start(row_bias[:, :], a["pos"][0]).then_inc(s["rest_in"], 16)
            sp.dma_start(tok[0:1, 0, :], a["cls"][0]).then_inc(s["rest_in"], 16)
            sp.dma_start(gam_b[:, :], a["tg"].partition_broadcast(NC)).then_inc(s["rest_in"], 16)
            sp.dma_start(bet_b[:, :], a["tb"].partition_broadcast(NC)).then_inc(s["rest_in"], 16)
            sp.dma_start(bv_b[:, :], a["bv"].partition_broadcast(S)).then_inc(s["rest_in"], 16)
            sp.dma_start(bo_b[:, :], a["bo"].partition_broadcast(S)).then_inc(s["rest_in"], 16)
            sp.dma_start(h[NC:S, :, :], a["txt"].rearrange("b t d -> t b d")).then_inc(s["txt_in"], 16)
            for w, v in ((w_q, "Wq"), (w_k, "Wk"), (w_v, "Wv"), (w_g, "Wg"), (w_o, "Wo"), (w_r, "Wr")):
                sp.dma_start(w[:, :, :], a[v].rearrange("(k p) n -> p k n", p=P)).then_inc(s["attn_in"], 16)
            for m, v in enumerate(("w1s", "w2s", "w3s")):
                sp.dma_start(raw[m][:, :].rearrange("p (k n) -> p k n", k=a[v].shape[0] // P),
                             a[v].rearrange("(k p) n -> p k n", p=P)).then_inc(s[f"w{m}_in"], 16)

            def load_weights(k, m, again=False):
                if m < 2:
                    sp.wait_ge(s["w12_lo"], 2 * k - 1 + m)
                else:
                    sp.wait_ge(s["w3_lo"], k)
                if again:
                    v = a[("w1s", "w2s", "w3s")[m]].rearrange("(k p) n -> p k n", p=P)
                else:
                    v = a[("W1", "W2", "W3")[m]][bass.ds(k - 1, 1)].rearrange("e (k p) n -> p (e k) n", p=P)
                sp.dma_start(raw[m][:, :].rearrange("p (k n) -> p k n", k=v.shape[1]), v).then_inc(s[f"w{m}_in"], 16)

            def load_rows(t, block):
                sp.wait_ge(s["x_tr"], t)
                sp.dma_start(xr[:, :], xs[bass.ds(block * ROWS, ROWS), :]).then_inc(s["xr_in"], 16)

            def store_tile(t, done="y_st"):
                sp.wait_ge(s["y_ev"], t + 1)
                sp.dma_start(ys[bass.ds(t * ROWS, ROWS), :], y_sb[:, :]).then_inc(s[done], 16)

            def load_next(split, m):
                with sp.If(split > 0):
                    with sp.If(split < E):
                        k = nc.s_assert_within(split, 1, E - 1, skip_runtime_bounds_check_because="the two Ifs")
                        load_weights(k + 1, m)
                    with sp.If(split == E):
                        load_weights(AGAIN, m, again=True)

            for m in range(3):
                load_weights(1, m)
            sp.wait_ge(s["zero_out"], 32)
            sp.wait_ge(s["zero_y"], 16)
            sp.wait_ge(s["h2_st"], 16 * NG)
            full = SH - 1
            last = T - full * ROWS
            sp.dma_start(h_fl[:, 0:full, :], hs[0:full * ROWS, :].rearrange("(c p) d -> p c d", p=ROWS)).then_inc(s["h_in"], 16)
            sp.dma_start(h_fl[0:last, full, :], hs[full * ROWS:T, :]).then_inc(s["h_in"], 16)
            sp.wait_ge(s["xn2_st"], 16 * NG)
            with sp.Fori(1, EARLY - 2) as t:
                load_rows(t + 2, t + 2)
                store_tile(t - 1)
            sp.wait_ge(s["scattered"], 16 * B)
            load_rows(EARLY, SH)
            store_tile(EARLY - 3)
            for m in range(3):
                load_weights(2, m)
            load_rows(EARLY + 1, SH + 1)
            store_tile(EARLY - 2)
            load_weights(3, 0)
            load_weights(3, 1)
            sp.wait_ge(s["tab_ok"], 1)
            nt = sp.value_load(tab[0:1, LAST:LAST + 1], min_val=EARLY + E - 1, max_val=EARLY + MAXR - 1) + 1
            with sp.Fori(EARLY, nt) as t:
                block = sp.value_load(tab[0:1, bass.ds(t - EARLY + ROWS_AT, 1)], min_val=EARLY, max_val=SH + MAXR - 1)
                load_rows(t + 2, block)
                split12 = sp.value_load(tab[0:1, bass.ds(t - EARLY + SPLIT12, 1)], min_val=0, max_val=AGAIN)
                split3 = sp.value_load(tab[0:1, bass.ds(t - EARLY + SPLIT3, 1)], min_val=0, max_val=AGAIN)
                load_next(split3, 2)
                load_next(split12, 0)
                store_tile(t - 1)
                load_next(split12, 1)
            store_tile(nt - 1, "last_st")
            for j in range(2, LATE):
                load_rows(nt + j, EARLY + j)
            sp.wait_ge(s["last_st"], 16)
            sp.dma_start(ysh[:, :, :], ys[0:EARLY * ROWS, :].rearrange("(c p) d -> p c d", p=ROWS)).then_inc(s["ysh_in"], 16)
            flat = out.rearrange("b t d -> (b t) d")

            def store(c):
                n = min(ROWS, T - c * ROWS)
                sp.dma_start(flat[c * ROWS:c * ROWS + n, :], h_fl[0:n, c, :]).then_inc(s["out_st"], 16)

            for j in range(LATE - 1):
                sp.wait_ge(s["late_out"], j + 1)
                store(EARLY + j)
            for c in range(EARLY):
                sp.wait_ge(s["sum2"], c + 1)
                store(c)
            sp.wait_ge(s["late_out"], LATE)
            store(SH - 1)
            sp.wait_ge(s["out_st"], 16 * SH)

        @block.gpsimd
        def _(pool):
            pool.memset(zero[:, :], 0.0).then_inc(s["zero_set"], 1)
            pool.memset(eps[:, :], EPS).then_inc(s["eps_set"], 1)
            pool.memset(tokT_all[:, :, :, 0:1], 0.0)
            pool.memset(tokT[:, :, :, :], 0.0).then_inc(s["col_set"], 1)
            pool.wait_ge(s["rest_in"], 112)
            pool.wait_ge(s["txt_in"], 16)
            pool.wait_ge(s["zero_set"], 1)
            pool.dma_start(xs[SH * ROWS:, :].rearrange("(c p) d -> p c d", p=P),
                           zero[:, :].unsqueeze(1).to_broadcast([P, MAXR, D])).then_inc(s["zero_out"], 16)
            pool.dma_start(xs[T:SH * ROWS, :], zero[0:SH * ROWS - T, :]).then_inc(s["zero_out"], 16)
            n = MAXR - E
            pool.dma_start(ys[(EARLY + E) * ROWS:, :].rearrange("(c p) d -> p c d", p=P),
                           zero[:, :].unsqueeze(1).to_broadcast([P, n, D])).then_inc(s["zero_y"], 16)

            def residual_bias(g):
                pool.wait_ge(s["ht_ok"], g + 1)
                pool.wait_ge(s["h2_st"], 16 * g)
                pool.wait_ge(s["xn2_ok"], g)
                pool.tensor_tensor(h2[:, :, :], h[:, bass.ds(g * GB, GB), :],
                                   bo_b[:, :].unsqueeze(1).to_broadcast([S, GB, D]), ALU.add).then_inc(s["hb_ok"], 1)

            def lower(k, m, slot):
                pool.wait_ge(s["w12_hi"], 2 * k + m + 1)
                w = slice(m * WCOLS, (m + 1) * WCOLS)
                lo, hi = w_lo[:, slot, w], w_hi[:, slot, w]
                if not isinstance(k, int):
                    lo, hi = (x.rearrange("p a n -> p (a n)") for x in (lo, hi))
                pool.tensor_tensor(lo, raw[m][:, :], hi.bitcast(F32), ALU.subtract).then_inc(s["w12_lo"], 1)

            def x4(g):
                pool.wait_ge(s["ht_c"], g + 1)
                pool.tensor_tensor(h[0:NC, bass.ds(g * GB, GB), :], tok[:, :, :],
                                   bet_b[:, :].unsqueeze(1).to_broadcast([NC, GB, D]), ALU.add).then_inc(s["ht_ok"], 1)

            lower(0, 0, 0)
            lower(0, 1, 0)
            x4(1)
            residual_bias(0)
            with pool.Fori(1, NG - 1) as i:
                x4(i + 1)
                residual_bias(i)
            residual_bias(NG - 1)
            pool.wait_ge(s["rows_ok"], 1)
            pool.wait_ge(s["xn2_cp"], 16 * NG)
            pool.wait_ge(s["zero_out"], 32)
            for b in range(B):
                pool.indirect_dma_start(out=xs, out_offset=bass.IndirectOffsetOnAxis(ap=rows_sb[0:S, 0, b:b + 1], axis=0),
                                        in_=h[0:S, b, :], in_offset=None).then_inc(s["scattered"], 16)
            pool.dma_start(row_d[0:T, :].rearrange("(b t) o -> t (b o)", t=S), rows_sb[0:S, 1, :],
                           allow_slow_non_contiguous=True).then_inc(s["row_st"], 16)
            pool.wait_ge(s["row_st"], 16)
            full, rest_rows = T // ROWS, T % ROWS
            pool.dma_start(row_t[:, 0:full], row_d[0:full * ROWS, :].rearrange("(c p) o -> p (c o)", p=ROWS),
                           allow_slow_non_contiguous=True)\
                .then_inc(s["row_in"], 16)
            pool.dma_start(row_t[0:rest_rows, full:full + 1], row_d[full * ROWS:T, :]).then_inc(s["row_in"], 16)
            with pool.Fori(1, AGAIN + 1) as k:
                lower(k, 0, bass.ds(k % RING, 1))
                lower(k, 1, bass.ds(k % RING, 1))
            pool.wait_ge(s["row_in"], 32)
            pool.wait_ge(s["last_st"], 16)
            for c in list(range(EARLY, SH)) + list(range(EARLY)):
                n = min(ROWS, T - c * ROWS)
                pool.indirect_dma_start(out=yg[0:n, c, :], out_offset=None, in_=ys,
                                        in_offset=bass.IndirectOffsetOnAxis(ap=row_t[0:n, c:c + 1], axis=0))\
                    .then_inc(s["gathered_late" if c >= EARLY else "gathered"], 16)

        @block.tensor
        def _(pe):
            ident = cst("ident")

            def mm(o, l, r, start, stop):
                return pe.matmul(o, l, r, start=start, stop=stop)

            def x1():
                for j in range(2 * KX):
                    pe.wait_ge(s["imgp_dve"], 1)
                    if j >= 2 * KX // C:
                        pe.wait_ge(s["imgp_act"], 1)
                    if j >= 4 * KX // C:
                        pe.wait_ge(s["imgp_dve"], 2)
                    if j >= 8:
                        pe.wait_ge(s["pt_act"] if j % 2 == 0 else s["pt_dve"], (j - 8) // 2 + 1)
                    k = j // 2
                    for q in range(HP // 2):
                        wp = j % 2 * (HP // 2) + q
                        at = wp * PATCH * PATCH + (k % 2) * P
                        last = pe.transpose(banks[j % 8][:, q * QR:(q + 1) * QR], img_p[:, k // 2, at:at + P],
                                            ident[0:QR, 0:QR])
                    last.then_inc(s["xtr"], 1)

            def x2(bank, batches, ks):
                b0, b1 = batches
                for k in ks:
                    pe.wait_ge(s["pt_act"], k + 1)
                    pe.wait_ge(s["pt_dve"], k + 1)
                    for m in range(KD):
                        last = mm(bank[:, m, 0:(b1 - b0) * NP], w_tok[:, k, m * P:(m + 1) * P],
                                  pt[:, k, :].rearrange("p (n b) -> p n b", b=B)[:, :, b0:b1], k == 0, k == KX - 1)
                if k == KX - 1:
                    last.then_inc(s["tokmm"], 1)

            def x3(g):
                if isinstance(g, int) and g == 0:
                    pe.wait_ge(s["emb0_act"], 1)
                    pe.wait_ge(s["emb0_dve"], 1)
                else:
                    pe.wait_ge(s["tokT_ok"], g)
                pe.wait_ge(s["v_ok"], g)
                for b in range(GB):
                    for m in range(KD):
                        at = (b % 2) * D + m * P
                        last = pe.transpose(pT[0:S, b // 2, at:at + P], tokT[:, m, b, :], ident)
                last.then_inc(s["tok_t"], 1)

            def transposes(bank, src, name):
                for m in range(KD):
                    for b in range(GB):
                        last = pe.transpose(bank[:, m, b * S:(b + 1) * S], src[:, b, m * P:(m + 1) * P], ident[0:S, 0:S])
                    last.then_inc(s[name], 1)

            def x6(g):
                pe.wait_ge(s["xn_ok"], g + 1)
                if not isinstance(g, int) or g > 1:
                    pe.wait_ge(s["lg_ok"], g - 1)
                transposes(pT, xn, "xn_t")

            def project(bank, w, name):
                for m in range(KD):
                    for k in range(KD):
                        last = mm(bank[:, m, 0:GS], w[:, k, m * P:(m + 1) * P], xnT[:, k, :], k == 0, k == KD - 1)
                    last.then_inc(s[name], 1)

            def to_tokens(bank, left, w, name):
                for b in range(GB):
                    for k in range(KD):
                        last = mm(bank[0:S, b // 2, (b % 2) * D:(b % 2 + 1) * D], left[:, k, b * S:(b + 1) * S],
                                  w[:, k, :], k == 0, k == KD - 1)
                last.then_inc(s[name], 1)

            def x7_qk(g):
                pe.wait_ge(s["xnT_act"], g + 1)
                pe.wait_ge(s["xnT_dve"], g + 1)
                pe.wait_ge(s["p_ok"], 2 * GB * g)
                project(pS[:, 2:4, :], w_q, "q_mm")
                project(pS[:, 0:2, :], w_k, "k_mm")

            def x7_vg(g):
                to_tokens(pT, xnT, w_v, "v_mm")
                pe.wait_ge(s["q_ok"], g + 1)
                project(pS[:, 2:4, :], w_g, "g_mm")

            def scores(g, b):
                for half in range(2):
                    if b == 0:
                        pe.wait_ge(s["q_ok"], g + 1)
                        pe.wait_ge(s["k_ok"], g + 1)
                        pe.wait_ge(s["g_ok"], g + 1)
                    else:
                        pe.wait_ge(s["p_ok"], 2 * (GB * g + b) - 1 + half)
                    for m in range(KD):
                        for r in (2 * half, 2 * half + 1):
                            q = slice(32 * r, 32 * r + 32)
                            last = mm(pS[0:S, r, m * 2 * S:(m + 1) * 2 * S], kT[q, m, b * S:(b + 1) * S],
                                      qq[q, m, b, :, :], True, True)
                    last.then_inc(s["sc"], 1)

            def retain(g, b):
                if b == 0:
                    pe.wait_ge(s["v_ok"], g + 1)
                    pe.wait_ge(s["h2_ok"], g)
                if b >= 2:
                    pe.wait_ge(s["rt_ok"], GB * g + b - 1)
                for half in range(2):
                    pe.wait_ge(s["p_ok"], 2 * (GB * g + b) + 1 + half)
                    for m in range(KD):
                        for r in (2 * half, 2 * half + 1):
                            last = mm(pV[32 * r:32 * r + 32, b % 2, m * 2 * S:(m + 1) * 2 * S],
                                      vv[:, b, m * P + 32 * r:m * P + 32 * r + 32],
                                      pr[:, b % 2, r * 4 + m * 2:r * 4 + m * 2 + 2, :], True, True)
                last.then_inc(s["pv"], 1)

            def y1(g, between):
                for b in range(GB + 1):
                    if b < GB:
                        scores(g, b)
                    if b:
                        retain(g, b - 1)
                    if b in between:
                        between[b]()

            def column_sums(bank, src, name):
                for m in range(KD):
                    last = mm(bank[:, 0:GS], cst("ones"), src[:, m, :], m == 0, m == KD - 1)
                last.then_inc(s[name], 1)

            def y2_mean(g):
                pe.wait_ge(s["rt_ok"], GB * g + GB)
                column_sums(pV[:, 0, :], rT, "mean_mm")

            def y2_var(g):
                pe.wait_ge(s["sq_ok"], g + 1)
                column_sums(pV[:, 1, :], sqT, "var_mm")

            def y4(g):
                pe.wait_ge(s["u_ok"], g + 1)
                to_tokens(pV, uT, w_o, "o_mm")

            def y6_transpose(g, last=False):
                pe.wait_ge(s["xn2_ok"], g + 1)
                pe.wait_ge(s["v_ok"], min(g + 2, NG) if isinstance(g, int) else g + 2)
                if last:
                    pe.wait_ge(s["lg_ok"], g)
                elif isinstance(g, int) and g == NG - 2:
                    pass
                else:
                    pe.wait_ge(s["tok_ok"], g + 3)
                transposes(pT, xn2, "x2_t")

            def y6_logits(g):
                pe.wait_ge(s["x2T_ok"], g + 1)
                for b in range(GB):
                    for k in range(KD):
                        last = mm(pT[0:S, 0, b * E:(b + 1) * E], x2T[:, k, b * S:(b + 1) * S], w_r[:, k, :],
                                  k == 0, k == KD - 1)
                last.then_inc(s["lg_mm"], 1)

            def x_transpose(t, bank):
                pe.wait_ge(s["xr_in"], 16 * t + 16)
                for m in range(KD):
                    last = pe.transpose(bank[:, m * ROWS:(m + 1) * ROWS], xr[:, m * P:(m + 1) * P], ident)
                last.then_inc(s["x_tr"], 1)

            def weights_ready(k):
                pe.wait_ge(s["w12_hi"], 2 * k + 2)
                pe.wait_ge(s["w12_lo"], 2 * k + 2)

            def x_ready(t):
                pe.wait_ge(s["x_hi"], t + 1)
                pe.wait_ge(s["x_lo"], t + 1)

            def up(hf, slot, name):
                for k in range(KD):
                    xh, xl = xT_hi[:, k, :], xT_lo[:, k, :]
                    for part, st, w in ((xh, True, w_hi), (xh, False, w_lo), (xl, False, w_hi)):
                        for j in range(2):
                            at = j * WCOLS + k * F + hf * HALF
                            last = mm(pU[hf][j], part, w[:, slot, at:at + HALF],
                                      k == 0 and st, k == KD - 1 and part is xl)
                last.then_inc(s[name], 1)

            pe.wait_ge(s["const_in"], 16)
            pe.wait_ge(s["vecs_in"], 96)
            pe.transpose(pV[:, 0, 0:6 * KD], vec_rows[:, :], ident[0:6 * KD, 0:6 * KD]).then_inc(s["vec_t"], 1)
            pe.wait_ge(s["vec_ok"], 1)
            x1()
            pe.wait_ge(s["rest_in"], 112)
            pe.wait_ge(s["pt_act"], 4)
            pe.wait_ge(s["pt_dve"], 4)
            x2(pV, (0, GB), range(KX))
            x2(pS, (GB, B), range(KX // 3))
            x3(0)
            x2(pS, (GB, B), range(KX // 3, KX))
            x6(0)
            pe.wait_ge(s["attn_in"], 96)
            pe.wait_ge(s["emb_act"], 1)
            pe.wait_ge(s["emb_dve"], 1)
            x7_qk(0)
            x7_vg(0)

            def step(i, first=False):
                if first:
                    y1(i, {0: lambda: x3(i + 1)})
                else:
                    y1(i, {0: lambda: x3(i + 1), 3: lambda: y6_transpose(i - 1), 4: lambda: y6_logits(i - 1)})
                x6(i + 1)
                y2_mean(i)
                x7_qk(i + 1)
                y2_var(i)
                x7_vg(i + 1)
                y4(i)
            step(0, first=True)
            with pe.Fori(1, NG - 1) as i:
                step(i)
            y1(NG - 1, {3: lambda: y6_transpose(NG - 2), 4: lambda: y6_logits(NG - 2)})
            y2_mean(NG - 1)
            x_transpose(0, pX0)
            y2_var(NG - 1)
            weights_ready(0)
            x_ready(0)
            up(0, 0, "up0")
            up(1, 0, "up1")
            y4(NG - 1)
            pe.wait_ge(s["h2_ok"], NG)
            x_transpose(1, pX)
            y6_transpose(NG - 1, last=True)
            y6_logits(NG - 1)

            def count():
                pe.wait_ge(s["pick_ok"], 1)
                picks = pick[:, :, :].rearrange("t b e -> t (b e)")
                mm(pC[:, 0:B * E], cst("earlier", S), picks, True, True)
                mm(pC[:, B * E:2 * B * E], cst("ones", S)[:, 0:S], picks, True, True).then_inc(s["count_mm"], 1)
                pe.wait_ge(s["count_ok"], 1)

            def hid_transpose(hf, name):
                for c in range(FC):
                    last = pe.transpose(pH[hf][:, c * P:(c + 1) * P], hid[:, hf, c * P:(c + 1) * P], ident)
                last.then_inc(s[name], 1)

            def down(hf, slot):
                for c in range(FC):
                    at = 2 * WCOLS + (hf * FC + c) * D
                    for n, (l, w) in enumerate(((hT_hi, w_hi), (hT_hi, w_lo), (hT_lo, w_hi))):
                        last = mm(pY, l[:, hf, c, :], w[:, slot, at:at + D], hf == 0 and c == 0 and n == 0,
                                  hf == 1 and c == FC - 1 and n == 2)
                return last

            def slot(t, e, at, e1, at1, counting=False, ahead=True, final=False, late=0):
                pe.wait_ge(s["hid0"], t)
                pe.wait_ge(s["hid_lo0"], t - 1)
                hid_transpose(0, "hid_tr0")
                if not final:
                    weights_ready(e)
                    x_ready(t)
                    up(0, at, "up0")
                if counting:
                    count()
                pe.wait_ge(s["hid1"], t)
                pe.wait_ge(s["hid_lo1"], t - 1)
                hid_transpose(1, "hid_tr1")
                pe.wait_ge(s["hid_lo0"], t)
                pe.wait_ge(s["w3_hi"], e1 + 1)
                pe.wait_ge(s["w3_lo"], e1 + 1)
                if late:
                    pe.wait_ge(s["late_out"], late)
                else:
                    pe.wait_ge(s["y_ev"], t - 1)
                down(0, at1)
                if not final:
                    up(1, at, "up1")
                    if ahead:
                        x_transpose(t + 1, pX)
                pe.wait_ge(s["hid_lo1"], t)
                down(1, at1).then_inc(s["y_mm"], 1)

            pe.wait_ge(s["lg_ok"], NG)
            slot(1, 0, 0, 0, 0, counting=True)
            with pe.Fori(2, EARLY) as t:
                slot(t, 0, 0, 0, 0)
            pe.wait_ge(s["tab_ok"], 1)
            nt = pe.value_load(tab[0:1, LAST:LAST + 1], min_val=EARLY + E - 1, max_val=EARLY + MAXR - 1) + 1
            with pe.Fori(EARLY, nt) as t:
                e1 = pe.value_load(tab[0:1, bass.ds(t - EARLY, 1)], min_val=0, max_val=E)
                e = pe.value_load(tab[0:1, bass.ds(t - EARLY + 1, 1)], min_val=1, max_val=E)
                slot(t, e, bass.ds(e % RING, 1), e1, bass.ds(e1 % RING, 1))
            slot(nt, AGAIN, AGAIN % RING, E, E % RING)
            for j in range(1, LATE):
                slot(nt + j, AGAIN, AGAIN % RING, AGAIN, AGAIN % RING, ahead=j < LATE - 1, late=j - 1)
            slot(nt + LATE, AGAIN, AGAIN % RING, AGAIN, AGAIN % RING, final=True, late=LATE - 1)

        @block.scalar
        def _(act):
            def deviation(name, n, g):
                l = lns[name]
                act.wait_ge(s[name + "_mv"], g + 1)
                act.activation(l["sd"][0:n, :], l["mv"][0:n, :, 1], ACT.Sqrt, bias=eps[0:n, :]).then_inc(s[name + "_sd"], 1)

            def norm(name, src, dst, done, n, g):
                l = lns[name]
                act.wait_ge(s[name + "_nmr"], g + 1)
                for b in range(GB):
                    last = act.activation(dst[:, b, :], src(b), ACT.Identity, bias=l["nmr"][0:n, b:b + 1],
                                          scale=l["r"][0:n, b:b + 1])
                last.then_inc(s[done], 1)

            def regroup(c):
                act.wait_ge(s["img_in"], 16 * HP)
                act.activation(img_p[:, c, :].rearrange("q (wp r v) -> q wp r v", r=PATCH, v=PATCH),
                           img[:, c, :].rearrange("q (r wp v) -> q wp r v", r=PATCH, v=PATCH), ACT.Copy).then_inc(s["imgp_act"], 1)

            def x1():
                for j in range(0, 2 * KX, 2):
                    act.wait_ge(s["xtr"], j + 1)
                    act.activation(pt[:, j // 2, 0:XH], banks[j % 8][:, 0:XH], ACT.Copy).then_inc(s["pt_act"], 1)

            def embedded(m, n_mm, src, batches, dst, done):
                b0, b1 = batches
                act.wait_ge(s["tokmm"], n_mm)
                act.activation(dst.rearrange("p b (hp wp) -> p wp hp b", wp=HP),
                               src[:, m, 0:(b1 - b0) * NP].rearrange("p (wp hp b) -> p wp hp b", hp=HP, b=b1 - b0),
                               ACT.Identity, bias=vec[:, m:m + 1]).then_inc(s[done], 1)

            def split_hi(k, m):
                act.wait_ge(s[f"w{m}_in"], 16 * k + 16)
                w = slice(m * WCOLS, (m + 1) * WCOLS)
                if isinstance(k, int):
                    hi = w_hi[:, k % RING, w]
                else:
                    hi = w_hi[:, bass.ds(k % RING, 1), w].rearrange("p a n -> p (a n)")
                act.activation(hi, raw[m][:, :], ACT.Copy).then_inc(s["w12_hi"], 1)

            def x2(g):
                act.wait_ge(s["tok_t"], g)
                act.activation(tokT[:, :, :, 0:NC], tokT_all[:, :, bass.ds(g * GB, GB), :], ACT.Copy).then_inc(s["tokT_ok"], 1)

            def x4(g):
                norm("lt", lambda b: tok[:, b, :], tok, "tn_ok", NC, g)

            def x5(g):
                act.wait_ge(s["xn_t"], 2 * g)
                norm("lx", lambda b: h[:, bass.ds(g * GB + b, 1), :].rearrange("t b d -> t (b d)"), xn, "xn_ok", S, g)

            def x6(g):
                act.wait_ge(s["xn_t"], 2 * g + 1)
                act.wait_ge(s["g_mm"], 2 * g)
                act.activation(xnT[:, 0, :], pT[:, 0, 0:GS], ACT.Copy).then_inc(s["xnT_act"], 1)

            def x7_keys(g):
                act.wait_ge(s["sc"], 2 * GB * g)
                for m in range(KD):
                    act.wait_ge(s["k_mm"], 2 * g + m + 1)
                    last = act.activation(kT[:, m, :], pS[:, m, 0:GS], ACT.Identity, bias=vec[:, 2 * KD + m:2 * KD + m + 1])
                last.then_inc(s["k_ok"], 1)

            def x7_gate(g):
                act.wait_ge(s["u_ok"], g)
                for m in range(KD):
                    act.wait_ge(s["g_mm"], 2 * g + m + 1)
                    last = act.activation(gate[:, m, :], pS[:, 2 + m, 0:GS], ACT.Sigmoid,
                                          bias=vec[:, 3 * KD + m:3 * KD + m + 1])
                last.then_inc(s["g_ok"], 1)

            def retained(b):
                return pV[:, b % 2, 0:4 * S].rearrange("p (m o t) -> p m o t", m=KD, o=2)

            def y1(g, b):
                act.wait_ge(s["pv"], GB * g + b + 1)
                act.activation(r_even[:, b % 2, :, :], retained(b)[:, :, 0, :], ACT.Copy, scale=cst("even")).then_inc(s["re_ok"], 1)

            def y2_square(g):
                act.wait_ge(s["cen_ok"], g + 1)
                act.wait_ge(s["var_mm"], g)
                act.activation(sqT[:, :, :], rT[:, :, :], ACT.Square).then_inc(s["sq_ok"], 1)

            def y2_deviation(g):
                act.wait_ge(s["var_mm"], g + 1)
                act.wait_ge(s["zn_ok"], g)
                act.activation(sdT[:, :], pV[:, 1, 0:GS], ACT.Sqrt, bias=eps[:, :], scale=1.0 / D).then_inc(s["sdT_ok"], 1)

            def y3(g):
                act.wait_ge(s["zn_ok"], g + 1)
                act.wait_ge(s["o_mm"], g)
                for m in range(KD):
                    last = act.activation(uT[:, m, :], rT[:, m, :], ACT.Identity,
                                          scale=vec[:, 4 * KD + m:4 * KD + m + 1], bias=vec[:, 5 * KD + m:5 * KD + m + 1])
                last.then_inc(s["z_ok"], 1)

            def y5(g):
                act.wait_ge(s["xn2_st"], 16 * g)
                act.wait_ge(s["xn2_cp"], 16 * g)
                act.wait_ge(s["x2_t"], 2 * g)
                norm("l2", lambda b: h2[:, b, :], xn2, "xn2_ok", S, g)
                hrows = hs[0:T, :].rearrange("(b t) d -> t b d", t=S)
                act.dma_start(hrows[:, bass.ds(g * GB, GB), :], h2[:, :, :]).then_inc(s["h2_st"], 16)
                act.wait_ge(s["xn2_ok"], g + 1)
                act.dma_start(tokens[:, bass.ds(g * GB, GB), :], xn2[:, :, :]).then_inc(s["xn2_st"], 16)
                act.dma_start(h[0:S, bass.ds(g * GB, GB), :], xn2[:, :, :]).then_inc(s["xn2_cp"], 16)

            def y6_transposed(g):
                act.wait_ge(s["lg_mm"], g)
                for m in range(KD):
                    act.wait_ge(s["x2_t"], 2 * g + m + 1)
                    last = act.activation(x2T[:, m, :], pT[:, m, 0:GS], ACT.Copy)
                last.then_inc(s["x2T_ok"], 1)

            def y6_logits(g):
                act.wait_ge(s["lg_mm"], g + 1)
                act.activation(lg[:, bass.ds(g * GB, GB), :].rearrange("t b e -> t (b e)"), pT[0:S, 0, 0:GB * E],
                               ACT.Copy).then_inc(s["lg_ok"], 1)

            def load_rows(block):
                act.dma_start(xr[:, :], xs[bass.ds(block * ROWS, ROWS), :]).then_inc(s["xr_in"], 16)

            def x_hi(t, bank):
                act.wait_ge(s["x_tr"], t + 1)
                act.activation(xT_hi[:, :, :].rearrange("p k n -> p (k n)"), bank, ACT.Copy).then_inc(s["x_hi"], 1)

            def gelu(hf, t):
                act.wait_ge(s[f"up{hf}"], t + 1)
                act.wait_ge(s[f"hid{hf}"], t)
                act.activation(gl[:, hf, :], pU[hf][0], ACT.Gelu).then_inc(s[f"gelu{hf}"], 1)

            act.wait_ge(s["eps_set"], 1)
            regroup(1)
            x1()
            act.wait_ge(s["xtr"], 2 * KX)
            act.wait_ge(s["vec_ok"], 1)
            act.wait_ge(s["col_set"], 1)
            embedded(0, 1, pV, (0, GB), tokT[:, 0, :, 1:NC], "emb0_act")
            split_hi(0, 0)
            split_hi(0, 1)
            act.wait_ge(s["txt_in"], 16)
            deviation("lt", NC, 0)
            x4(0)
            embedded(0, 2, pS, (GB, B), tokT_all[:, 0, GB:B, 1:NC], "emb_act")
            deviation("lx", S, 0)
            x5(0)
            x6(0)
            act.wait_ge(s["vec_ok"], 1)
            x7_keys(0)
            x7_gate(0)
            act.wait_ge(s["emb_act"], 1)
            act.wait_ge(s["emb_dve"], 1)

            def step(i, first=False, last=False):
                deviation("lt", NC, i + 1)
                x4(i + 1)
                y1(i, 0)
                y1(i, 1)
                if not first:
                    deviation("l2", S, i - 1)
                if not first:
                    y5(i - 1)
                deviation("lx", S, i + 1)
                y1(i, 2)
                if not first:
                    y6_transposed(i - 1)
                y1(i, 3)
                x5(i + 1)
                if not first:
                    y6_logits(i - 1)
                x6(i + 1)
                y2_square(i)
                x7_keys(i + 1)
                y2_deviation(i)
                y3(i)
                x7_gate(i + 1)
                if not last:
                    x2(i + 2)
            x2(1)
            step(0, first=True)
            with act.Fori(1, NG - 2) as i:
                step(i)
            step(NG - 2, last=True)
            act.wait_ge(s["zero_out"], 32)
            act.wait_ge(s["xn2_st"], 16)
            load_rows(0)
            y1(NG - 1, 0)
            deviation("l2", S, NG - 2)
            y1(NG - 1, 1)
            y5(NG - 2)
            y1(NG - 1, 2)
            y6_transposed(NG - 2)
            y1(NG - 1, 3)
            y6_logits(NG - 2)
            y2_square(NG - 1)
            x_hi(0, pX0)
            load_rows(1)
            y2_deviation(NG - 1)
            y3(NG - 1)
            gelu(0, 0)
            gelu(1, 0)
            deviation("l2", S, NG - 1)
            y5(NG - 1)
            x_hi(1, pX)
            act.wait_ge(s["xn2_st"], 16 * (NG - 1))
            load_rows(2)
            y6_transposed(NG - 1)
            y6_logits(NG - 1)
            assert 2 * ROWS <= GS and 3 * ROWS <= (NG - 1) * GS

            def slot(t, look=None, split=None, evacuate=True, ahead=True, final=False):
                act.wait_ge(s["hid_tr0"], t)
                act.activation(hT_hi[:, 0, :, :].rearrange("p c n -> p (c n)"), pH[0], ACT.Copy).then_inc(s["hid_hi0"], 1)
                if look:
                    look()
                if not final:
                    gelu(0, t)
                act.wait_ge(s["hid_tr1"], t)
                act.wait_ge(s["y_mm"], t - 1)
                act.activation(hT_hi[:, 1, :, :].rearrange("p c n -> p (c n)"), pH[1], ACT.Copy).then_inc(s["hid_hi1"], 1)
                if split:
                    split(0)
                if not final:
                    gelu(1, t)
                    if ahead:
                        x_hi(t + 1, pX)
                if split:
                    split(1)
                if evacuate:
                    act.wait_ge(s["y_mm"], t)
                    act.wait_ge(s["y_st"], 16 * (t - 1))
                    act.activation(y_sb[:, :], pY, ACT.Copy).then_inc(s["y_ev"], 1)

            act.wait_ge(s["zero_y"], 16)
            slot(1, split=lambda m: split_hi(1, m))
            with act.Fori(2, EARLY - 1) as t:
                slot(t)
            act.wait_ge(s["scattered"], 16 * B)
            slot(EARLY - 1, split=lambda m: split_hi(2, m))
            act.wait_ge(s["tab_ok"], 1)
            nt = act.value_load(tab[0:1, LAST:LAST + 1], min_val=EARLY + E - 1, max_val=EARLY + MAXR - 1) + 1
            with act.Fori(EARLY, nt) as t:
                at = {}

                def look():
                    at["split"] = act.value_load(tab[0:1, bass.ds(t - EARLY + SPLIT12, 1)], min_val=0, max_val=AGAIN)

                def split_next(m):
                    with act.If(at["split"] > 0):
                        split_hi(at["split"], m)
                slot(t, look, split_next)
            slot(nt)
            for j in range(1, LATE):
                slot(nt + j, evacuate=False, ahead=j < LATE - 1)
            slot(nt + LATE, evacuate=False, final=True)

        @block.vector
        def _(dve):
            def sums(name, src, n, batches):
                for b in batches:
                    last = dve.bn_stats(lns[name]["st"][0:n, b, :], src(b))
                return last

            def stats(name, src, n, g, batches=range(GB)):
                l = lns[name]
                sums(name, src, n, batches).then_inc(s[name + "_st"], 1)
                dve.wait_ge(s[name + "_st"], g + 1)
                dve.memset(l["tick"][0:1, :], 0.0)
                for b in range(GB):
                    last = dve.bn_aggr(l["mv"][0:n, b, :], l["st"][0:n, b, :])
                last.then_inc(s[name + "_mv"], 1)

            def recip(name, n, g, with_mean=True):
                l = lns[name]
                dve.wait_ge(s[name + "_sd"], g + 1)
                dve.reciprocal(l["r"][0:n, :], l["sd"][0:n, :]).then_inc(s[name + "_r"], 1)
                if with_mean:
                    dve.wait_ge(s[name + "_r"], g + 1)
                    dve.scalar_tensor_tensor(out=l["nmr"][0:n, :], in0=l["mv"][0:n, :, 0], scalar=-1.0,
                                             in1=l["r"][0:n, :], op0=ALU.mult, op1=ALU.mult).then_inc(s[name + "_nmr"], 1)

            def regroup(c):
                dve.wait_ge(s["img_in"], 16 * HP)
                dve.tensor_copy(img_p[:, c, :].rearrange("q (wp r v) -> q wp r v", r=PATCH, v=PATCH),
                                img[:, c, :].rearrange("q (r wp v) -> q wp r v", r=PATCH, v=PATCH)).then_inc(s["imgp_dve"], 1)

            def x1():
                for j in range(1, 2 * KX, 2):
                    dve.wait_ge(s["xtr"], j + 1)
                    dve.tensor_copy(pt[:, j // 2, XH:2 * XH], banks[j % 8][:, 0:XH]).then_inc(s["pt_dve"], 1)

            def embedded(m, n_mm, src, batches, dst, done):
                b0, b1 = batches
                dve.wait_ge(s["tokmm"], n_mm)
                dve.tensor_scalar(dst.rearrange("p b (hp wp) -> p wp hp b", wp=HP),
                                  src[:, m, 0:(b1 - b0) * NP].rearrange("p (wp hp b) -> p wp hp b", hp=HP, b=b1 - b0),
                                  vec[:, m:m + 1], None, ALU.add).then_inc(s[done], 1)

            def split3(k):
                w3 = slice(2 * WCOLS, 3 * WCOLS)
                if isinstance(k, int):
                    lo, hi = w_lo[:, k % RING, w3], w_hi[:, k % RING, w3]
                else:
                    lo, hi = (w[:, bass.ds(k % RING, 1), w3].rearrange("p a n -> p (a n)") for w in (w_lo, w_hi))
                dve.wait_ge(s["w2_in"], 16 * k + 16)
                dve.tensor_copy(hi, raw[2][:, :]).then_inc(s["w3_hi"], 1)
                dve.wait_ge(s["w3_hi"], k + 1)
                dve.tensor_tensor(lo, raw[2][:, :], hi.bitcast(F32), ALU.subtract).then_inc(s["w3_lo"], 1)

            def x_lo(t, bank):
                dve.wait_ge(s["x_hi"], t + 1)
                dve.tensor_tensor(xT_lo[:, :, :].rearrange("p k n -> p (k n)"), bank,
                                  xT_hi[:, :, :].rearrange("p k n -> p (k n)").bitcast(F32), ALU.subtract).then_inc(s["x_lo"], 1)

            def hidden(hf, t):
                dve.wait_ge(s[f"gelu{hf}"], t + 1)
                if not isinstance(t, int) or t > 0:
                    dve.wait_ge(s[f"hid_tr{hf}"], t)
                dve.tensor_tensor(hid[:, hf, :], pU[hf][1], gl[:, hf, :], ALU.mult).then_inc(s[f"hid{hf}"], 1)

            def hidden_lo(hf, t):
                dve.wait_ge(s[f"hid_hi{hf}"], t + 1)
                f = "p c n -> p (c n)"
                dve.tensor_tensor(hT_lo[:, hf, :, :].rearrange(f), pH[hf], hT_hi[:, hf, :, :].rearrange(f).bitcast(F32),
                                  ALU.subtract).then_inc(s[f"hid_lo{hf}"], 1)

            def x3(g):
                dve.wait_ge(s["tok_t"], g + 1)
                dve.wait_ge(s["ht_ok"], g)
                dve.tensor_tensor(tok[:, :, :], pT[0:NC, :, :].rearrange("t a (b d) -> t (a b) d", d=D),
                                  row_bias[:, :].unsqueeze(1).to_broadcast([NC, GB, D]), ALU.add).then_inc(s["tok_ok"], 1)

            def x4a(g):
                dve.wait_ge(s["tok_ok"], g + 1)
                sums("lt", lambda b: tok[:, b, :], NC, range(GB // 2))

            def x4b(g):
                stats("lt", lambda b: tok[:, b, :], NC, g, range(GB // 2, GB))

            def x4c(g):
                recip("lt", NC, g)

            def x4d(g):
                dve.wait_ge(s["tn_ok"], g + 1)
                dve.tensor_tensor(tok[:, :, :], tok[:, :, :], gam_b[:, :].unsqueeze(1).to_broadcast([NC, GB, D]), ALU.mult)\
                    .then_inc(s["ht_c"], 1)

            def x5a(g):
                dve.wait_ge(s["ht_ok"], g + 1)
                dve.memset(tick[:, 1:2], 0.0)
                stats("lx", lambda b: h[:, bass.ds(g * GB + b, 1), :].rearrange("t b d -> t (b d)"), S, g)

            def x5b(g):
                recip("lx", S, g)

            def x6(g):
                dve.wait_ge(s["xn_t"], 2 * g + 2)
                dve.wait_ge(s["g_mm"], 2 * g)
                dve.tensor_copy(xnT[:, 1, :], pT[:, 1, 0:GS]).then_inc(s["xnT_dve"], 1)

            def x7_queries(g):
                dve.wait_ge(s["sc"], 2 * GB * g)
                for m in range(KD):
                    dve.wait_ge(s["q_mm"], 2 * g + m + 1)
                    for o, which in enumerate(("even", "odd")):
                        last = dve.tensor_scalar(qq[:, m, :, o, :], pS[:, 2 + m, 0:GS].rearrange("p (b t) -> p b t", b=GB),
                                                 vec[:, KD + m:KD + m + 1], cst(which), ALU.add, ALU.mult)
                last.then_inc(s["q_ok"], 1)

            def x7_values(g):
                dve.wait_ge(s["v_mm"], g + 1)
                dve.wait_ge(s["pv"], GB * g)
                dve.tensor_tensor(vv[:, :, :], pT[0:S, :, :].rearrange("t a (b d) -> t (a b) d", d=D),
                                  bv_b[:, :].unsqueeze(1).to_broadcast([S, GB, D]), ALU.add).then_inc(s["v_ok"], 1)

            def y1(g, b):
                for half in range(2):
                    dve.wait_ge(s["sc"], 2 * (GB * g + b) + 1 + half)
                    if b >= 2:
                        dve.wait_ge(s["pv"], GB * g + b - 1)
                    a = 2 * half
                    dve.tensor_tensor(pr[:, b % 2, 8 * half:8 * half + 8, :].rearrange("t (r m) s -> t r m s", r=2),
                                      pS[0:S, a:a + 2, 0:4 * S].rearrange("t r (m s) -> t r m s", m=4),
                                      cst("decay", S).unsqueeze(1).unsqueeze(1).to_broadcast([S, 2, 4, S]), ALU.mult)\
                        .then_inc(s["p_ok"], 1)

            def y1_gather(g, b):
                dve.wait_ge(s["re_ok"], GB * g + b + 1)
                odd = pV[:, b % 2, 0:4 * S].rearrange("p (m o t) -> p m o t", m=KD, o=2)[:, :, 1, :]
                dve.scalar_tensor_tensor(out=rT[:, :, b * S:(b + 1) * S], in0=odd, scalar=cst("odd"), in1=r_even[:, b % 2, :, :],
                                         op0=ALU.mult, op1=ALU.add).then_inc(s["rt_ok"], 1)

            def y2_center(g):
                dve.wait_ge(s["mean_mm"], g + 1)
                dve.scalar_tensor_tensor(out=rT[:, :, :], in0=pV[:, 0:1, 0:GS].to_broadcast([P, KD, GS]), scalar=-1.0 / D,
                                         in1=rT[:, :, :], op0=ALU.mult, op1=ALU.add).then_inc(s["cen_ok"], 1)

            def y2_scale(g):
                dve.wait_ge(s["sdT_ok"], g + 1)
                dve.reciprocal(sdT[:, :], sdT[:, :]).then_inc(s["rinv_ok"], 1)
                dve.wait_ge(s["rinv_ok"], g + 1)
                dve.tensor_tensor(rT[:, :, :], rT[:, :, :], sdT[:, :].unsqueeze(1).to_broadcast([P, KD, GS]), ALU.mult)\
                    .then_inc(s["zn_ok"], 1)

            def y3(g):
                dve.wait_ge(s["z_ok"], g + 1)
                dve.tensor_tensor(uT[:, :, :], uT[:, :, :], gate[:, :, :], ALU.mult).then_inc(s["u_ok"], 1)

            def y4(g):
                dve.wait_ge(s["o_mm"], g + 1)
                dve.wait_ge(s["hb_ok"], g + 1)
                dve.tensor_tensor(h2[:, :, :], pV[0:S, :, :].rearrange("t a (b d) -> t (a b) d", d=D), h2[:, :, :],
                                  ALU.add).then_inc(s["h2_ok"], 1)

            def y5a(g):
                dve.wait_ge(s["h2_ok"], g + 1)
                dve.memset(tick[:, 4:5], 0.0)
                sums("l2", lambda b: h2[:, b, :], S, range(GB // 2))

            def y5b(g):
                stats("l2", lambda b: h2[:, b, :], S, g, range(GB // 2, GB))

            def y5c(g):
                recip("l2", S, g)

            dve.wait_ge(s["vec_t"], 1)
            dve.tensor_copy(vec[:, :], pV[:, 0, 0:6 * KD]).then_inc(s["vec_ok"], 1)
            dve.wait_ge(s["vec_ok"], 1)
            dve.wait_ge(s["rest_in"], 112)
            dve.tensor_tensor(row_bias[0:1, :], row_bias[0:1, :], tok[0:1, 0, :], ALU.add).then_inc(s["cls_ok"], 1)
            regroup(0)
            regroup(2)
            x1()
            dve.wait_ge(s["xtr"], 2 * KX)
            dve.wait_ge(s["cls_ok"], 1)
            dve.wait_ge(s["col_set"], 1)
            embedded(1, 1, pV, (0, GB), tokT[:, 1, :, 1:NC], "emb0_dve")
            x3(0)
            x4a(0)
            x4b(0)
            x4c(0)
            x4d(0)
            dve.wait_ge(s["ht_c"], 1)
            dve.tensor_tensor(h[0:NC, 0:GB, :], tok[:, :, :], bet_b[:, :].unsqueeze(1).to_broadcast([NC, GB, D]), ALU.add)\
                .then_inc(s["ht_ok"], 1)
            embedded(1, 2, pS, (GB, B), tokT_all[:, 1, GB:B, 1:NC], "emb_dve")
            dve.wait_ge(s["txt_in"], 16)
            x5a(0)
            x5b(0)
            x6(0)
            x7_queries(0)
            x7_values(0)

            def step(i, first=False):
                y1(i, 0)
                x3(i + 1)
                x4a(i + 1)
                y1(i, 1)
                x4b(i + 1)
                if not first:
                    y5a(i - 1)
                x4c(i + 1)
                y1(i, 2)
                if not first:
                    y5b(i - 1)
                y1_gather(i, 0)
                x4d(i + 1)
                y1_gather(i, 1)
                if not first:
                    y5c(i - 1)
                y1(i, 3)
                x5a(i + 1)
                x5b(i + 1)
                y1_gather(i, 2)
                y1_gather(i, 3)
                x6(i + 1)
                y2_center(i)
                x7_queries(i + 1)
                y2_scale(i)
                x7_values(i + 1)
                y3(i)
                y4(i)
            assert GB == 4
            step(0, first=True)
            with dve.Fori(1, NG - 1) as i:
                step(i)
            y1(NG - 1, 0)
            y5a(NG - 2)
            y5b(NG - 2)
            y1(NG - 1, 1)
            y5c(NG - 2)
            y1_gather(NG - 1, 0)
            y1(NG - 1, 2)
            y1_gather(NG - 1, 1)
            split3(0)
            y1(NG - 1, 3)
            y1_gather(NG - 1, 2)
            y1_gather(NG - 1, 3)
            y2_center(NG - 1)
            x_lo(0, pX0)
            y2_scale(NG - 1)
            y3(NG - 1)
            hidden(0, 0)
            hidden(1, 0)
            y4(NG - 1)
            y5a(NG - 1)
            y5b(NG - 1)
            y5c(NG - 1)
            x_lo(1, pX)

            n = {"route": 0, "count_ok": 0}

            def then(ins, name="route"):
                n[name] += 1
                ins.then_inc(s[name], 1)
                dve.wait_ge(s[name], n[name])

            dve.wait_ge(s["lg_ok"], NG)
            be = [S, B, E]
            then(dve.tensor_reduce(mx[:, :], lg[:, :, :], AX.X, ALU.max))
            then(dve.tensor_tensor(eq[:, :, :], lg[:, :, :], mx[:, :].unsqueeze(2).to_broadcast(be), ALU.is_equal))
            then(dve.scalar_tensor_tensor(out=posm[:, :, :], in0=eq[:, :, :], scalar=-float(E),
                                          in1=cst("expert_late", S).unsqueeze(1).to_broadcast(be),
                                          op0=ALU.mult, op1=ALU.add))
            then(dve.tensor_reduce(idx[:, :], posm[:, :, :], AX.X, ALU.min))
            dve.tensor_tensor(pick[:, :, :], cst("expert", S).unsqueeze(1).to_broadcast(be),
                              idx[:, :].unsqueeze(2).to_broadcast(be), ALU.is_equal).then_inc(s["pick_ok"], 1)
            hidden_lo(0, 0)
            hidden(0, 1)
            dve.wait_ge(s["count_mm"], 1)
            dve.tensor_copy(befo[:, :, :], pC[:, 0:B * E].rearrange("t (b e) -> t b e", e=E))
            then(dve.tensor_copy(tot[:, :, :], pC[:, B * E:2 * B * E].rearrange("t (b e) -> t e b", e=E)), "count_ok")
            hidden_lo(1, 0)
            hidden(1, 1)
            x_lo(2, pX)

            def slot(t, between=None, look=None, ahead=True, final=False):
                hidden_lo(0, t - 1)
                if look:
                    look()
                if not final:
                    hidden(0, t)
                hidden_lo(1, t - 1)
                if between:
                    between()
                if not final:
                    if ahead:
                        x_lo(t + 1, pX)
                    hidden(1, t)

            def places():
                fl = "t e b -> t (e b)"
                then(dve.tensor_tensor_scan(cin[:, :, :].rearrange(fl), cst("ones", S)[:, 0:B * E], tot[:, :, :].rearrange(fl),
                                            0.0, ALU.mult, ALU.add))
                then(dve.tensor_tensor(cex[:, :, :], cin[:, :, :], tot[:, :, :], ALU.subtract))
                then(dve.tensor_tensor(cnt[:, :], cin[:, :, B - 1], cex[:, :, 0], ALU.subtract))
                then(dve.tensor_tensor(over[:, :, :], cnt[:, :].unsqueeze(2).to_broadcast([S, E, NTHR]),
                                       cst("thr", S).unsqueeze(1).to_broadcast([S, E, NTHR]), ALU.is_gt))
                then(dve.tensor_reduce(tiles[:, :], over[:, :, :], AX.X, ALU.add))
                then(dve.tensor_tensor_scan(tin[:, :], cst("ones", S)[:, 0:E], tiles[:, :], 0.0, ALU.mult, ALU.add))
                then(dve.tensor_tensor(tex[:, :], tin[:, :], tiles[:, :], ALU.subtract))

            def rows_and_table():
                then(dve.scalar_tensor_tensor(out=delta[:, :], in0=tex[:, :], scalar=float(ROWS), in1=cex[:, :, 0],
                                              op0=ALU.mult, op1=ALU.subtract))
                then(dve.tensor_tensor(pos[:, :, :].rearrange("t b e -> t e b"), cex[:, :, :],
                                       delta[:, :].unsqueeze(2).to_broadcast([S, E, B]), ALU.add))
                then(dve.tensor_tensor(posm[:, :, :], pos[:, :, :], befo[:, :, :], ALU.add))
                then(dve.tensor_tensor(pos[:, :, :], posm[:, :, :], pick[:, :, :], ALU.mult))
                then(dve.tensor_reduce(row_f[:, :], pos[:, :, :], AX.X, ALU.add))
                dve.tensor_scalar(rows_sb[0:S, 0, :], row_f[:, :], float(SH * ROWS), None, ALU.add)
                dve.tensor_scalar(rows_sb[0:S, 1, :], row_f[:, :], float(EARLY * ROWS), None, ALU.add).then_inc(s["rows_ok"], 1)
                then(dve.tensor_tensor(ord_c[:, :, :], tex[0:1, :].unsqueeze(1).to_broadcast([1, MAXR, E]),
                                       cst("tile", 1).unsqueeze(2).to_broadcast([1, MAXR, E]), ALU.is_le))
                dve.memset(tab_f[0:1, 0:1], 0.0)
                n_tiles = tin[0:1, E - 1:E]
                then(dve.tensor_reduce(tab_f[0:1, 1:LAST], ord_c[:, :, :], AX.X, ALU.add))
                dve.tensor_scalar(tab_f[0:1, LAST:LAST + 1], n_tiles, float(EARLY - 1), None, ALU.add)
                experts = tab_f[0:1, 1:LAST]
                then(dve.tensor_tensor(first[:, :], experts, tab_f[0:1, 0:MAXR], ALU.subtract))
                dve.scalar_tensor_tensor(out=tab_f[0:1, SPLIT3:SPLIT3 + MAXR], in0=experts, scalar=1.0, in1=first[:, :],
                                         op0=ALU.add, op1=ALU.mult)
                then(dve.scalar_tensor_tensor(out=second[:, :], in0=experts, scalar=float(E), in1=first[:, :],
                                              op0=ALU.is_lt, op1=ALU.mult))
                dve.scalar_tensor_tensor(out=tab_f[0:1, SPLIT12:SPLIT12 + MAXR], in0=experts, scalar=2.0, in1=second[:, :],
                                         op0=ALU.add, op1=ALU.mult)
                dve.tensor_scalar(beyond[:, :], cst("tile", 1), 2.0, n_tiles, ALU.add, ALU.is_ge)
                then(dve.tensor_scalar(back[:, :], n_tiles, -1.0, float(EARLY - SH), ALU.mult, ALU.add))
                then(dve.scalar_tensor_tensor(out=beyond[:, :], in0=beyond[:, :], scalar=back[:, :], in1=cst("tile", 1),
                                              op0=ALU.mult, op1=ALU.add))
                then(dve.tensor_scalar(tab_f[0:1, ROWS_AT:ROWS_AT + MAXR], beyond[:, :], float(SH + 2), None, ALU.add))
                dve.tensor_copy(tab[0:1, :], tab_f[:, :]).then_inc(s["tab_ok"], 1)

            def route():
                places()
                rows_and_table()
            slot(2, route)
            with dve.Fori(3, EARLY - 2) as t:
                slot(t)
            slot(EARLY - 2, lambda: split3(1))
            slot(EARLY - 1)
            dve.wait_ge(s["tab_ok"], 1)
            nt = dve.value_load(tab[0:1, LAST:LAST + 1], min_val=EARLY + E - 1, max_val=EARLY + MAXR - 1) + 1
            with dve.Fori(EARLY, nt) as t:
                at = {}

                def look():
                    at["split"] = dve.value_load(tab[0:1, bass.ds(t - EARLY + SPLIT3, 1)], min_val=0, max_val=AGAIN)

                def split_next():
                    with dve.If(at["split"] > 0):
                        split3(at["split"])
                slot(t, split_next, look)
            def rows(c):
                return min(ROWS, T - c * ROWS)

            def residual_and_shared():
                dve.wait_ge(s["h_in"], 32)
                dve.wait_ge(s["ysh_in"], 16)
                for c in range(EARLY):
                    dve.tensor_tensor(ysh[:, c, :], ysh[:, c, :], h_fl[:, c, :], ALU.add).then_inc(s["sum1"], 1)

            def residual_and_routed():
                dve.wait_ge(s["gathered_late"], 16 * LATE)
                for c in range(EARLY, SH):
                    dve.tensor_tensor(yg[0:rows(c), c, :], yg[0:rows(c), c, :], h_fl[0:rows(c), c, :], ALU.add)\
                        .then_inc(s["sum3"], 1)

            def late_out(j):
                c = EARLY + j
                dve.wait_ge(s["y_mm"], nt + j + 1)
                dve.wait_ge(s["sum3"], LATE)
                dve.tensor_tensor(h_fl[0:rows(c), c, :], pY[0:rows(c), :], yg[0:rows(c), c, :], ALU.add)\
                    .then_inc(s["late_out"], 1)

            slot(nt)
            for j in range(1, LATE):
                slot(nt + j, ahead=j < LATE - 1)
                if j == 1:
                    residual_and_routed()
                late_out(j - 1)
            slot(nt + LATE, final=True)
            residual_and_shared()
            dve.wait_ge(s["gathered"], 16 * EARLY)
            dve.wait_ge(s["sum1"], EARLY)
            for c in range(EARLY):
                dve.tensor_tensor(h_fl[:, c, :], ysh[:, c, :], yg[:, c, :], ALU.add).then_inc(s["sum2"], 1)
            late_out(LATE - 1)


INS = {"x": "x", "txt": "txt", "tok_W": "L0_tok_W", "tok_b": "L0_tok_b", "cls": "L0_tok_cls_token",
       "pos": "L0_tok_pos_embedding", "tg": "L0_tok_gamma", "tb": "L0_tok_beta", "Wq": "L0_attn_Wq", "bq": "L0_attn_bq",
       "Wk": "L0_attn_Wk", "bk": "L0_attn_bk", "Wv": "L0_attn_Wv", "bv": "L0_attn_bv", "Wg": "L0_attn_Wg",
       "bg": "L0_attn_bg", "Wo": "L0_attn_Wo", "bo": "L0_attn_bo", "ga": "L0_attn_gamma", "ba": "L0_attn_beta",
       "w1s": "L0_ffn_w1s", "w2s": "L0_ffn_w2s", "w3s": "L0_ffn_w3s", "W1": "L0_ffn_W1", "W2": "L0_ffn_W2",
       "W3": "L0_ffn_W3", "Wr": "L0_ffn_Wg"}


def kernel(**inputs):
    import concourse.bacc as bacc
    from concourse.bass_utils import run_bass_kernel_spmd

    nc = bacc.Bacc("TRN2", target_bir_lowering=False, num_devices=1)
    arrays = {n: np.ascontiguousarray(inputs[full]) for n, full in INS.items()}
    B, C, H, _ = arrays["x"].shape
    z = shapes_of(B, C, H, arrays["txt"].shape[1], arrays["txt"].shape[2], arrays["w1s"].shape[1])
    arrays["const"], cols = constants(z)
    aps = {n: nc.dram_tensor("in_" + n, v.shape, F32, kind="ExternalInput").ap() for n, v in arrays.items()}
    out = nc.dram_tensor("out_h", (B, z["S"], z["D"]), F32, kind="ExternalOutput").ap()
    build(nc, aps, out, z, cols)
    r = run_bass_kernel_spmd(nc, [{"in_" + n: v for n, v in arrays.items()}], core_ids=[0])
    return r.results[0]["out_h"]
```
